# Optimizing a Trainium2 kernel written in Bass

```python
import numpy as np
import jax
import jax.numpy as jnp

def _softmax(x, axis=-1):
    return jax.nn.softmax(x, axis=axis)

def _gelu(x):
    return jax.nn.gelu(x, approximate=True)

def _silu(x):
    return jax.nn.silu(x)

def _sigmoid(x):
    return jax.nn.sigmoid(x)

def _layernorm(x, axis=-1, eps=1e-05):
    m = jnp.mean(x, axis=axis, keepdims=True)
    v = jnp.var(x, axis=axis, keepdims=True)
    return (x - m) / jnp.sqrt(v + eps)

def _scatter_add(tgt, idx, src, axis=0):
    return tgt.at[idx].add(src)

def _segment_sum(src, seg, n):
    return jax.ops.segment_sum(src, seg, n)
kernel_name = 'mk_gnn_resnorm_d4_gnn_r8_aa80c3'

def setup_inputs(seed: int=0):
    np.random.seed(seed)
    _w = jnp.asarray

    def _rec_inputs():
        import jax
        import jax.numpy as jnp
        _gk = jax.random.key(seed)
        x = -0.001003 + 1 * jax.random.normal(jax.random.fold_in(_gk, 1), (256, 768), jnp.float32)
        _s = jax.random.randint(jax.random.fold_in(_gk, 2), (2048,), 0, 256, jnp.int32)
        _d = jax.random.randint(jax.random.fold_in(_gk, 3), (2048,), 0, 256, jnp.int32)
        _loop = jnp.arange(256, dtype=jnp.int32)
        src = jnp.concatenate([_s, _d, _loop])
        dst = jnp.concatenate([_d, _s, _loop])
        _o = jnp.argsort(dst, stable=True)
        src = src[_o]
        dst = dst[_o]
        edge_type_3 = jax.random.randint(jax.random.fold_in(_gk, 12), (4352,), 0, 3, jnp.int32)
        edge_type_34 = jax.random.randint(jax.random.fold_in(_gk, 13), (4352,), 0, 34, jnp.int32)
        return (x, src, dst, edge_type_3, edge_type_34)
    x, src, dst, edge_type_3, edge_type_34 = _rec_inputs()

    def _L0_gnn_setup():
        import jax, jax.numpy as jnp
        import numpy as np
        NUM_RELATIONS = 3

        def _rgcn(x, W_rel, W_root, bias, src, dst, etype):
            n = x.shape[0]
            xr = jnp.einsum('ni,rio->rno', x, W_rel)
            msg = xr[etype, src]
            out = x @ W_root + bias
            for r in range(NUM_RELATIONS):
                m = etype == r
                s = jax.ops.segment_sum(jnp.where(m[:, None], msg, 0.0), dst, num_segments=n)
                c = jax.ops.segment_sum(m.astype(x.dtype), dst, num_segments=n)
                out = out + s / jnp.maximum(c, 1.0)[:, None]
            return out

        def _gate(h, q, Wg, bg, Wq, bq):
            B, L, F = q.shape
            N = h.shape[0] // B
            h3 = h.reshape(B, N, F)
            hg = jnp.einsum('bnf,gf->bng', h3, Wg[:, :F])
            qg = jnp.einsum('blf,gf->blg', q, Wg[:, F:]) + bg
            attn = jax.nn.sigmoid(hg[:, :, None, :] + qg[:, None, :, :])
            qi = jnp.einsum('bnlf,blf->bnf', attn, q)
            alpha = jax.nn.sigmoid(jnp.einsum('bnf,gf->bng', h3, Wq[:, :F]) + jnp.einsum('bnf,gf->bng', qi, Wq[:, F:]) + bq)
            hn = alpha * jnp.tanh(qi) + (1.0 - alpha) * h3
            return hn.reshape(B * N, F)
        key = jax.random.key(seed)
        ks = jax.random.split(key, 16)
        F = 768
        BN, E, B, L = (256, 8192, 8, 64)
        s = 0.02
        return {'x': jax.random.normal(ks[0], (BN, F), jnp.float32), 'edge_index': jax.random.randint(ks[1], (2, E), 0, BN), 'edge_type': jax.random.randint(ks[2], (E,), 0, NUM_RELATIONS), 'query_embs': jax.random.normal(ks[3], (B, L, F), jnp.float32), 'W_rel1': jax.random.normal(ks[4], (NUM_RELATIONS, F, F), jnp.float32) * s, 'W_root1': jax.random.normal(ks[5], (F, F), jnp.float32) * s, 'b1': jnp.zeros((F,), jnp.float32), 'W_rel2': jax.random.normal(ks[6], (NUM_RELATIONS, F, F), jnp.float32) * s, 'W_root2': jax.random.normal(ks[7], (F, F), jnp.float32) * s, 'b2': jnp.zeros((F,), jnp.float32), 'Wg': jax.random.normal(ks[8], (F, 2 * F), jnp.float32) * s, 'bg': jnp.zeros((F,), jnp.float32), 'Wq': jax.random.normal(ks[9], (F, 2 * F), jnp.float32) * s, 'bq': jnp.zeros((F,), jnp.float32)}
    _L0_gnn_all = _L0_gnn_setup()
    _L0_gnn_in = {k: v for k, v in _L0_gnn_all.items() if k in ('query_embs', 'W_rel1', 'W_root1', 'b1', 'W_rel2', 'W_root2', 'b2', 'Wg', 'bg', 'Wq', 'bq')}
    del _L0_gnn_all

    def _L1_gnn_setup():
        import jax, jax.numpy as jnp
        import numpy as np
        N_NODES = 1250
        N_EDGES = 12500
        DIM = 768
        key = jax.random.key(seed)
        k1, k2, k3, k4 = jax.random.split(key, 4)
        x = jax.random.normal(k1, (N_NODES, DIM), dtype=jnp.float32)
        edge_index = jax.random.randint(k2, (2, N_EDGES), 0, N_NODES, dtype=jnp.int32)
        W = jax.random.normal(k3, (DIM, DIM), dtype=jnp.float32) / np.sqrt(DIM)
        b = jnp.zeros((DIM,), dtype=jnp.float32)
        return {'x': x, 'edge_index': edge_index, 'W': W, 'b': b}
    _L1_gnn_all = _L1_gnn_setup()
    _L1_gnn_in = {k: v for k, v in _L1_gnn_all.items() if k in ('W', 'b')}
    del _L1_gnn_all

    def _L2_gnn_setup():
        import jax, jax.numpy as jnp
        import numpy as np
        NEG_SLOPE = 0.2
        EPS = 1e-16
        N_NODES = 4096
        N_EDGES = 20000
        DIM = 768
        HEADS1 = 4
        OUT1 = DIM // HEADS1
        HEADS2 = 1
        OUT2 = DIM
        N_REL = 3

        def rgat_conv(x, W, q, k, b, src, dst, etype, heads, out_ch, n_nodes):
            xr = jnp.einsum('nd,rdf->rnf', x, W)
            oi = xr[etype, dst]
            oj = xr[etype, src]
            qi = oi @ q
            kj = oj @ k
            alpha = jax.nn.leaky_relu(qi + kj, NEG_SLOPE)
            m = jax.ops.segment_max(alpha, dst, num_segments=n_nodes)
            e = jnp.exp(alpha - m[dst])
            z = jax.ops.segment_sum(e, dst, num_segments=n_nodes)
            a = e / (z[dst] + EPS)
            msg = (a[:, :, None] * oj.reshape(-1, heads, out_ch)).reshape(-1, heads * out_ch)
            out = jax.ops.segment_sum(msg, dst, num_segments=n_nodes)
            return out + b
        key = jax.random.key(seed)
        ks = jax.random.split(key, 12)
        s = 0.02
        return {'x': jax.random.normal(ks[0], (N_NODES, DIM), dtype=jnp.float32), 'edge_index': jax.random.randint(ks[1], (2, N_EDGES), 0, N_NODES, dtype=jnp.int64), 'edge_type': jax.random.randint(ks[2], (N_EDGES,), 0, N_REL, dtype=jnp.int64), 'W1': jax.random.normal(ks[3], (N_REL, DIM, HEADS1 * OUT1), dtype=jnp.float32) * s, 'q1': jax.random.normal(ks[4], (HEADS1 * OUT1, HEADS1), dtype=jnp.float32) * s, 'k1': jax.random.normal(ks[5], (HEADS1 * OUT1, HEADS1), dtype=jnp.float32) * s, 'b1': jnp.zeros((HEADS1 * OUT1,), dtype=jnp.float32), 'W2': jax.random.normal(ks[6], (N_REL, DIM, HEADS2 * OUT2), dtype=jnp.float32) * s, 'q2': jax.random.normal(ks[7], (HEADS2 * OUT2, HEADS2), dtype=jnp.float32) * s, 'k2': jax.random.normal(ks[8], (HEADS2 * OUT2, HEADS2), dtype=jnp.float32) * s, 'b2': jnp.zeros((HEADS2 * OUT2,), dtype=jnp.float32)}
    _L2_gnn_all = _L2_gnn_setup()
    _L2_gnn_in = {k: v for k, v in _L2_gnn_all.items() if k in ('W1', 'q1', 'k1', 'b1', 'W2', 'q2', 'k2', 'b2')}
    del _L2_gnn_all

    def _L3_gnn_setup():
        import jax, jax.numpy as jnp
        import numpy as np
        N_NODES = 1250
        N_EDGES = 12500
        N_REL = 34
        DIM = 768

        def _graph_encoder(x, edge_index, edge_type, W_rel, W_root, b_rgcn, W_gcn, b_gcn):
            n = x.shape[0]
            src, dst = (edge_index[0], edge_index[1])
            ones = jnp.ones((src.shape[0],), dtype=x.dtype)
            seg = edge_type * n + dst
            agg = jax.ops.segment_sum(x[src], seg, num_segments=N_REL * n)
            cnt = jax.ops.segment_sum(ones, seg, num_segments=N_REL * n)
            mean = agg.reshape(N_REL, n, -1) / jnp.maximum(cnt, 1.0).reshape(N_REL, n, 1)
            h1 = jnp.einsum('rni,rio->no', mean, W_rel) + x @ W_root + b_rgcn
            xw = h1 @ W_gcn
            deg = jax.ops.segment_sum(ones, dst, num_segments=n) + 1.0
            dinv = jax.lax.rsqrt(deg)
            norm = dinv[src] * dinv[dst]
            out = jax.ops.segment_sum(xw[src] * norm[:, None], dst, num_segments=n)
            out = out + xw * (dinv * dinv)[:, None]
            return out + b_gcn
        key = jax.random.key(seed)
        ks = jax.random.split(key, 6)
        scale = 1.0 / np.sqrt(DIM)
        x = jax.random.normal(ks[0], (N_NODES, DIM), dtype=jnp.float32)
        edge_index = jax.random.randint(ks[1], (2, N_EDGES), 0, N_NODES, dtype=jnp.int32)
        edge_type = jax.random.randint(ks[2], (N_EDGES,), 0, N_REL, dtype=jnp.int32)
        W_rel = jax.random.normal(ks[3], (N_REL, DIM, DIM), dtype=jnp.float32) * scale
        W_root = jax.random.normal(ks[4], (DIM, DIM), dtype=jnp.float32) * scale
        b_rgcn = jnp.zeros((DIM,), dtype=jnp.float32)
        W_gcn = jax.random.normal(ks[5], (DIM, DIM), dtype=jnp.float32) * scale
        b_gcn = jnp.zeros((DIM,), dtype=jnp.float32)
        return {'x': x, 'edge_index': edge_index, 'edge_type': edge_type, 'W_rel': W_rel, 'W_root': W_root, 'b_rgcn': b_rgcn, 'W_gcn': W_gcn, 'b_gcn': b_gcn}
    _L3_gnn_all = _L3_gnn_setup()
    _L3_gnn_in = {k: v for k, v in _L3_gnn_all.items() if k in ('W_rel', 'W_root', 'b_rgcn', 'W_gcn', 'b_gcn')}
    del _L3_gnn_all
    return {'x': x, 'src': src, 'dst': dst, 'edge_type_3': edge_type_3, 'edge_type_34': edge_type_34, 'L0_gnn_query_embs': _L0_gnn_in['query_embs'], 'L0_gnn_W_rel1': _L0_gnn_in['W_rel1'], 'L0_gnn_W_root1': _L0_gnn_in['W_root1'], 'L0_gnn_b1': _L0_gnn_in['b1'], 'L0_gnn_W_rel2': _L0_gnn_in['W_rel2'], 'L0_gnn_W_root2': _L0_gnn_in['W_root2'], 'L0_gnn_b2': _L0_gnn_in['b2'], 'L0_gnn_Wg': _L0_gnn_in['Wg'], 'L0_gnn_bg': _L0_gnn_in['bg'], 'L0_gnn_Wq': _L0_gnn_in['Wq'], 'L0_gnn_bq': _L0_gnn_in['bq'], 'L1_gnn_W': _L1_gnn_in['W'], 'L1_gnn_b': _L1_gnn_in['b'], 'L2_gnn_W1': _L2_gnn_in['W1'], 'L2_gnn_q1': _L2_gnn_in['q1'], 'L2_gnn_k1': _L2_gnn_in['k1'], 'L2_gnn_b1': _L2_gnn_in['b1'], 'L2_gnn_W2': _L2_gnn_in['W2'], 'L2_gnn_q2': _L2_gnn_in['q2'], 'L2_gnn_k2': _L2_gnn_in['k2'], 'L2_gnn_b2': _L2_gnn_in['b2'], 'L3_gnn_W_rel': _L3_gnn_in['W_rel'], 'L3_gnn_W_root': _L3_gnn_in['W_root'], 'L3_gnn_b_rgcn': _L3_gnn_in['b_rgcn'], 'L3_gnn_W_gcn': _L3_gnn_in['W_gcn'], 'L3_gnn_b_gcn': _L3_gnn_in['b_gcn']}

def reference(x, src, dst, edge_type_3, edge_type_34, L0_gnn_query_embs, L0_gnn_W_rel1, L0_gnn_W_root1, L0_gnn_b1, L0_gnn_W_rel2, L0_gnn_W_root2, L0_gnn_b2, L0_gnn_Wg, L0_gnn_bg, L0_gnn_Wq, L0_gnn_bq, L1_gnn_W, L1_gnn_b, L2_gnn_W1, L2_gnn_q1, L2_gnn_k1, L2_gnn_b1, L2_gnn_W2, L2_gnn_q2, L2_gnn_k2, L2_gnn_b2, L3_gnn_W_rel, L3_gnn_W_root, L3_gnn_b_rgcn, L3_gnn_W_gcn, L3_gnn_b_gcn):
    import jax
    import jax.numpy as jnp

    def _L0_gnn_ref(x, edge_index, edge_type, query_embs, W_rel1, W_root1, b1, W_rel2, W_root2, b2, Wg, bg, Wq, bq):
        import jax, jax.numpy as jnp
        import numpy as np
        NUM_RELATIONS = 3

        def _rgcn(x, W_rel, W_root, bias, src, dst, etype):
            n = x.shape[0]
            xr = jnp.einsum('ni,rio->rno', x, W_rel)
            msg = xr[etype, src]
            out = x @ W_root + bias
            for r in range(NUM_RELATIONS):
                m = etype == r
                s = jax.ops.segment_sum(jnp.where(m[:, None], msg, 0.0), dst, num_segments=n)
                c = jax.ops.segment_sum(m.astype(x.dtype), dst, num_segments=n)
                out = out + s / jnp.maximum(c, 1.0)[:, None]
            return out

        def _gate(h, q, Wg, bg, Wq, bq):
            B, L, F = q.shape
            N = h.shape[0] // B
            h3 = h.reshape(B, N, F)
            hg = jnp.einsum('bnf,gf->bng', h3, Wg[:, :F])
            qg = jnp.einsum('blf,gf->blg', q, Wg[:, F:]) + bg
            attn = jax.nn.sigmoid(hg[:, :, None, :] + qg[:, None, :, :])
            qi = jnp.einsum('bnlf,blf->bnf', attn, q)
            alpha = jax.nn.sigmoid(jnp.einsum('bnf,gf->bng', h3, Wq[:, :F]) + jnp.einsum('bnf,gf->bng', qi, Wq[:, F:]) + bq)
            hn = alpha * jnp.tanh(qi) + (1.0 - alpha) * h3
            return hn.reshape(B * N, F)
        src, dst = (edge_index[0], edge_index[1])
        h = jax.nn.relu(_rgcn(x, W_rel1, W_root1, b1, src, dst, edge_type))
        h = _gate(h, query_embs, Wg, bg, Wq, bq)
        h = jax.nn.relu(_rgcn(h, W_rel2, W_root2, b2, src, dst, edge_type))
        h = _gate(h, query_embs, Wg, bg, Wq, bq)
        return h

    def _L1_gnn_ref(x, edge_index, W, b):
        import jax, jax.numpy as jnp
        import numpy as np
        N_NODES = 1250
        N_EDGES = 12500
        DIM = 768
        n = x.shape[0]
        loop = jnp.arange(n, dtype=edge_index.dtype)
        src = jnp.concatenate([edge_index[0], loop])
        dst = jnp.concatenate([edge_index[1], loop])
        deg = jax.ops.segment_sum(jnp.ones_like(dst, dtype=x.dtype), dst, num_segments=n)
        deg_inv_sqrt = jnp.where(deg > 0, jax.lax.rsqrt(deg), 0.0)
        norm = deg_inv_sqrt[src] * deg_inv_sqrt[dst]
        h = x @ W
        msg = h[src] * norm[:, None]
        out = jax.ops.segment_sum(msg, dst, num_segments=n)
        return out + b

    def _L2_gnn_ref(x, edge_index, edge_type, W1, q1, k1, b1, W2, q2, k2, b2):
        import jax, jax.numpy as jnp
        import numpy as np
        NEG_SLOPE = 0.2
        EPS = 1e-16
        N_NODES = 4096
        N_EDGES = 20000
        DIM = 768
        HEADS1 = 4
        OUT1 = DIM // HEADS1
        HEADS2 = 1
        OUT2 = DIM
        N_REL = 3

        def rgat_conv(x, W, q, k, b, src, dst, etype, heads, out_ch, n_nodes):
            xr = jnp.einsum('nd,rdf->rnf', x, W)
            oi = xr[etype, dst]
            oj = xr[etype, src]
            qi = oi @ q
            kj = oj @ k
            alpha = jax.nn.leaky_relu(qi + kj, NEG_SLOPE)
            m = jax.ops.segment_max(alpha, dst, num_segments=n_nodes)
            e = jnp.exp(alpha - m[dst])
            z = jax.ops.segment_sum(e, dst, num_segments=n_nodes)
            a = e / (z[dst] + EPS)
            msg = (a[:, :, None] * oj.reshape(-1, heads, out_ch)).reshape(-1, heads * out_ch)
            out = jax.ops.segment_sum(msg, dst, num_segments=n_nodes)
            return out + b
        src, dst = (edge_index[0], edge_index[1])
        n = x.shape[0]
        h = rgat_conv(x, W1, q1, k1, b1, src, dst, edge_type, HEADS1, OUT1, n)
        h = jax.nn.elu(h)
        out = rgat_conv(h, W2, q2, k2, b2, src, dst, edge_type, HEADS2, OUT2, n)
        return out

    def _L3_gnn_ref(x, edge_index, edge_type, W_rel, W_root, b_rgcn, W_gcn, b_gcn):
        import jax, jax.numpy as jnp
        import numpy as np
        N_NODES = 1250
        N_EDGES = 12500
        N_REL = 34
        DIM = 768

        def _graph_encoder(x, edge_index, edge_type, W_rel, W_root, b_rgcn, W_gcn, b_gcn):
            n = x.shape[0]
            src, dst = (edge_index[0], edge_index[1])
            ones = jnp.ones((src.shape[0],), dtype=x.dtype)
            seg = edge_type * n + dst
            agg = jax.ops.segment_sum(x[src], seg, num_segments=N_REL * n)
            cnt = jax.ops.segment_sum(ones, seg, num_segments=N_REL * n)
            mean = agg.reshape(N_REL, n, -1) / jnp.maximum(cnt, 1.0).reshape(N_REL, n, 1)
            h1 = jnp.einsum('rni,rio->no', mean, W_rel) + x @ W_root + b_rgcn
            xw = h1 @ W_gcn
            deg = jax.ops.segment_sum(ones, dst, num_segments=n) + 1.0
            dinv = jax.lax.rsqrt(deg)
            norm = dinv[src] * dinv[dst]
            out = jax.ops.segment_sum(xw[src] * norm[:, None], dst, num_segments=n)
            out = out + xw * (dinv * dinv)[:, None]
            return out + b_gcn
        return _graph_encoder(x, edge_index, edge_type, W_rel, W_root, b_rgcn, W_gcn, b_gcn)
    edge_index = jnp.stack([src, dst])
    x = _layernorm(x + _L0_gnn_ref(x, edge_index, edge_type_3, L0_gnn_query_embs, L0_gnn_W_rel1, L0_gnn_W_root1, L0_gnn_b1, L0_gnn_W_rel2, L0_gnn_W_root2, L0_gnn_b2, L0_gnn_Wg, L0_gnn_bg, L0_gnn_Wq, L0_gnn_bq), axis=-1)
    x = _layernorm(x + _L1_gnn_ref(x, edge_index, L1_gnn_W, L1_gnn_b), axis=-1)
    x = _layernorm(x + _L2_gnn_ref(x, edge_index, edge_type_3, L2_gnn_W1, L2_gnn_q1, L2_gnn_k1, L2_gnn_b1, L2_gnn_W2, L2_gnn_q2, L2_gnn_k2, L2_gnn_b2), axis=-1)
    x = _layernorm(x + _L3_gnn_ref(x, edge_index, edge_type_34, L3_gnn_W_rel, L3_gnn_W_root, L3_gnn_b_rgcn, L3_gnn_W_gcn, L3_gnn_b_gcn), axis=-1)
    return x

_drawn_inputs = setup_inputs


def setup_inputs(seed=0):
    import zlib

    import numpy as np

    out = dict(_drawn_inputs(seed))
    spreads = {'L0_gnn_b1': (0.0, 0.425),
     'L0_gnn_b2': (0.0, 0.1),
     'L0_gnn_bg': (0.0, 0.376),
     'L0_gnn_bq': (0.0, 0.451),
     'L1_gnn_b': (0.0, 0.1),
     'L2_gnn_b1': (0.0, 0.1),
     'L2_gnn_b2': (0.0, 0.1),
     'L3_gnn_b_rgcn': (0.0, 0.1),
     'L3_gnn_b_gcn': (0.0, 0.1)}
    factors = {'L2_gnn_q1': 8.0, 'L2_gnn_k1': 8.0, 'L2_gnn_q2': 8.0, 'L2_gnn_k2': 8.0}
    for name, (base, spread) in spreads.items():
        noise = np.random.default_rng([zlib.crc32(name.encode()), seed]).standard_normal(out[name].shape)
        drawn = base * np.exp(spread * noise) if base else spread * noise
        out[name] = jnp.asarray(drawn.astype(out[name].dtype))
    for name, factor in factors.items():
        out[name] = (out[name] * factor).astype(out[name].dtype)
    return out
```

```python
from contextlib import ExitStack

import concourse.bass as bass
from concourse import mybir

P = 128
F32 = mybir.dt.float32
BF16 = mybir.dt.bfloat16
I32 = mybir.dt.int32
ALU = mybir.AluOpType
ACT = mybir.ActivationFunctionType
AX = mybir.AxisListType

NODES, FEAT, EDGES = 256, 768, 4352
NT = NODES // P
KC = FEAT // P
EC = EDGES // P
HALF = FEAT // 2
BATCH, QLEN = 8, 64
BN = NODES // BATCH
PAIRS = BN // 2
BLOCKS = PAIRS // 2
R3, R34 = 3, 34
HEADS1 = 4
SLOPE, MASKED = 0.2, -1e30


def build(nc, A):
    with ExitStack() as ctx:
        def sb(name, shape, dt=F32):
            return ctx.enter_context(nc.sbuf_tensor(name, shape, dt))

        def sem(name):
            return ctx.enter_context(nc.semaphore(name))

        PS = ctx.enter_context(nc.psum_tensor("PS", [P, 8, 512], F32))
        W = [sb(f"W{i}", [P, KC, FEAT]) for i in range(2)]
        xN, hN = sb("xN", [P, NT, FEAT]), sb("hN", [P, NT, FEAT])
        xT, hT = sb("xT", [P, KC, NODES]), sb("hT", [P, KC, NODES])
        SMALL = 16 * 11
        MT = [sb(f"MT{i}", [P, KC, NODES]) for i in range(2)]
        CNT = sb("CNT", [P, R3, NT, NODES])
        NRM = sb("NRM", [P, R3, NT, NODES])
        AI = sb("AI", [P, NT, NODES])
        S1 = sb("S1", [P, EC, NODES], BF16)
        arena = sb("arena", [P, 14848])
        selmem = sb("selmem", [P, 3072])
        ident, ones = sb("ident", [P, P]), sb("ones", [P, P])
        iota1 = sb("iota1", [P, NODES])
        relid = sb("relid", [P, R34])
        keys = sb("keys", [P, 4, EC], I32)
        keyf = sb("keyf", [P, 4, EC])
        ekey = sb("ekey", [P, 2, EC])
        biasT = sb("biasT", [P, 3, KC])
        biasN = sb("biasN", [P, 6, FEAT])
        qk1, qk2 = sb("qk1", [P, KC, 2 * HEADS1]), sb("qk2", [P, KC, 2])
        qkT = sb("qkT", [2 * HEADS1, R3 * NODES])
        qkN = sb("qkN", [P, NT, R3, 2 * HEADS1])
        RC = sb("RC", [P, 2, NODES])
        stats, mv = sb("stats", [P, NT, 2, 6]), sb("mv", [P, NT, 2])
        sd, rstd = sb("sd", [P, NT]), sb("rstd", [P, NT])
        eps = sb("eps", [P, 1])
        dinv = sb("dinv", [P, NT])
        rmax, nmax = sb("rmax", [P, 8]), sb("nmax", [P, 8])
        zsum, zinv = sb("zsum", [P, 8]), sb("zinv", [P, 8])

        def view(t, at, n, dt=F32):
            v = t[:, at:at + n]
            return v if dt == F32 else v.bitcast(dt)

        QH = view(arena, 0, 6144).rearrange("p (b f) -> p b f", b=BATCH)
        SIG = [view(arena, 6144 + 1536 * i, 1536) for i in range(2)]
        PRD = [view(arena, 9216 + 1536 * i, 1536) for i in range(2)]
        QD = [view(arena, 12288 + FEAT * i, FEAT) for i in range(2)]
        qiT = SIG[0].rearrange("p (k n) -> p k n", k=KC)
        tanhT = SIG[1].rearrange("p (k n) -> p k n", k=KC)
        alphaT = PRD[0].rearrange("p (k n) -> p k n", k=KC)
        qiN = hN
        qT = [MT[0], MT[1]]
        E = [view(arena, 6144 + 4352 * i, 4352, BF16).rearrange("p (c n) -> p c n", c=EC) for i in range(2)]
        XR = view(arena, 0, 4608).rearrange("p (r t f) -> p r t f", r=R3, t=NT)
        XT = view(arena, 4608, 4608).rearrange("p (r k n) -> p r k n", r=R3, k=KC)
        SC = [view(arena, 9216 + 768 * i, 768) for i in range(2)]
        EX = [view(arena, 10752 + 768 * i, 768) for i in range(2)]
        PT = [view(arena, 12288 + 768 * i, 768).rearrange("p (c n) -> p c n", c=R3 * NT) for i in range(2)]
        SEL = view(selmem, 0, 2048).rearrange("p (i m) -> p i m", i=PAIRS)
        RED = view(selmem, 2048, 512).rearrange("p (i m) -> p i m", i=PAIRS)
        CN = view(selmem, 0, 1536).rearrange("p (t c) -> p t c", t=NT)
        NM = view(selmem, 1536, 1536).rearrange("p (t c) -> p t c", t=NT)
        A34 = [CNT[:, i] for i in range(2)]
        N34 = [NRM[:, i] for i in range(2)]

        keys_in, x_in, q_in, small_in, out_done = (sem(n) for n in ("keys_in", "x_in", "q_in", "small_in", "out_done"))
        w_in = [sem("w_in0"), sem("w_in1")]
        qd_in = [sem("qd_in0"), sem("qd_in1")]
        w_used = sem("w_used")
        pool_step, consts = sem("pool_step"), sem("consts")
        dve_step, act_step = sem("dve_step"), sem("act_step")
        sel_ready, s1_ready, e_ready = sem("sel_ready"), sem("s1_ready"), sem("e_ready")
        cnt_summed, cnt_copied = sem("cnt_summed"), sem("cnt_copied")
        deg_spread, nrm_ready = sem("deg_spread"), sem("nrm_ready")
        ai_ready, deg_summed, dinv_sd, dinv_ready = sem("ai_ready"), sem("deg_summed"), sem("dinv_sd"), sem("dinv_ready")
        agg_done, mt_copied = sem("agg_done"), sem("mt_copied")
        qg_copied = sem("qg_copied")
        relu_done = sem("relu_done")
        hg_copied = sem("hg_copied")
        sums_done, attn_done, prod_done, red_done = sem("sums_done"), sem("attn_done"), sem("prod_done"), sem("red_done")
        qi_copied, qi_turned, qiT_copied, tanh_done = sem("qi_copied"), sem("qi_turned"), sem("qiT_copied"), sem("tanh_done")
        alpha_done, gate_done = sem("alpha_done"), sem("gate_done")
        h_turned, hN_ready = sem("h_turned"), sem("hN_ready")
        var_ready, sd_ready, ln_done, x_turned, xT_ready = (sem(n) for n in ("var_ready", "sd_ready", "ln_done", "x_turned", "xT_ready"))
        gcn_scaled, gcn_sum = sem("gcn_scaled"), sem("gcn_sum")
        cn_turned, cn_ready = sem("cn_turned"), sem("cn_ready")
        xr_copied, xr_turned, xrT_copied = sem("xr_copied"), sem("xr_turned"), sem("xrT_copied")
        qk_done, qk_copied, qkn_done, qkn_copied = sem("qk_done"), sem("qk_copied"), sem("qkn_done"), sem("qkn_copied")
        key_spread, score_done, max_ready, exp_done = sem("key_spread"), sem("score_done"), sem("max_ready"), sem("exp_done")
        p_ready, p_turned, pt_copied, att_sum, att_done = (sem(n) for n in ("p_ready", "p_turned", "pt_copied", "att_sum", "att_done"))
        elu_min, elu_exp = sem("elu_min"), sem("elu_exp")
        h1_copied = sem("h1_copied")

        turned = lambda a: a.rearrange("(p t) n -> p t n", t=KC)
        WgT, WqT = A["WgT"], A["WqT"]
        gate_w = [WgT[0:FEAT], WqT[0:FEAT], WqT[FEAT:]]
        stream = [WgT[FEAT:], A["W_root1"]] + [A["W_rel1"][r] for r in range(R3)] + gate_w
        stream += [A["W_root2"]] + [A["W_rel2"][r] for r in range(R3)] + gate_w
        stream += [A["L1_W"]] + [A["W1"][r] for r in range(R3)] + [A["W2"][r] for r in range(R3)] + [A["L3_root"]]
        FIRST34 = len(stream)
        LOOP34 = (R34 - 2) // 2

        block = ctx.enter_context(nc.Block())

        @block.sync
        def _(sp):
            for i, n in enumerate(("src", "dst", "t3", "t34")):
                sp.dma_start(keys[:, i, :], A[n].rearrange("(p c) -> p c", c=EC)).then_inc(keys_in, 16)
            for i in range(2):
                sp.dma_start(qT[i][:], turned(A["qT"])[:, :, i * NODES:(i + 1) * NODES]).then_inc(q_in, 16)
            for m, w in enumerate(stream):
                if m >= 2:
                    sp.wait_ge(w_used, m - 1)
                sp.dma_start(W[m % 2][:], turned(w)).then_inc(w_in[m % 2], 16)
            with sp.Fori(0, LOOP34 + 1) as i:
                for j in range(2):
                    sp.wait_ge(w_used, i * 2 + (FIRST34 + j - 1))
                    sp.dma_start(W[(FIRST34 + j) % 2][:], A["L3_rel"][bass.ds(i * 2 + j, 1)].rearrange("a (p t) n -> p (a t) n", t=KC)
                                 ).then_inc(w_in[(FIRST34 + j) % 2], 16)
            m = FIRST34 + R34
            sp.wait_ge(w_used, m - 1)
            sp.dma_start(W[m % 2][:], turned(A["L3_gcn"])).then_inc(w_in[m % 2], 16)
            sp.wait_ge(ln_done, 4)
            sp.dma_start(A["out"].rearrange("(t p) f -> p t f", p=P), xN[:]).then_inc(out_done, 16)
            sp.wait_ge(out_done, 16)

        @block.gpsimd
        def _(pool):
            steps = [0]

            def then(ins):
                steps[0] += 1
                ins.then_inc(pool_step, 1)
                pool.wait_ge(pool_step, steps[0])

            pool.dma_start(xN[:], A["x"].rearrange("(t p) f -> p t f", p=P)).then_inc(x_in, 16)
            pool.dma_start(xT[:], turned(A["xT"])).then_inc(x_in, 16)
            for i, n in enumerate(("b1", "b2", "bq")):
                pool.dma_start(biasT[:, i, :], A[n].rearrange("(p t) -> p t", t=KC)).then_inc(small_in, 16)
            for i, n in enumerate(("bg", "L1_b", "L2_b1", "L2_b2", "b_rgcn", "b_gcn")):
                pool.dma_start(biasN[:, i, :], A[n].partition_broadcast(P)).then_inc(small_in, 16)
            for t, n in ((qk1, "qk1"), (qk2, "qk2")):
                pool.dma_start(t[:], turned(A[n])).then_inc(small_in, 16)
            then(nc.gpsimd.iota(iota1[:], pattern=[[1, NODES]], base=1, channel_multiplier=0,
                                allow_small_or_imprecise_dtypes=True))
            then(nc.gpsimd.iota(relid[:], pattern=[[1, R34]], base=0, channel_multiplier=0,
                                allow_small_or_imprecise_dtypes=True))
            then(nc.gpsimd.memset(ones[:], 1.0))
            then(nc.gpsimd.memset(RED, 0.0))
            for j in range(2):
                v = RED[64 * j:64 * j + 64]
                then(nc.gpsimd.affine_select(out=v, in_=v, compare_op=ALU.not_equal, fill=1.0, base=j,
                                             pattern=[[2, PAIRS], [-1, BN]], channel_multiplier=0))
            then(nc.gpsimd.memset(ident[:], 0.0))
            nc.gpsimd.affine_select(out=ident[:], in_=ident[:], compare_op=ALU.not_equal, fill=1.0, base=0,
                                    pattern=[[-1, P]], channel_multiplier=1).then_inc(consts, 1)
            for g in range(2):
                with pool.Fori(0, BATCH // 2) as i:
                    for s in range(2):
                        if g == 0:
                            pool.wait_ge(cnt_summed, R3)
                            pool.wait_ge(prod_done, i * (2 * BLOCKS) + 1)
                        else:
                            pool.wait_ge(prod_done, i * (2 * BLOCKS) + (g * BATCH + s - 1) * BLOCKS + 1)
                        for j in range(2):
                            pool.dma_start(QD[s][64 * j:64 * j + 64, :],
                                           A["q"][bass.ds(i * (2 * QLEN) + s * QLEN, QLEN), :]).then_inc(qd_in[s], 16)

        @block.tensor
        def _(pe):
            def weights(m):
                pe.wait_ge(w_in[m % 2], 16 * (m // 2 + 1))

            def natural(bank, T, Wm, first=True, last=True):
                for t in range(NT):
                    for h in range(2):
                        for k in range(KC):
                            mm = pe.matmul(PS[:, bank + 2 * t + h, 0:HALF], T[:, k, t * P:(t + 1) * P],
                                           Wm[:, k, h * HALF:(h + 1) * HALF],
                                           start=first and k == 0, stop=last and k == KC - 1)
                return mm

            def turned_product(bank, T, Wm, first=True, last=True):
                for m in range(KC):
                    for k in range(KC):
                        mm = pe.matmul(PS[:, bank + m // 2, (m % 2) * NODES:(m % 2 + 1) * NODES], Wm[:, k, m::KC],
                                       T[:, k, :], start=first and k == 0 and m % 2 == 0,
                                       stop=last and k == KC - 1 and m % 2 == 1, skip_group_check=True)
                return mm

            def counts(n, e):
                pe.wait_ge(e_ready, n + 1)
                pe.wait_ge(cnt_copied, n)
                for s in range(NT):
                    for c in range(EC):
                        mm = pe.matmul(PS[:, 4, s * NODES:(s + 1) * NODES], S1[:, c, s * P:(s + 1) * P], E[e][:, c, :],
                                       start=c == 0, stop=c == EC - 1)
                mm.then_inc(cnt_summed, 1)

            def spread_counts(n, cnt):
                pe.wait_ge(cnt_copied, n + 1)
                pe.wait_ge(nrm_ready, n)
                for s in range(NT):
                    mm = pe.matmul(PS[:, 5, 0:NODES], ones[:], cnt[:, s, :], start=s == 0, stop=s == NT - 1)
                mm.then_inc(deg_spread, 1)

            def aggregate(n, x, nrm):
                for j in range(3):
                    if not isinstance(n, int) or n * 3 + j > 1:
                        pe.wait_ge(mt_copied, n * 3 + j - 1)
                    for kk in range(2):
                        k = 2 * j + kk
                        for s in range(NT):
                            mm = pe.matmul(PS[:, 6 + j % 2, kk * NODES:(kk + 1) * NODES], x[:, s, k::KC], nrm[:, s, :],
                                           start=s == 0, stop=s == NT - 1)
                    mm.then_inc(agg_done, 1)

            def to_natural(bank, T):
                for t in range(NT):
                    for k in range(KC):
                        mm = pe.transpose(PS[:, bank + 2 * t + k // 4, (k % 4) * P:(k % 4 + 1) * P],
                                          T[:, k, t * P:(t + 1) * P], ident[:])
                return mm

            def to_turned(bank, N):
                for k in range(KC):
                    for t in range(NT):
                        mm = pe.transpose(PS[:, bank + k // 2, (k % 2) * NODES + t * P:(k % 2) * NODES + (t + 1) * P],
                                          N[:, t, k::KC], ident[:])
                return mm

            pe.sem_inc(red_done, 1)
            weights(0)
            pe.wait_ge(q_in, 32)
            for i in range(2):
                mm = natural(4 * i, qT[i], W[0])
            mm.then_inc(w_used, 1)

            pe.wait_ge(consts, 1)
            pe.wait_ge(s1_ready, 1)
            pe.wait_ge(qg_copied, 2)
            for r in range(R3):
                pe.wait_ge(e_ready, r + 1)
                if r:
                    pe.wait_ge(cnt_copied, r)
                for s in range(NT):
                    for c in range(EC):
                        mm = pe.matmul(PS[:, 4, s * NODES:(s + 1) * NODES], S1[:, c, s * P:(s + 1) * P], E[r % 2][:, c, :],
                                       start=c == 0, stop=c == EC - 1)
                mm.then_inc(cnt_summed, 1)
                pe.wait_ge(cnt_copied, r + 1)
                if r:
                    pe.wait_ge(nrm_ready, r)
                for s in range(NT):
                    mm = pe.matmul(PS[:, 5, 0:NODES], ones[:], CNT[:, r, s, :], start=s == 0, stop=s == NT - 1)
                mm.then_inc(deg_spread, 1)
            pe.wait_ge(ai_ready, 1)
            for t in range(NT):
                for s in range(NT):
                    mm = pe.matmul(PS[:, 4, t:t + 1], AI[:, s, t * P:(t + 1) * P], ones[:, 0:1], start=s == 0, stop=s == NT - 1)
            mm.then_inc(deg_summed, 1)

            for g in range(2):
                m0 = 1 + 7 * g
                src, srcT = (xN, xT) if g == 0 else (hN, hT)
                if g == 0:
                    pe.wait_ge(x_in, 32)
                else:
                    pe.wait_ge(gate_done, 1)
                weights(m0)
                if g:
                    pe.wait_ge(hN_ready, 1)
                turned_product(0, srcT, W[m0 % 2], last=False).then_inc(w_used, 1)
                for r in range(R3):
                    if g == 0:
                        pe.wait_ge(nrm_ready, r + 1)
                    n = g * R3 + r
                    aggregate(n, src, NRM[:, r])
                    pe.wait_ge(mt_copied, 3 * (n + 1))
                    weights(m0 + 1 + r)
                    mm = turned_product(0, MT[n % 2], W[(m0 + 1 + r) % 2], first=False, last=r == R3 - 1)
                    mm.then_inc(w_used, 1)
                pe.wait_ge(relu_done, g + 1)
                weights(m0 + 4)
                natural(4, hT, W[(m0 + 4) % 2]).then_inc(w_used, 1)
                pe.wait_ge(hg_copied, 8 * (g + 1))
                pe.wait_ge(sel_ready, 2)
                with pe.Fori(0, NT) as t:
                    nb0 = t * (4 * BLOCKS) + g * BATCH * BLOCKS

                    def reduce(q):
                        pe.wait_ge(prod_done, nb0 + (q + 2))
                        for u in range(2):
                            i = 2 * (q % BLOCKS) + u
                            b = q // BLOCKS
                            for h in range(2):
                                mm = pe.matmul(PS[32 * b:32 * b + 32, 6 + h, 0:HALF], RED[:, i, :],
                                               PRD[q % 2][:, u * FEAT + h * HALF:u * FEAT + (h + 1) * HALF],
                                               start=i == 0, stop=i == PAIRS - 1)
                        mm.then_inc(red_done, 1)

                    for q in range(4 * BLOCKS):
                        i0, b = 2 * (q % BLOCKS), q // BLOCKS
                        if q >= 2 or g:
                            pe.wait_ge(attn_done, nb0 + (q - 1))
                        base = 3 * (q % 2)
                        for u, lo, hi, bank, at in ((0, 0, 512, 0, 0), (0, 512, 768, 1, 0), (1, 0, 256, 1, 256), (1, 256, 768, 2, 0)):
                            mm = pe.matmul(PS[:, base + bank, at:at + hi - lo], SEL[0:96, i0 + u, :],
                                           QH[0:96, bass.ds(t * 4 + b, 1), lo:hi].rearrange("p a f -> p (a f)"), start=True, stop=True)
                        mm.then_inc(sums_done, 1)
                        if q >= 2:
                            if q == 2:
                                pe.wait_ge(qi_copied, t + (2 * g + 1))
                            reduce(q - 2)
                    reduce(4 * BLOCKS - 2)
                    reduce(4 * BLOCKS - 1)
                pe.wait_ge(qi_copied, 2 * g + 3)
                to_turned(0, qiN).then_inc(qi_turned, 1)
                weights(m0 + 5)
                turned_product(3, hT, W[(m0 + 5) % 2], last=False).then_inc(w_used, 1)
                pe.wait_ge(qiT_copied, g + 1)
                weights(m0 + 6)
                turned_product(3, qiT, W[(m0 + 6) % 2], first=False).then_inc(w_used, 1)
                pe.wait_ge(gate_done, g + 1)
                to_natural(0, hT).then_inc(h_turned, 1)

            def turn_x(n):
                pe.wait_ge(ln_done, n)
                to_turned(0, xN).then_inc(x_turned, 1)
                pe.wait_ge(xT_ready, n)

            turn_x(1)
            m = 15
            weights(m)
            natural(4, xT, W[m % 2]).then_inc(w_used, 1)

            def gcn_aggregate(n):
                pe.wait_ge(gcn_scaled, n)
                for t in range(NT):
                    for h in range(2):
                        for s in range(NT):
                            mm = pe.matmul(PS[:, 2 * t + h, 0:HALF], AI[:, s, t * P:(t + 1) * P],
                                           hN[:, s, h * HALF:(h + 1) * HALF], start=s == 0, stop=s == NT - 1)
                mm.then_inc(gcn_sum, 1)

            gcn_aggregate(1)
            for t in range(NT):
                for c in range(R3 * NT):
                    mm = pe.transpose(PS[:, 4 + 2 * t + c // 4, (c % 4) * P:(c % 4 + 1) * P],
                                      CNT[:, c // NT, c % NT, t * P:(t + 1) * P], ident[:])
            mm.then_inc(cn_turned, 1)

            turn_x(2)
            u0 = 0
            for l, (H, qk, T) in enumerate(((HEADS1, qk1, xT), (1, qk2, hT))):
                m0 = 16 + R3 * l
                for r in range(R3):
                    m = m0 + r
                    weights(m)
                    if r == 0:
                        pe.wait_ge(cn_ready, 1)
                    n = l * R3 + r
                    if n >= 2:
                        pe.wait_ge(xr_copied, n - 1)
                    natural(4 * (r % 2), T, W[m % 2]).then_inc(w_used, 1)
                pe.wait_ge(xr_copied, R3 * (l + 1))
                for j in range(9):
                    if l * 9 + j >= 2:
                        pe.wait_ge(xrT_copied, l * 9 + j - 1)
                    for kk in range(2):
                        r, k = divmod(2 * j + kk, KC)
                        for t in range(NT):
                            mm = pe.transpose(PS[:, j % 2, kk * NODES + t * P:kk * NODES + (t + 1) * P], XR[:, r, t, k::KC], ident[:])
                    mm.then_inc(xr_turned, 1)
                pe.wait_ge(small_in, SMALL)
                pe.wait_ge(xrT_copied, 9 * (l + 1))
                for r in range(R3):
                    for k in range(KC):
                        mm = pe.matmul(PS[0:2 * H, 2 + r // 2, (r % 2) * NODES:(r % 2 + 1) * NODES], qk[:, k, :], XT[:, r, k, :],
                                       start=k == 0, stop=k == KC - 1)
                mm.then_inc(qk_done, 1)
                pe.wait_ge(qk_copied, l + 1)
                for t in range(NT):
                    for r in range(R3):
                        mm = pe.transpose(PS[:, 0, (t * R3 + r) * 2 * H:(t * R3 + r + 1) * 2 * H],
                                          qkT[0:2 * H, r * NODES + t * P:r * NODES + (t + 1) * P], ident[0:2 * H, 0:2 * H])
                mm.then_inc(qkn_done, 1)
                for h in range(H):
                    if h:
                        pe.wait_ge(score_done, u0 + 2 * h)
                    sel = ident[0:2 * H, H + h:H + h + 1].to_broadcast([2 * H, P])
                    pe.matmul(PS[:, 4, :], sel, qkT[0:2 * H, 0:512], start=True, stop=True)
                    pe.matmul(PS[:, 5, 0:256], sel, qkT[0:2 * H, 512:768], start=True, stop=True).then_inc(key_spread, 1)
                    for t in range(NT):
                        u = u0 + 2 * h + t
                        pe.wait_ge(p_ready, u + 1)
                        if u > u0:
                            pe.wait_ge(pt_copied, u)
                        for c in range(R3 * NT):
                            mm = pe.transpose(PS[:, 6 + c // 4, (c % 4) * P:(c % 4 + 1) * P], EX[u % 2][:, c * P:(c + 1) * P], ident[:])
                        mm.then_inc(p_turned, 1)
                        pe.wait_ge(pt_copied, u + 1)
                        if u == u0:
                            pe.wait_ge(qkn_copied, l + 1)
                        width = min(FEAT // H, HALF)
                        for part in range(FEAT // H // width):
                            at = h * (FEAT // H) + part * width
                            for c in range(R3 * NT):
                                mm = pe.matmul(PS[:, 2 * t + at // HALF, at % HALF:at % HALF + width], PT[u % 2][:, c, :],
                                               XR[:, c // NT, c % NT, at:at + width], start=c == 0, stop=c == R3 * NT - 1)
                        mm.then_inc(att_sum, 1)
                u0 += 2 * H
                if l == 0:
                    pe.wait_ge(att_done, 1)
                    to_turned(0, hN).then_inc(h_turned, 1)
                    pe.wait_ge(hN_ready, 2)

            turn_x(3)
            m = FIRST34 - 1
            weights(m)
            pe.wait_ge(ln_done, 3)
            natural(0, xT, W[m % 2], last=False).then_inc(w_used, 1)
            counts(R3, 1)
            spread_counts(R3, A34[0])

            def relation(r, j, nxt=True, last=False):
                if nxt:
                    counts(r + (R3 + 1), j % 2)
                pe.wait_ge(nrm_ready, r + (R3 + 1))
                aggregate(r + 2 * R3, xN, N34[j])
                if nxt:
                    spread_counts(r + (R3 + 1), A34[1 - j])
                pe.wait_ge(mt_copied, (r + (2 * R3 + 1)) * 3)
                slot = (FIRST34 + j) % 2
                pe.wait_ge(w_in[slot], (r - j) * 8 + 16 * ((FIRST34 + j) // 2 + 1))
                natural(0, MT[j], W[slot], first=False, last=last).then_inc(w_used, 1)

            with pe.Fori(0, LOOP34) as i:
                for j in range(2):
                    relation(i * 2 + j, j)
            relation(R34 - 2, 0)
            relation(R34 - 1, 1, nxt=False, last=True)
            pe.wait_ge(h1_copied, 1)
            to_turned(4, hN).then_inc(h_turned, 1)
            pe.wait_ge(hN_ready, 3)
            m = FIRST34 + R34
            weights(m)
            natural(4, hT, W[m % 2]).then_inc(w_used, 1)
            gcn_aggregate(2)

        @block.scalar
        def _(act):
            def turned_out(bank):
                return PS[:, bank:bank + 3, :].rearrange("p b (k n) -> p (b k) n", k=2)

            act.wait_ge(small_in, SMALL)

            def counts_copy(n, cnt):
                act.wait_ge(cnt_summed, n + 1)
                nc.scalar.copy(cnt, PS[:, 4, :].rearrange("p (s n) -> p s n", s=NT)).then_inc(cnt_copied, 1)

            def mt_copy(n, buf):
                for j in range(3):
                    act.wait_ge(agg_done, n * 3 + (j + 1))
                    nc.scalar.copy(MT[buf][:, 2 * j:2 * j + 2, :], PS[:, 6 + j % 2, :].rearrange("p (k n) -> p k n", k=2)
                                   ).then_inc(mt_copied, 1)

            for r in range(R3):
                counts_copy(r, CNT[:, r])
            act.wait_ge(deg_summed, 1)
            nc.scalar.activation(dinv[:], PS[:, 4, 0:NT], ACT.Sqrt).then_inc(dinv_sd, 1)

            for g in range(2):
                for r in range(R3):
                    n = g * R3 + r
                    if r >= 2:
                        act.wait_ge(w_used, 1 + 7 * g + 1 + (r - 1))
                    mt_copy(n, n % 2)
                act.wait_ge(w_used, 7 * g + 5)
                for m in range(KC):
                    ins = nc.scalar.activation(hT[:, m, :], PS[:, m // 2, (m % 2) * NODES:(m % 2 + 1) * NODES], ACT.Relu,
                                               bias=biasT[:, g, m:m + 1])
                ins.then_inc(relu_done, 1)
                act.wait_ge(w_used, 7 * g + 6)
                for b in range(0, BATCH, 2):
                    q, t = b % 4, b // 4
                    nc.scalar.copy(QH[64:96, b, :].rearrange("p (h f) -> p h f", h=2),
                                   PS[32 * q:32 * q + 32, 4 + 2 * t:6 + 2 * t, 0:HALF]).then_inc(hg_copied, 1)
                with act.Fori(0, BATCH * BLOCKS // 2) as i:
                    for q in range(2):
                        nb = i * 2 + (q + g * BATCH * BLOCKS)
                        act.wait_ge(sums_done, nb + 1)
                        act.wait_ge(prod_done, nb if q or g else i * 2 + 1)
                        nc.scalar.activation(SIG[q], PS[:, 3 * q:3 * q + 3, :].rearrange("p b n -> p (b n)"), ACT.Sigmoid
                                             ).then_inc(attn_done, 1)
                act.wait_ge(qiT_copied, g + 1)
                nc.scalar.activation(tanhT, turned_out(0), ACT.Tanh).then_inc(tanh_done, 1)
                act.wait_ge(w_used, 7 * g + 8)
                for m in range(KC):
                    ins = nc.scalar.activation(alphaT[:, m, :], PS[:, 3 + m // 2, (m % 2) * NODES:(m % 2 + 1) * NODES],
                                               ACT.Sigmoid, bias=biasT[:, 2, m:m + 1])
                ins.then_inc(alpha_done, 1)

            def norm_x(n):
                act.wait_ge(var_ready, n)
                nc.scalar.activation(sd[:], mv[:, :, 1], ACT.Sqrt, bias=eps[:, 0:1]).then_inc(sd_ready, 1)

            def turn_x(n):
                act.wait_ge(x_turned, n)
                nc.scalar.copy(xT[:], turned_out(0)).then_inc(xT_ready, 1)

            def scale_rows(n):
                act.wait_ge(w_used, 16 if n == 1 else FIRST34 + R34 + 1)
                if n == 1:
                    act.wait_ge(dinv_ready, 1)
                for t in range(NT):
                    ins = nc.scalar.activation(hN[:, t, :].rearrange("p (h f) -> p h f", h=2), PS[:, 4 + 2 * t:6 + 2 * t, 0:HALF],
                                               ACT.Copy, scale=dinv[:, t:t + 1])
                ins.then_inc(gcn_scaled, 1)

            norm_x(1)
            turn_x(1)
            scale_rows(1)
            norm_x(2)
            turn_x(2)
            u0 = 0
            for l, H in enumerate((HEADS1, 1)):
                for r in range(R3):
                    act.wait_ge(w_used, 17 + l * R3 + r)
                    for t in range(NT):
                        ins = nc.scalar.copy(XR[:, r, t, :].rearrange("p (h f) -> p h f", h=2),
                                             PS[:, 4 * (r % 2) + 2 * t:4 * (r % 2) + 2 * t + 2, 0:HALF])
                    ins.then_inc(xr_copied, 1)
                act.wait_ge(qkn_copied, l + 1)
                for h in range(H):
                    act.wait_ge(key_spread, u0 // 2 + h + 1)
                    for t in range(NT):
                        u = u0 + 2 * h + t
                        if u >= 2:
                            act.wait_ge(exp_done, u - 1)
                        for r in range(R3):
                            ins = nc.scalar.activation(SC[u % 2][:, r * NODES:(r + 1) * NODES],
                                                       PS[:, 4 + r // 2, (r % 2) * NODES:(r % 2 + 1) * NODES], ACT.Identity,
                                                       bias=qkN[:, t, r, h:h + 1])
                        ins.then_inc(score_done, 1)
                        act.wait_ge(max_ready, u + 1)
                        if u >= 2:
                            act.wait_ge(p_turned, u - 1)
                        nc.scalar.activation(EX[u % 2], SC[u % 2], ACT.Exp, bias=nmax[:, u % 8:u % 8 + 1]).then_inc(exp_done, 1)
                u0 += 2 * H
                if l == 0:
                    act.wait_ge(elu_min, 1)
                    nc.scalar.activation(xT[:], MT[0][:], ACT.Exp).then_inc(elu_exp, 1)
                    act.wait_ge(h_turned, 3)
                    nc.scalar.copy(hT[:], turned_out(0)).then_inc(hN_ready, 1)
            norm_x(3)
            turn_x(3)
            counts_copy(R3, A34[0])

            def relation(r, j, nxt=True):
                if nxt:
                    act.wait_ge(nrm_ready, r + R3)
                    counts_copy(r + (R3 + 1), A34[1 - j])
                act.wait_ge(w_used, r + (FIRST34 - 1))
                mt_copy(r + 2 * R3, j)

            with act.Fori(0, LOOP34) as i:
                for j in range(2):
                    relation(i * 2 + j, j)
            relation(R34 - 2, 0)
            relation(R34 - 1, 1, nxt=False)
            act.wait_ge(h_turned, 4)
            nc.scalar.copy(hT[:], turned_out(4)).then_inc(hN_ready, 1)
            scale_rows(2)
            norm_x(4)

        @block.vector
        def _(dve):
            steps = [0]

            def then(ins):
                steps[0] += 1
                ins.then_inc(dve_step, 1)
                dve.wait_ge(dve_step, steps[0])

            V = nc.vector
            dve.sem_inc(prod_done, 1)
            dve.sem_inc(qi_copied, 1)

            def onehot(out, key):
                return V.tensor_tensor(out, iota1[:].unsqueeze(1).to_broadcast([P, EC, NODES]),
                                       key.unsqueeze(2).to_broadcast([P, EC, NODES]), ALU.is_equal)

            then(V.memset(eps[:], 1e-5))
            dve.wait_ge(keys_in, 64)
            then(V.tensor_copy(keyf[:], keys[:]))
            then(V.tensor_scalar(keyf[:, 0:2, :], keyf[:, 0:2, :], 1.0, None, ALU.add))
            dve.wait_ge(consts, 1)
            onehot(S1[:], keyf[:, 0, :]).then_inc(s1_ready, 1)
            sv = SEL.rearrange("p i (j l) -> p (i j) l", j=2)
            V.tensor_copy(sv[0:64], ident[0:64, 0:64].unsqueeze(1).to_broadcast([64, 2 * PAIRS, QLEN])).then_inc(sel_ready, 1)
            V.tensor_copy(sv[64:96], ident[64:96, 64:96].unsqueeze(2).to_broadcast([32, 2 * PAIRS, QLEN])).then_inc(sel_ready, 1)
            dve.wait_ge(w_used, 1)
            dve.wait_ge(small_in, SMALL)
            for i in range(2):
                for t in range(NT):
                    for j in range(2):
                        ins = V.tensor_tensor(QH[0:64, 4 * i + 2 * t + j, :].rearrange("p (h f) -> p h f", h=2),
                                              PS[64 * j:64 * j + 64, 4 * i + 2 * t:4 * i + 2 * t + 2, 0:HALF],
                                              biasN[0:64, 0, :].rearrange("p (h f) -> p h f", h=2), ALU.add)
                ins.then_inc(qg_copied, 1)

            for r in range(R3 + 1):
                if r < R3:
                    then(V.scalar_tensor_tensor(out=ekey[:, r % 2, :], in0=keyf[:, 2, :], scalar=float(r), in1=keyf[:, 1, :],
                                                op0=ALU.is_equal, op1=ALU.mult))
                    if r == 2:
                        dve.wait_ge(cnt_summed, 1)
                    onehot(E[r % 2], ekey[:, r % 2, :]).then_inc(e_ready, 1)
                if r >= 1:
                    n = r - 1
                    dve.wait_ge(deg_spread, n + 1)
                    then(V.tensor_scalar(RC[:, 0, :], PS[:, 5, 0:NODES], 1.0, None, ALU.max))
                    then(V.reciprocal(RC[:, 1, :], RC[:, 0, :]))
                    V.tensor_tensor(NRM[:, n], CNT[:, n], RC[:, 1, :].unsqueeze(1).to_broadcast([P, NT, NODES]), ALU.mult
                                    ).then_inc(nrm_ready, 1)
            then(V.tensor_tensor(AI[:], CNT[:, 0], CNT[:, 1], ALU.add))
            then(V.tensor_tensor(AI[:], AI[:], CNT[:, 2], ALU.add))
            for s in range(NT):
                ins = V.tensor_tensor(AI[:, s, s * P:(s + 1) * P], AI[:, s, s * P:(s + 1) * P], ident[:], ALU.add)
            ins.then_inc(ai_ready, 1)
            dve.wait_ge(dinv_sd, 1)
            V.reciprocal(dinv[:], dinv[:]).then_inc(dinv_ready, 1)

            for g in range(2):
                dve.wait_ge(w_used, 7 * g + 6)
                for b in range(1, BATCH, 2):
                    q, t = b % 4, b // 4
                    V.tensor_copy(QH[64:96, b, :].rearrange("p (h f) -> p h f", h=2),
                                  PS[32 * q:32 * q + 32, 4 + 2 * t:6 + 2 * t, 0:HALF]).then_inc(hg_copied, 1)
                with dve.Fori(0, NT) as t:
                    nb0 = t * (4 * BLOCKS) + g * BATCH * BLOCKS
                    for q in range(4 * BLOCKS):
                        b = q // BLOCKS
                        if q % BLOCKS == 0:
                            dve.wait_ge(qd_in[b % 2], t * 64 + (g * 4 * 32 + (b // 2 + 1) * 32))
                        dve.wait_ge(attn_done, nb0 + (q + 1))
                        dve.wait_ge(red_done, nb0 + q if q or g else t * (4 * BLOCKS) + 1)
                        V.tensor_tensor(PRD[q % 2].rearrange("p (u f) -> p u f", u=2), SIG[q % 2].rearrange("p (u f) -> p u f", u=2),
                                        QD[b % 2].unsqueeze(1).to_broadcast([P, 2, FEAT]), ALU.mult).then_inc(prod_done, 1)
                    dve.wait_ge(red_done, nb0 + (4 * BLOCKS + 1))
                    V.tensor_copy(qiN[:, bass.ds(t, 1), :].rearrange("p a (h f) -> p (a h) f", h=2), PS[:, 6:8, 0:HALF]).then_inc(qi_copied, 1)
                dve.wait_ge(qi_turned, g + 1)
                V.tensor_copy(qiT, PS[:, 0:3, :].rearrange("p b (k n) -> p (b k) n", k=2)).then_inc(qiT_copied, 1)
                dve.wait_ge(tanh_done, g + 1)
                then(V.tensor_tensor(tanhT, tanhT, hT[:], ALU.subtract))
                dve.wait_ge(alpha_done, g + 1)
                then(V.tensor_tensor(tanhT, tanhT, alphaT, ALU.mult))
                V.tensor_tensor(hT[:], hT[:], tanhT, ALU.add).then_inc(gate_done, 1)
                dve.wait_ge(h_turned, g + 1)
                for t in range(NT):
                    ps = PS[:, 2 * t:2 * t + 2, :].rearrange("p b n -> p (b n)")[:, 0:FEAT].rearrange("p (k n) -> p k n", k=KC)
                    if g == 0:
                        ins = V.tensor_copy(hN[:, t, :].rearrange("p (n k) -> p k n", k=KC), ps)
                    else:
                        xv = xN[:, t, :].rearrange("p (n k) -> p k n", k=KC)
                        ins = V.tensor_tensor(xv, ps, xv, ALU.add)
                if g == 0:
                    ins.then_inc(hN_ready, 1)
                else:
                    then(ins)

            def layer_norm(n):
                for t in range(NT):
                    for h in range(2):
                        ins = V.bn_stats(stats[:, t, h, :], xN[:, t, h * HALF:(h + 1) * HALF])
                then(ins)
                for t in range(NT):
                    ins = V.bn_aggr(mv[:, t, :], stats[:, t, :, :])
                ins.then_inc(var_ready, 1)
                dve.wait_ge(sd_ready, n)
                then(V.reciprocal(rstd[:], sd[:]))
                for t in range(NT):
                    ins = V.tensor_scalar(xN[:, t, :], xN[:, t, :], mv[:, t, 0:1], rstd[:, t:t + 1], ALU.subtract, ALU.mult)
                ins.then_inc(ln_done, 1)
                dve.wait_ge(ln_done, n)

            def gcn_out(n, bias):
                then(V.tensor_tensor(xN[:], xN[:], biasN[:, bias, :].unsqueeze(1).to_broadcast([P, NT, FEAT]), ALU.add))
                dve.wait_ge(gcn_sum, n)
                for t in range(NT):
                    xv = xN[:, t, :].rearrange("p (h f) -> p h f", h=2)
                    ins = V.scalar_tensor_tensor(out=xv, in0=PS[:, 2 * t:2 * t + 2, 0:HALF], scalar=dinv[:, t:t + 1], in1=xv,
                                                 op0=ALU.mult, op1=ALU.add)
                then(ins)

            layer_norm(1)
            dve.wait_ge(x_turned, 1)
            gcn_out(1, 1)
            layer_norm(2)
            dve.wait_ge(x_turned, 2)
            dve.wait_ge(cn_turned, 1)
            for t in range(NT):
                ins = V.tensor_copy(CN[:, t, :], PS[:, 4 + 2 * t:6 + 2 * t, :].rearrange("p b n -> p (b n)")[:, 0:FEAT])
            then(ins)
            V.tensor_scalar(NM, CN, 0.5, MASKED, ALU.is_lt, ALU.mult).then_inc(cn_ready, 1)
            dve.wait_ge(cn_ready, 1)

            u0 = 0
            for l, (H, bias) in enumerate(((HEADS1, 2), (1, 3))):
                for j in range(9):
                    dve.wait_ge(xr_turned, l * 9 + j + 1)
                    r, k = divmod(2 * j, KC)
                    V.tensor_copy(XT[:, r, k:k + 2, :], PS[:, j % 2, :].rearrange("p (k n) -> p k n", k=2)).then_inc(xrT_copied, 1)
                dve.wait_ge(qk_done, l + 1)
                V.tensor_copy(qkT[0:2 * H, :], PS[0:2 * H, 2:4, :].rearrange("p b n -> p (b n)")[:, 0:R3 * NODES]).then_inc(qk_copied, 1)
                dve.wait_ge(qkn_done, l + 1)
                V.tensor_copy(qkN[:, :, :, 0:2 * H], PS[:, 0, 0:NT * R3 * 2 * H].rearrange("p (t r h) -> p t r h", t=NT, r=R3)
                              ).then_inc(qkn_copied, 1)
                for h in range(H):
                    for t in range(NT):
                        u = u0 + 2 * h + t
                        c = u % 8
                        dve.wait_ge(score_done, u + 1)
                        then(V.scalar_tensor_tensor(out=SC[u % 2], in0=SC[u % 2], scalar=SLOPE, in1=SC[u % 2],
                                                    op0=ALU.mult, op1=ALU.max))
                        then(V.tensor_tensor_reduce(SC[u % 2], SC[u % 2], NM[:, t, :], 1.0, -3e38, ALU.add, ALU.max,
                                                    rmax[:, c:c + 1]))
                        V.tensor_scalar(nmax[:, c:c + 1], rmax[:, c:c + 1], -1.0, None, ALU.mult).then_inc(max_ready, 1)
                        dve.wait_ge(exp_done, u + 1)
                        V.tensor_tensor_reduce(EX[u % 2], EX[u % 2], CN[:, t, :], 1.0, 0.0, ALU.mult, ALU.add, zsum[:, c:c + 1]
                                               ).then_inc(p_ready, 1)
                        dve.wait_ge(p_ready, u + 1)
                        then(V.tensor_scalar(zinv[:, c:c + 1], zsum[:, c:c + 1], 1e-16, None, ALU.add))
                        then(V.reciprocal(zinv[:, c:c + 1], zinv[:, c:c + 1]))
                        dve.wait_ge(p_turned, u + 1)
                        V.tensor_copy(PT[u % 2], PS[:, 6:8, :].rearrange("p b (c n) -> p (b c) n", c=4)[:, 0:R3 * NT, :]
                                      ).then_inc(pt_copied, 1)
                dve.wait_ge(att_sum, u0 + 2 * H)
                if l == 1:
                    then(V.tensor_tensor(xN[:], xN[:], biasN[:, bias, :].unsqueeze(1).to_broadcast([P, NT, FEAT]), ALU.add))
                width = min(FEAT // H, HALF)
                for h in range(H):
                    for t in range(NT):
                        c = (u0 + 2 * h + t) % 8
                        for part in range(FEAT // H // width):
                            at = h * (FEAT // H) + part * width
                            other = biasN[:, bias, at:at + width] if l == 0 else xN[:, t, at:at + width]
                            dest = hN if l == 0 else xN
                            ins = V.scalar_tensor_tensor(out=dest[:, t, at:at + width],
                                                         in0=PS[:, 2 * t + at // HALF, at % HALF:at % HALF + width],
                                                         scalar=zinv[:, c:c + 1], in1=other, op0=ALU.mult, op1=ALU.add)
                then(ins)
                u0 += 2 * H
                if l == 0:
                    flat = lambda a: a.rearrange("p a b -> p (a b)")
                    V.tensor_scalar(flat(MT[0][:]), flat(hN[:]), 0.0, None, ALU.min).then_inc(elu_min, 1)
                    then(V.tensor_scalar(hN[:], hN[:], 0.0, -1.0, ALU.max, ALU.add))
                    dve.wait_ge(elu_exp, 1)
                    V.tensor_tensor(flat(hN[:]), flat(hN[:]), flat(xT[:]), ALU.add).then_inc(att_done, 1)
                    dve.wait_ge(att_done, 1)
            layer_norm(3)
            dve.wait_ge(x_turned, 3)

            def keys34(r, buf):
                return V.scalar_tensor_tensor(out=ekey[:, buf, :], in0=keyf[:, 3, :], scalar=relid[:, r], in1=keyf[:, 1, :],
                                              op0=ALU.is_equal, op1=ALU.mult)

            key_ready = ctx.enter_context(nc.semaphore("key_ready"))
            rc_step = ctx.enter_context(nc.semaphore("rc_step"))

            def onehot34(r, rel, buf):
                dve.wait_ge(cnt_summed, r + 2)
                keys34(rel, buf).then_inc(key_ready, 1)
                dve.wait_ge(key_ready, r + 1)
                onehot(E[buf], ekey[:, buf, :]).then_inc(e_ready, 1)

            def normalise34(r, j):
                dve.wait_ge(deg_spread, r + (R3 + 1))
                V.tensor_scalar(RC[:, 0, :], PS[:, 5, 0:NODES], 1.0, None, ALU.max).then_inc(rc_step, 1)
                dve.wait_ge(rc_step, r * 2 + 1)
                V.reciprocal(RC[:, 1, :], RC[:, 0, :]).then_inc(rc_step, 1)
                dve.wait_ge(rc_step, r * 2 + 2)
                dve.wait_ge(agg_done, (r + (2 * R3 - 1)) * 3)
                V.tensor_tensor(N34[j], A34[j], RC[:, 1, :].unsqueeze(1).to_broadcast([P, NT, NODES]), ALU.mult).then_inc(nrm_ready, 1)

            onehot34(0, slice(0, 1), 1)
            with dve.Fori(0, LOOP34) as i:
                for j in range(2):
                    onehot34(i * 2 + (j + 1), bass.ds(i * 2 + (j + 1), 1), j)
                    normalise34(i * 2 + j, j)
            onehot34(R34 - 1, slice(R34 - 1, R34), 0)
            normalise34(R34 - 2, 0)
            normalise34(R34 - 1, 1)
            dve.wait_ge(w_used, FIRST34 + R34)
            for t in range(NT):
                ins = V.tensor_tensor(hN[:, t, :].rearrange("p (h f) -> p h f", h=2), PS[:, 2 * t:2 * t + 2, 0:HALF],
                                      biasN[:, 4, :].rearrange("p (h f) -> p h f", h=2), ALU.add)
            ins.then_inc(h1_copied, 1)
            gcn_out(2, 5)
            layer_norm(4)


_IN = {
    "x": ("x", None), "xT": ("x", "T"), "q": ("L0_gnn_query_embs", "rows"), "qT": ("L0_gnn_query_embs", "rowsT"),
    "src": ("src", None), "dst": ("dst", None), "t3": ("edge_type_3", None), "t34": ("edge_type_34", None),
    "W_rel1": ("L0_gnn_W_rel1", None), "W_root1": ("L0_gnn_W_root1", None), "b1": ("L0_gnn_b1", None),
    "W_rel2": ("L0_gnn_W_rel2", None), "W_root2": ("L0_gnn_W_root2", None), "b2": ("L0_gnn_b2", None),
    "WgT": ("L0_gnn_Wg", "T"), "bg": ("L0_gnn_bg", None), "WqT": ("L0_gnn_Wq", "T"), "bq": ("L0_gnn_bq", None),
    "L1_W": ("L1_gnn_W", None), "L1_b": ("L1_gnn_b", None),
    "W1": ("L2_gnn_W1", None), "qk1": (("L2_gnn_q1", "L2_gnn_k1"), "cols"), "L2_b1": ("L2_gnn_b1", None),
    "W2": ("L2_gnn_W2", None), "qk2": (("L2_gnn_q2", "L2_gnn_k2"), "cols"), "L2_b2": ("L2_gnn_b2", None),
    "L3_rel": ("L3_gnn_W_rel", None), "L3_root": ("L3_gnn_W_root", None), "b_rgcn": ("L3_gnn_b_rgcn", None),
    "L3_gcn": ("L3_gnn_W_gcn", None), "b_gcn": ("L3_gnn_b_gcn", None),
}


def kernel(**inputs):
    import numpy as np
    import concourse.bacc as bacc
    from concourse.bass_utils import run_bass_kernel_spmd

    nc = bacc.Bacc("TRN2", target_bir_lowering=False, num_devices=1)
    arrays, handles = {}, {}
    for name, (source, layout) in _IN.items():
        if layout == "cols":
            a = np.concatenate([np.asarray(inputs[n]) for n in source], axis=1)
        else:
            a = np.asarray(inputs[source])
        if layout in ("rows", "rowsT"):
            a = a.reshape(-1, a.shape[-1])
        if layout in ("T", "rowsT"):
            a = a.T
        a = np.ascontiguousarray(a)
        arrays[f"in_{name}"] = a
        handles[name] = nc.dram_tensor(f"in_{name}", a.shape, mybir.dt.from_np(a.dtype), kind="ExternalInput").ap()
    handles["out"] = nc.dram_tensor("out", (NODES, FEAT), F32, kind="ExternalOutput").ap()
    build(nc, handles)
    r = run_bass_kernel_spmd(nc, [arrays], core_ids=[0])
    return r.results[0]["out"]
```

```python
from contextlib import ExitStack

import concourse.bass as bass
from concourse import mybir

P = 128
F32 = mybir.dt.float32
F32R = mybir.dt.float32r
BF16 = mybir.dt.bfloat16
I32 = mybir.dt.int32
ALU = mybir.AluOpType
ACT = mybir.ActivationFunctionType
AX = mybir.AxisListType

NODES, FEAT, EDGES = 256, 768, 4352
NT = NODES // P
KC = FEAT // P
EC = EDGES // P
HALF = FEAT // 2
BATCH, QLEN = 8, 64
BN = NODES // BATCH
PAIRS = BN // 2
BLOCKS = PAIRS // 2
R3, R34 = 3, 34
HEADS1 = 4
SLOPE, MASKED = 0.2, -1e30
CAP = 2 * P
THIRD = FEAT // 3
PAIRS34 = R34 // 2
CREDIT = 7


def build(nc, A):
    with ExitStack() as ctx:
        def sb(name, shape, dt=F32):
            return ctx.enter_context(nc.sbuf_tensor(name, shape, dt))

        def sem(name):
            return ctx.enter_context(nc.semaphore(name))

        PS = ctx.enter_context(nc.psum_tensor("PS", [P, 8, 512], F32))
        W = [sb(f"W{i}", [P, KC, FEAT]) for i in range(2)]
        xN, hN = sb("xN", [P, NT, FEAT]), sb("hN", [P, NT, FEAT])
        xT, hT = sb("xT", [P, KC, NODES]), sb("hT", [P, KC, NODES])
        SMALL = 16 * 11
        AI = sb("AI", [P, NT, NODES])
        base = (nc.sbuf_base + 63) // 64 * 64
        ctx.enter_context(nc.sbuf_tensor("stretch", [P, 111 * 256], F32))

        def put(name, shape, dt, at):
            return nc.alloc_sbuf_tensor_at(name, shape, dt, offset=base + int(at * 1024))

        MT = [put(f"MT{i}", [P, KC, NODES], F32, 6 * i) for i in range(2)]
        CNT = put("CNT", [P, R3, NT, NODES], F32, 12)
        NRM = put("NRM", [P, R3, NT, NODES], F32, 18)
        S1 = put("S1", [P, EC, NODES], BF16, 24)
        arena = put("arena", [P, 14848], F32, 41)
        selmem = put("selmem", [P, 3072], F32, 99)
        ident, ones = sb("ident", [P, P]), sb("ones", [P, P])
        iota1 = sb("iota1", [P, NODES])
        relid = sb("relid", [P, R34])
        keys = sb("keys", [P, 4, EC], I32)
        keyf = sb("keyf", [P, 4, EC])
        ekey = sb("ekey", [P, 2, EC])
        biasT = sb("biasT", [P, 3, KC])
        biasN = sb("biasN", [P, 6, FEAT])
        qk1, qk2 = sb("qk1", [P, KC, 2 * HEADS1]), sb("qk2", [P, KC, 2])
        qkT = sb("qkT", [2 * HEADS1, R3 * NODES])
        qkN = sb("qkN", [P, NT, R3, 2 * HEADS1])
        RC = sb("RC", [P, 2, NODES])
        stats, mv = sb("stats", [P, NT, 2, 6]), sb("mv", [P, NT, 2])
        sd, rstd = sb("sd", [P, NT]), sb("rstd", [P, NT])
        eps = sb("eps", [P, 1])
        dinv = sb("dinv", [P, NT])
        rmax, nmax = sb("rmax", [P, 8]), sb("nmax", [P, 8])
        zsum, zinv = sb("zsum", [P, 8]), sb("zinv", [P, 8])

        def view(t, at, n, dt=F32):
            v = t[:, at:at + n]
            return v if dt == F32 else v.bitcast(dt)

        QH = view(arena, 0, 6144).rearrange("p (b f) -> p b f", b=BATCH)
        SIG = [view(arena, 6144 + 1536 * i, 1536) for i in range(2)]
        PRD = [view(arena, 9216 + 1536 * i, 1536) for i in range(2)]
        QD = [view(arena, 12288 + FEAT * i, FEAT) for i in range(2)]
        qiT = SIG[0].rearrange("p (k n) -> p k n", k=KC)
        tanhT = SIG[1].rearrange("p (k n) -> p k n", k=KC)
        alphaT = PRD[0].rearrange("p (k n) -> p k n", k=KC)
        qiN = hN
        qT = [MT[0], MT[1]]
        E = [view(arena, 6144 + 4352 * i, 4352, BF16).rearrange("p (c n) -> p c n", c=EC) for i in range(2)]
        XR = view(arena, 0, 4608).rearrange("p (r t f) -> p r t f", r=R3, t=NT)
        XT = view(arena, 4608, 4608).rearrange("p (r k n) -> p r k n", r=R3, k=KC)
        SC = [view(arena, 9216 + 768 * i, 768) for i in range(2)]
        EX = [view(arena, 10752 + 768 * i, 768) for i in range(2)]
        PT = [view(arena, 12288 + 768 * i, 768).rearrange("p (c n) -> p c n", c=R3 * NT) for i in range(2)]
        SEL = view(selmem, 0, 2048).rearrange("p (i m) -> p i m", i=PAIRS)
        RED = view(selmem, 2048, 512).rearrange("p (i m) -> p i m", i=PAIRS)
        CN = view(selmem, 0, 1536).rearrange("p (t c) -> p t c", t=NT)
        NM = view(selmem, 1536, 1536).rearrange("p (t c) -> p t c", t=NT)
        OH = view(arena, 6144, 1156).rearrange("p (r c) -> p r c", r=R34)
        RUN = view(arena, 7300, 1156)
        KEEP = view(arena, 8456, 1156)
        OHB = view(arena, 9612, 578, BF16).rearrange("p (r c) -> p r c", r=R34)
        PRES, INCL, SLOT1 = (hN[0:R34, 0, 256 * i:256 * i + 256] for i in range(3))
        SLOTB = hN[0:R34, 1, 0:128].bitcast(BF16)
        WS = [[put(f"W{x}{q}", [P, KC, THIRD], F32R, 41 + 12 * q + 6 * i) for q in range(3)] for i, x in enumerate(("hi", "lo"))]
        MS = [[put(f"M{x}{b}", [P, KC, NODES], F32R, 77 + 12 * b + 6 * i) for b in range(2)] for i, x in enumerate(("hi", "lo"))]
        XS = [put(f"X{x}", [P, NT, FEAT], F32R, 6 * i) for i, x in enumerate(("hi", "lo"))]
        BB = put("BB", [P, NT * NODES], F32R, 12)
        CT = [put(f"CT{j}", [P, NODES], F32R, 14 + j) for j in range(2)]
        YS = [[put(f"Y{x}{b}", [P, THIRD], F32R, 16 + 2 * b + i) for b in range(2)] for i, x in enumerate(("hi", "lo"))]
        OS = [put(f"OS{j}", [P, 2, NODES], BF16, 20 + j) for j in range(2)]
        OT = [put(f"OT{j}", [P, 2, P], BF16, 22 + 0.5 * j) for j in range(2)]
        SLB = put("SLB", [P, R34 * NODES], BF16, 24)
        PAY = sb("PAY", [P, EC, 2])
        KS = sb("KS", [P, 2 * R34, 2])
        POS, GIX = sb("POS", [P, EC], I32), sb("GIX", [P, EC], I32)
        t34f = sb("t34f", [P, 3, EC])
        offs = sb("offs", [P, R34])
        UT = sb("UT", [P, P])
        pidx1, onesb = sb("pidx1", [P, 1]), sb("onesb", [P, 1], BF16)
        zrow = sb("zrow", [P, 2 * 2 * R34])
        bad, flag = sb("bad", [P, 2]), sb("flag", [P, 1], I32)
        rcs, rcm = sb("rcs", [P, 2, 2]), sb("rcm", [P, 2])
        key_ready, rc_step = sem("key_ready"), sem("rc_step")
        slot_tab = nc.dram_tensor("slot_tab", (R34 * NODES, 1), F32).ap()
        slot_tabb = nc.dram_tensor("slot_tabb", (R34 * NODES,), BF16).ap()
        by_rel = nc.dram_tensor("by_rel", (R34 * CAP, 2), F32).ap()
        A34 = [CNT[:, i] for i in range(2)]
        N34 = [NRM[:, i] for i in range(2)]

        keys_in, x_in, q_in, small_in, out_done = (sem(n) for n in ("keys_in", "x_in", "q_in", "small_in", "out_done"))
        w_in = [sem("w_in0"), sem("w_in1")]
        qd_in = [sem("qd_in0"), sem("qd_in1")]
        w_used = sem("w_used")
        pool_step, consts = sem("pool_step"), sem("consts")
        dve_step, act_step = sem("dve_step"), sem("act_step")
        sel_ready, s1_ready, e_ready = sem("sel_ready"), sem("s1_ready"), sem("e_ready")
        cnt_summed, cnt_copied = sem("cnt_summed"), sem("cnt_copied")
        deg_spread, nrm_ready = sem("deg_spread"), sem("nrm_ready")
        ai_ready, deg_summed, dinv_sd, dinv_ready = sem("ai_ready"), sem("deg_summed"), sem("dinv_sd"), sem("dinv_ready")
        agg_done, mt_copied = sem("agg_done"), sem("mt_copied")
        qg_copied = sem("qg_copied")
        relu_done = sem("relu_done")
        hg_copied = sem("hg_copied")
        sums_done, attn_done, prod_done, red_done = sem("sums_done"), sem("attn_done"), sem("prod_done"), sem("red_done")
        qi_copied, qi_turned, qiT_copied, tanh_done = sem("qi_copied"), sem("qi_turned"), sem("qiT_copied"), sem("tanh_done")
        alpha_done, gate_done = sem("alpha_done"), sem("gate_done")
        h_turned, hN_ready = sem("h_turned"), sem("hN_ready")
        var_ready, sd_ready, ln_done, x_turned, xT_ready = (sem(n) for n in ("var_ready", "sd_ready", "ln_done", "x_turned", "xT_ready"))
        gcn_scaled, gcn_sum = sem("gcn_scaled"), sem("gcn_sum")
        cn_turned, cn_ready = sem("cn_turned"), sem("cn_ready")
        xr_copied, xr_turned, xrT_copied = sem("xr_copied"), sem("xr_turned"), sem("xrT_copied")
        qk_done, qk_copied, qkn_done, qkn_copied = sem("qk_done"), sem("qk_copied"), sem("qkn_done"), sem("qkn_copied")
        key_spread, score_done, max_ready, exp_done = sem("key_spread"), sem("score_done"), sem("max_ready"), sem("exp_done")
        p_ready, p_turned, pt_copied, att_sum, att_done = (sem(n) for n in ("p_ready", "p_turned", "pt_copied", "att_sum", "att_done"))
        elu_min, elu_exp = sem("elu_min"), sem("elu_exp")
        enc_done, h1_copied = sem("enc_done"), sem("h1_copied")
        run_ready, offs_done, d1_ready, c34_done, slots_ready, bad_ready, bad_summed, flag_ready, idx_ready = (
            sem(n) for n in ("run_ready", "offs_done", "d1_ready", "c34_done", "slots_ready", "bad_ready", "bad_summed",
                             "flag_ready", "idx_ready"))
        zero_out, tab_out, slot_in, sorted_out, sorted_in = (sem(n) for n in ("zero_out", "tab_out", "slot_in", "sorted_out", "sorted_in"))
        xs_hi, xs_ready, oh_ready, b_done, bb_ready, c_done, rc_max, rc_ready = (
            sem(n) for n in ("xs_hi", "xs_ready", "oh_ready", "b_done", "bb_ready", "c_done", "rc_max", "rc_ready"))
        msum_done, ms_hi, ms_ready, w_hi, w_lo, y_done, y_hi, y_ready, scat_done, ct_ready = (
            sem(n) for n in ("msum_done", "ms_hi", "ms_ready", "w_hi", "w_lo", "y_done", "y_hi", "y_ready", "scat_done", "ct_ready"))

        turned = lambda a: a.rearrange("(p t) n -> p t n", t=KC)
        WgT, WqT = A["WgT"], A["WqT"]
        gate_w = [WgT[0:FEAT], WqT[0:FEAT], WqT[FEAT:]]
        stream = [WgT[FEAT:], A["W_root1"]] + [A["W_rel1"][r] for r in range(R3)] + gate_w
        stream += [A["W_root2"]] + [A["W_rel2"][r] for r in range(R3)] + gate_w
        stream += [A["L1_W"]] + [A["W1"][r] for r in range(R3)] + [A["W2"][r] for r in range(R3)] + [A["L3_root"]]
        FIRST34 = len(stream)
        LOOP34 = (R34 - 2) // 2

        block = ctx.enter_context(nc.Block())

        @block.sync
        def _(sp):
            for i, n in enumerate(("src", "dst", "t3", "t34")):
                sp.dma_start(keys[:, i, :], A[n].rearrange("(p c) -> p c", c=EC)).then_inc(keys_in, 16)
            for i in range(2):
                sp.dma_start(qT[i][:], turned(A["qT"])[:, :, i * NODES:(i + 1) * NODES]).then_inc(q_in, 16)
            for m, w in enumerate(stream):
                if m >= 2:
                    sp.wait_ge(w_used, m - 1)
                sp.dma_start(W[m % 2][:], turned(w)).then_inc(w_in[m % 2], 16)
            with sp.Fori(0, LOOP34 + 1) as i:
                for j in range(2):
                    sp.wait_ge(w_used, i * 2 + (FIRST34 + j - 1))
                    sp.dma_start(W[(FIRST34 + j) % 2][:], A["L3_rel"][bass.ds(i * 2 + j, 1)].rearrange("a (p t) n -> p (a t) n", t=KC)
                                 ).then_inc(w_in[(FIRST34 + j) % 2], 16)
            m = FIRST34 + R34
            sp.wait_ge(w_used, m - 1)
            sp.dma_start(W[m % 2][:], turned(A["L3_gcn"])).then_inc(w_in[m % 2], 16)
            sp.wait_ge(ln_done, 4)
            sp.dma_start(A["out"].rearrange("(t p) f -> p t f", p=P), xN[:]).then_inc(out_done, 16)
            sp.wait_ge(out_done, 16)

        @block.gpsimd
        def _(pool):
            steps = [0]

            def then(ins):
                steps[0] += 1
                ins.then_inc(pool_step, 1)
                pool.wait_ge(pool_step, steps[0])

            pool.dma_start(xN[:], A["x"].rearrange("(t p) f -> p t f", p=P)).then_inc(x_in, 16)
            pool.dma_start(xT[:], turned(A["xT"])).then_inc(x_in, 16)
            for i, n in enumerate(("b1", "b2", "bq")):
                pool.dma_start(biasT[:, i, :], A[n].rearrange("(p t) -> p t", t=KC)).then_inc(small_in, 16)
            for i, n in enumerate(("bg", "L1_b", "L2_b1", "L2_b2", "b_rgcn", "b_gcn")):
                pool.dma_start(biasN[:, i, :], A[n].partition_broadcast(P)).then_inc(small_in, 16)
            for t, n in ((qk1, "qk1"), (qk2, "qk2")):
                pool.dma_start(t[:], turned(A[n])).then_inc(small_in, 16)
            then(nc.gpsimd.iota(iota1[:], pattern=[[1, NODES]], base=1, channel_multiplier=0,
                                allow_small_or_imprecise_dtypes=True))
            then(nc.gpsimd.iota(relid[:], pattern=[[1, R34]], base=0, channel_multiplier=0,
                                allow_small_or_imprecise_dtypes=True))
            then(nc.gpsimd.iota(pidx1[:], pattern=[[0, 1]], base=1, channel_multiplier=1,
                                allow_small_or_imprecise_dtypes=True))
            then(nc.gpsimd.memset(onesb[:], 1.0))
            then(nc.gpsimd.memset(zrow[:], 0.0))
            pool.dma_start(by_rel.rearrange("(p a) b -> p (a b)", p=P), zrow[:]).then_inc(zero_out, 16)
            then(nc.gpsimd.memset(ones[:], 1.0))
            then(nc.gpsimd.affine_select(out=UT[:], in_=ones[:], compare_op=ALU.is_gt, fill=0.0, base=0,
                                         pattern=[[1, P]], channel_multiplier=-1))
            then(nc.gpsimd.memset(RED, 0.0))
            for j in range(2):
                v = RED[64 * j:64 * j + 64]
                then(nc.gpsimd.affine_select(out=v, in_=v, compare_op=ALU.not_equal, fill=1.0, base=j,
                                             pattern=[[2, PAIRS], [-1, BN]], channel_multiplier=0))
            then(nc.gpsimd.memset(ident[:], 0.0))
            nc.gpsimd.affine_select(out=ident[:], in_=ident[:], compare_op=ALU.not_equal, fill=1.0, base=0,
                                    pattern=[[-1, P]], channel_multiplier=1).then_inc(consts, 1)
            pool.wait_ge(slots_ready, 1)
            pool.dma_start(slot_tab.rearrange("(r n) a -> r (n a)", r=R34), SLOT1).then_inc(tab_out, 16)
            pool.dma_start(slot_tabb.rearrange("(r n) -> r n", r=R34), SLOTB).then_inc(tab_out, 16)
            for g in range(2):
                with pool.Fori(0, BATCH // 2) as i:
                    for s in range(2):
                        if g == 0:
                            pool.wait_ge(c34_done, 1)
                            pool.wait_ge(prod_done, i * (2 * BLOCKS) + 1)
                        else:
                            pool.wait_ge(prod_done, i * (2 * BLOCKS) + (g * BATCH + s - 1) * BLOCKS + 1)
                        for j in range(2):
                            pool.dma_start(QD[s][64 * j:64 * j + 64, :],
                                           A["q"][bass.ds(i * (2 * QLEN) + s * QLEN, QLEN), :]).then_inc(qd_in[s], 16)

            pool.wait_ge(idx_ready, 1)
            pool.wait_ge(tab_out, 32)
            pool.wait_ge(zero_out, 16)
            for c in range(EC):
                pool.indirect_dma_start(PAY[:, c, 1:2], None, slot_tab, bass.IndirectOffsetOnAxis(GIX[:, c:c + 1], 0)
                                        ).then_inc(slot_in, 16)
            pool.wait_ge(slot_in, 16 * EC)
            for c in range(EC):
                pool.indirect_dma_start(by_rel, bass.IndirectOffsetOnAxis(POS[:, c:c + 1], 0), PAY[:, c, :], None
                                        ).then_inc(sorted_out, 16)
            pool.wait_ge(sorted_out, 16 * EC)
            pool.dma_start(KS[:].rearrange("p a b -> p (a b)"), by_rel.rearrange("(p a) b -> p (a b)", p=P)).then_inc(sorted_in, 16)
            pool.dma_start(SLB[:], slot_tabb.partition_broadcast(P)).then_inc(sorted_in, 16)

        @block.tensor
        def _(pe):
            def weights(m):
                pe.wait_ge(w_in[m % 2], 16 * (m // 2 + 1))

            def natural(bank, T, Wm, first=True, last=True):
                for t in range(NT):
                    for h in range(2):
                        for k in range(KC):
                            mm = pe.matmul(PS[:, bank + 2 * t + h, 0:HALF], T[:, k, t * P:(t + 1) * P],
                                           Wm[:, k, h * HALF:(h + 1) * HALF],
                                           start=first and k == 0, stop=last and k == KC - 1)
                return mm

            def turned_product(bank, T, Wm, first=True, last=True):
                for m in range(KC):
                    for k in range(KC):
                        mm = pe.matmul(PS[:, bank + m // 2, (m % 2) * NODES:(m % 2 + 1) * NODES], Wm[:, k, m::KC],
                                       T[:, k, :], start=first and k == 0 and m % 2 == 0,
                                       stop=last and k == KC - 1 and m % 2 == 1, skip_group_check=True)
                return mm

            def counts(n, e):
                pe.wait_ge(e_ready, n + 1)
                pe.wait_ge(cnt_copied, n)
                for s in range(NT):
                    for c in range(EC):
                        mm = pe.matmul(PS[:, 4, s * NODES:(s + 1) * NODES], S1[:, c, s * P:(s + 1) * P], E[e][:, c, :],
                                       start=c == 0, stop=c == EC - 1)
                mm.then_inc(cnt_summed, 1)

            def spread_counts(n, cnt):
                pe.wait_ge(cnt_copied, n + 1)
                pe.wait_ge(nrm_ready, n)
                for s in range(NT):
                    mm = pe.matmul(PS[:, 5, 0:NODES], ones[:], cnt[:, s, :], start=s == 0, stop=s == NT - 1)
                mm.then_inc(deg_spread, 1)

            def natural3(T, Wm, first=False, last=False):
                for t in range(NT):
                    for q in range(3):
                        at = 3 * t + q
                        for k in range(KC):
                            mm = pe.matmul(PS[:, at // 2, (at % 2) * THIRD:(at % 2 + 1) * THIRD], T[:, k, t * P:(t + 1) * P],
                                           Wm[:, k, q * THIRD:(q + 1) * THIRD], start=first and k == 0 and at % 2 == 0,
                                           stop=last and k == KC - 1 and at % 2 == 1, skip_group_check=True)
                return mm

            def aggregate(n, x, nrm):
                for j in range(3):
                    if not isinstance(n, int) or n * 3 + j > 1:
                        pe.wait_ge(mt_copied, n * 3 + j - 1)
                    for kk in range(2):
                        k = 2 * j + kk
                        for s in range(NT):
                            mm = pe.matmul(PS[:, 6 + j % 2, kk * NODES:(kk + 1) * NODES], x[:, s, k::KC], nrm[:, s, :],
                                           start=s == 0, stop=s == NT - 1)
                    mm.then_inc(agg_done, 1)

            def to_natural(bank, T):
                for t in range(NT):
                    for k in range(KC):
                        mm = pe.transpose(PS[:, bank + 2 * t + k // 4, (k % 4) * P:(k % 4 + 1) * P],
                                          T[:, k, t * P:(t + 1) * P], ident[:])
                return mm

            def to_turned(bank, N):
                for k in range(KC):
                    for t in range(NT):
                        mm = pe.transpose(PS[:, bank + k // 2, (k % 2) * NODES + t * P:(k % 2) * NODES + (t + 1) * P],
                                          N[:, t, k::KC], ident[:])
                return mm

            pe.sem_inc(red_done, 1)
            weights(0)
            pe.wait_ge(q_in, 32)
            for i in range(2):
                mm = natural(4 * i, qT[i], W[0])
            mm.then_inc(w_used, 1)

            pe.wait_ge(consts, 1)
            pe.wait_ge(s1_ready, 1)
            pe.wait_ge(qg_copied, 2)
            for r in range(R3):
                pe.wait_ge(e_ready, r + 1)
                if r:
                    pe.wait_ge(cnt_copied, r)
                for s in range(NT):
                    for c in range(EC):
                        mm = pe.matmul(PS[:, 4, s * NODES:(s + 1) * NODES], S1[:, c, s * P:(s + 1) * P], E[r % 2][:, c, :],
                                       start=c == 0, stop=c == EC - 1)
                mm.then_inc(cnt_summed, 1)
                pe.wait_ge(cnt_copied, r + 1)
                if r:
                    pe.wait_ge(nrm_ready, r)
                for s in range(NT):
                    mm = pe.matmul(PS[:, 5, 0:NODES], ones[:], CNT[:, r, s, :], start=s == 0, stop=s == NT - 1)
                mm.then_inc(deg_spread, 1)
            pe.wait_ge(ai_ready, 1)
            for t in range(NT):
                for s in range(NT):
                    mm = pe.matmul(PS[:, 4, t:t + 1], AI[:, s, t * P:(t + 1) * P], ones[:, 0:1], start=s == 0, stop=s == NT - 1)
            mm.then_inc(deg_summed, 1)

            for g in range(2):
                m0 = 1 + 7 * g
                src, srcT = (xN, xT) if g == 0 else (hN, hT)
                if g == 0:
                    pe.wait_ge(x_in, 32)
                else:
                    pe.wait_ge(gate_done, 1)
                weights(m0)
                if g:
                    pe.wait_ge(hN_ready, 1)
                turned_product(0, srcT, W[m0 % 2], last=False).then_inc(w_used, 1)
                for r in range(R3):
                    if g == 0:
                        pe.wait_ge(nrm_ready, r + 1)
                    n = g * R3 + r
                    aggregate(n, src, NRM[:, r])
                    pe.wait_ge(mt_copied, 3 * (n + 1))
                    weights(m0 + 1 + r)
                    mm = turned_product(0, MT[n % 2], W[(m0 + 1 + r) % 2], first=False, last=r == R3 - 1)
                    mm.then_inc(w_used, 1)
                    if n == 0:
                        pe.wait_ge(run_ready, 1)
                        pe.wait_ge(dinv_sd, 1)
                        pe.matmul(PS[:, 4, 0:R34], UT[:], RUN.rearrange("p (r c) -> p r c", r=R34)[:, :, EC - 1],
                                  start=True, stop=True).then_inc(offs_done, 1)
                        pe.wait_ge(d1_ready, 1)
                        for c in range(EC):
                            mm = pe.matmul(PS[0:R34, 5, NODES:2 * NODES], OHB[:, :, c], E[1][:, c, :], start=c == 0, stop=c == EC - 1)
                        mm.then_inc(c34_done, 1)
                    if n == 1:
                        pe.wait_ge(bad_ready, 1)
                        pe.matmul(PS[:, 4, 0:1], ones[0:R34, :], bad[0:R34, 0:1], start=True, stop=True).then_inc(bad_summed, 1)
                pe.wait_ge(relu_done, g + 1)
                pe.wait_ge(flag_ready, 1)
                weights(m0 + 4)
                natural(4, hT, W[(m0 + 4) % 2]).then_inc(w_used, 1)
                pe.wait_ge(hg_copied, 8 * (g + 1))
                pe.wait_ge(sel_ready, 2)
                with pe.Fori(0, NT) as t:
                    nb0 = t * (4 * BLOCKS) + g * BATCH * BLOCKS

                    def reduce(q):
                        pe.wait_ge(prod_done, nb0 + (q + 2))
                        for u in range(2):
                            i = 2 * (q % BLOCKS) + u
                            b = q // BLOCKS
                            for h in range(2):
                                mm = pe.matmul(PS[32 * b:32 * b + 32, 6 + h, 0:HALF], RED[:, i, :],
                                               PRD[q % 2][:, u * FEAT + h * HALF:u * FEAT + (h + 1) * HALF],
                                               start=i == 0, stop=i == PAIRS - 1)
                        mm.then_inc(red_done, 1)

                    for q in range(4 * BLOCKS):
                        i0, b = 2 * (q % BLOCKS), q // BLOCKS
                        if q >= 2 or g:
                            pe.wait_ge(attn_done, nb0 + (q - 1))
                        base = 3 * (q % 2)
                        for u, lo, hi, bank, at in ((0, 0, 512, 0, 0), (0, 512, 768, 1, 0), (1, 0, 256, 1, 256), (1, 256, 768, 2, 0)):
                            mm = pe.matmul(PS[:, base + bank, at:at + hi - lo], SEL[0:96, i0 + u, :],
                                           QH[0:96, bass.ds(t * 4 + b, 1), lo:hi].rearrange("p a f -> p (a f)"), start=True, stop=True)
                        mm.then_inc(sums_done, 1)
                        if q >= 2:
                            if q == 2:
                                pe.wait_ge(qi_copied, t + (2 * g + 1))
                            reduce(q - 2)
                    reduce(4 * BLOCKS - 2)
                    reduce(4 * BLOCKS - 1)
                pe.wait_ge(qi_copied, 2 * g + 3)
                to_turned(0, qiN).then_inc(qi_turned, 1)
                weights(m0 + 5)
                turned_product(3, hT, W[(m0 + 5) % 2], last=False).then_inc(w_used, 1)
                pe.wait_ge(qiT_copied, g + 1)
                weights(m0 + 6)
                turned_product(3, qiT, W[(m0 + 6) % 2], first=False).then_inc(w_used, 1)
                pe.wait_ge(gate_done, g + 1)
                to_natural(0, hT).then_inc(h_turned, 1)

            def turn_x(n):
                pe.wait_ge(ln_done, n)
                to_turned(0, xN).then_inc(x_turned, 1)
                pe.wait_ge(xT_ready, n)

            turn_x(1)
            m = 15
            weights(m)
            natural(4, xT, W[m % 2]).then_inc(w_used, 1)

            def gcn_aggregate(n):
                pe.wait_ge(gcn_scaled, n)
                for t in range(NT):
                    for h in range(2):
                        for s in range(NT):
                            mm = pe.matmul(PS[:, 2 * t + h, 0:HALF], AI[:, s, t * P:(t + 1) * P],
                                           hN[:, s, h * HALF:(h + 1) * HALF], start=s == 0, stop=s == NT - 1)
                mm.then_inc(gcn_sum, 1)

            gcn_aggregate(1)
            for t in range(NT):
                for c in range(R3 * NT):
                    mm = pe.transpose(PS[:, 4 + 2 * t + c // 4, (c % 4) * P:(c % 4 + 1) * P],
                                      CNT[:, c // NT, c % NT, t * P:(t + 1) * P], ident[:])
            mm.then_inc(cn_turned, 1)

            turn_x(2)
            u0 = 0
            for l, (H, qk, T) in enumerate(((HEADS1, qk1, xT), (1, qk2, hT))):
                m0 = 16 + R3 * l
                for r in range(R3):
                    m = m0 + r
                    weights(m)
                    if r == 0:
                        pe.wait_ge(cn_ready, 1)
                    n = l * R3 + r
                    if n >= 2:
                        pe.wait_ge(xr_copied, n - 1)
                    natural(4 * (r % 2), T, W[m % 2]).then_inc(w_used, 1)
                pe.wait_ge(xr_copied, R3 * (l + 1))
                for j in range(9):
                    if l * 9 + j >= 2:
                        pe.wait_ge(xrT_copied, l * 9 + j - 1)
                    for kk in range(2):
                        r, k = divmod(2 * j + kk, KC)
                        for t in range(NT):
                            mm = pe.transpose(PS[:, j % 2, kk * NODES + t * P:kk * NODES + (t + 1) * P], XR[:, r, t, k::KC], ident[:])
                    mm.then_inc(xr_turned, 1)
                pe.wait_ge(small_in, SMALL)
                pe.wait_ge(xrT_copied, 9 * (l + 1))
                for r in range(R3):
                    for k in range(KC):
                        mm = pe.matmul(PS[0:2 * H, 2 + r // 2, (r % 2) * NODES:(r % 2 + 1) * NODES], qk[:, k, :], XT[:, r, k, :],
                                       start=k == 0, stop=k == KC - 1)
                mm.then_inc(qk_done, 1)
                pe.wait_ge(qk_copied, l + 1)
                for t in range(NT):
                    for r in range(R3):
                        mm = pe.transpose(PS[:, 0, (t * R3 + r) * 2 * H:(t * R3 + r + 1) * 2 * H],
                                          qkT[0:2 * H, r * NODES + t * P:r * NODES + (t + 1) * P], ident[0:2 * H, 0:2 * H])
                mm.then_inc(qkn_done, 1)
                for h in range(H):
                    if h:
                        pe.wait_ge(score_done, u0 + 2 * h)
                    sel = ident[0:2 * H, H + h:H + h + 1].to_broadcast([2 * H, P])
                    pe.matmul(PS[:, 4, :], sel, qkT[0:2 * H, 0:512], start=True, stop=True)
                    pe.matmul(PS[:, 5, 0:256], sel, qkT[0:2 * H, 512:768], start=True, stop=True).then_inc(key_spread, 1)
                    for t in range(NT):
                        u = u0 + 2 * h + t
                        pe.wait_ge(p_ready, u + 1)
                        if u > u0:
                            pe.wait_ge(pt_copied, u)
                        for c in range(R3 * NT):
                            mm = pe.transpose(PS[:, 6 + c // 4, (c % 4) * P:(c % 4 + 1) * P], EX[u % 2][:, c * P:(c + 1) * P], ident[:])
                        mm.then_inc(p_turned, 1)
                        pe.wait_ge(pt_copied, u + 1)
                        if u == u0:
                            pe.wait_ge(qkn_copied, l + 1)
                        width = min(FEAT // H, HALF)
                        for part in range(FEAT // H // width):
                            at = h * (FEAT // H) + part * width
                            for c in range(R3 * NT):
                                mm = pe.matmul(PS[:, 2 * t + at // HALF, at % HALF:at % HALF + width], PT[u % 2][:, c, :],
                                               XR[:, c // NT, c % NT, at:at + width], start=c == 0, stop=c == R3 * NT - 1)
                        mm.then_inc(att_sum, 1)
                u0 += 2 * H
                if l == 0:
                    pe.wait_ge(att_done, 1)
                    to_turned(0, hN).then_inc(h_turned, 1)
                    pe.wait_ge(hN_ready, 2)

            turn_x(3)
            m = FIRST34 - 1
            weights(m)
            pe.wait_ge(ln_done, 3)
            natural3(xT, W[m % 2], first=True).then_inc(w_used, 1)

            def count_pair(p):
                pe.wait_ge(oh_ready, p + 1)
                pe.wait_ge(rc_ready, p + CREDIT)
                for j in range(2):
                    for t in range(NT):
                        for e in range(2):
                            mm = pe.matmul(PS[:, 7, t * NODES + j * P:t * NODES + (j + 1) * P], OS[j][:, e, t * P:(t + 1) * P],
                                           OT[j][:, e, :], start=e == 0, stop=e == 1)
                mm.then_inc(b_done, 1)

            def count_slots(p):
                pe.wait_ge(bb_ready, p + 1)
                for j in range(2):
                    for e in range(2):
                        mm = pe.matmul(PS[:, 7, j:j + 1], OT[j][:, e, :], onesb[:], start=e == 0, stop=e == 1)
                mm.then_inc(c_done, 1)

            def sum_sources(p, i):
                if i == 0:
                    pe.wait_ge(bb_ready, p + 1)
                pe.wait_ge(ms_ready, p * 3 + (CREDIT + (1 if i == 2 else 0)))
                for kk in range(2):
                    k = 2 * i + kk
                    n = 0
                    for t in range(NT):
                        for part in range(2):
                            mm = pe.matmul(PS[:, 5 + i % 2, kk * NODES:(kk + 1) * NODES], XS[part][:, t, k::KC],
                                           BB[:, t * NODES:(t + 1) * NODES], start=n == 0, stop=n == 3)
                            n += 1
                mm.then_inc(msum_done, 1)

            def product(p, s, mb):
                j, q = divmod(s, 3)
                if s == 0:
                    pe.wait_ge(ms_ready, p * 3 + (CREDIT + 3))
                if q < 2:
                    pe.wait_ge(w_lo, p * 4 + (2 * j + q + 1))
                else:
                    pe.wait_ge(w_used, p * 2 + (FIRST34 + j + 1))
                pe.wait_ge(y_ready, p * 6 + (s - 1 + CREDIT))
                n = 0
                for k in range(KC):
                    for a, b in ((0, 0), (1, 0), (0, 1)):
                        mm = pe.matmul(PS[:, 3 + s % 2, 0:THIRD], MS[a][mb][:, k, j * P:(j + 1) * P], WS[b][q][:, k, :],
                                       start=n == 0, stop=n == 17)
                        n += 1
                mm.then_inc(y_done, 1)

            def scatter(p, s, last=False):
                j, q = divmod(s, 3)
                pe.wait_ge(y_ready, p * 6 + (s + 1 + CREDIT))
                if q == 0:
                    pe.wait_ge(ct_ready, p * 2 + (j + 1))
                for t in range(NT):
                    at = 3 * t + q
                    for part in range(2):
                        mm = pe.matmul(PS[:, at // 2, (at % 2) * THIRD:(at % 2 + 1) * THIRD], CT[j][:, t * P:(t + 1) * P],
                                       YS[part][s % 2][:], start=False, stop=last and part == 1, skip_group_check=True)
                return mm.then_inc(enc_done if last else scat_done, 1)

            def pair(p, mb, nxt=True):
                for s in range(6):
                    product(p, s, mb)
                    if s:
                        scatter(p, s - 1)
                    if nxt and s == 0:
                        count_pair(p + 1)
                    if nxt and s == 1:
                        count_slots(p + 1)
                    if nxt and s >= 3:
                        sum_sources(p + 1, s - 3)
                scatter(p, 5, last=not nxt)

            overflow = pe.value_load(flag[0:1, 0:1])
            with pe.If(overflow < 1):
                for x in (c_done, y_done, scat_done):
                    pe.sem_inc(x, CREDIT)
                pe.wait_ge(xs_ready, 1)
                count_pair(0)
                count_slots(0)
                for i in range(3):
                    sum_sources(0, i)
                with pe.Fori(0, (PAIRS34 - 1) // 2) as i:
                    pair(i * 2, 0)
                    pair(i * 2 + 1, 1)
                pair(PAIRS34 - 1, 0, nxt=False)
            with pe.Else():
                pe.wait_ge(s1_ready, 2)
                counts(R3, 1)
                spread_counts(R3, A34[0])

                def relation(r, j, nxt=True, last=False):
                    if nxt:
                        counts(r + (R3 + 1), j % 2)
                    pe.wait_ge(nrm_ready, r + (R3 + 1))
                    aggregate(r + 2 * R3, xN, N34[j])
                    if nxt:
                        spread_counts(r + (R3 + 1), A34[1 - j])
                    pe.wait_ge(mt_copied, (r + (2 * R3 + 1)) * 3)
                    slot = (FIRST34 + j) % 2
                    pe.wait_ge(w_in[slot], (r - j) * 8 + 16 * ((FIRST34 + j) // 2 + 1))
                    mm = natural3(MT[j], W[slot], last=last)
                    mm.then_inc(w_used, 1)
                    return mm

                with pe.Fori(0, LOOP34) as i:
                    for j in range(2):
                        relation(i * 2 + j, j)
                relation(R34 - 2, 0)
                relation(R34 - 1, 1, nxt=False, last=True)
                pe.wait_ge(w_used, FIRST34 + R34)
                pe.sem_inc(enc_done, 1)
            pe.wait_ge(h1_copied, 1)
            to_turned(4, hN).then_inc(h_turned, 1)
            pe.wait_ge(hN_ready, 3)
            m = FIRST34 + R34
            weights(m)
            natural(4, hT, W[m % 2]).then_inc(w_used, 1)
            gcn_aggregate(2)

        @block.scalar
        def _(act):
            def turned_out(bank):
                return PS[:, bank:bank + 3, :].rearrange("p b (k n) -> p (b k) n", k=2)

            act.wait_ge(small_in, SMALL)

            def counts_copy(n, cnt):
                act.wait_ge(cnt_summed, n + 1)
                nc.scalar.copy(cnt, PS[:, 4, :].rearrange("p (s n) -> p s n", s=NT)).then_inc(cnt_copied, 1)

            def mt_copy(n, buf):
                for j in range(3):
                    act.wait_ge(agg_done, n * 3 + (j + 1))
                    nc.scalar.copy(MT[buf][:, 2 * j:2 * j + 2, :], PS[:, 6 + j % 2, :].rearrange("p (k n) -> p k n", k=2)
                                   ).then_inc(mt_copied, 1)

            for r in range(R3):
                counts_copy(r, CNT[:, r])
            act.wait_ge(deg_summed, 1)
            nc.scalar.activation(dinv[:], PS[:, 4, 0:NT], ACT.Sqrt).then_inc(dinv_sd, 1)

            for g in range(2):
                for r in range(R3):
                    n = g * R3 + r
                    if r >= 2:
                        act.wait_ge(w_used, 1 + 7 * g + 1 + (r - 1))
                    mt_copy(n, n % 2)
                act.wait_ge(w_used, 7 * g + 5)
                for m in range(KC):
                    ins = nc.scalar.activation(hT[:, m, :], PS[:, m // 2, (m % 2) * NODES:(m % 2 + 1) * NODES], ACT.Relu,
                                               bias=biasT[:, g, m:m + 1])
                ins.then_inc(relu_done, 1)
                act.wait_ge(w_used, 7 * g + 6)
                for b in range(0, BATCH, 2):
                    q, t = b % 4, b // 4
                    nc.scalar.copy(QH[64:96, b, :].rearrange("p (h f) -> p h f", h=2),
                                   PS[32 * q:32 * q + 32, 4 + 2 * t:6 + 2 * t, 0:HALF]).then_inc(hg_copied, 1)
                with act.Fori(0, BATCH * BLOCKS // 2) as i:
                    for q in range(2):
                        nb = i * 2 + (q + g * BATCH * BLOCKS)
                        act.wait_ge(sums_done, nb + 1)
                        act.wait_ge(prod_done, nb if q or g else i * 2 + 1)
                        nc.scalar.activation(SIG[q], PS[:, 3 * q:3 * q + 3, :].rearrange("p b n -> p (b n)"), ACT.Sigmoid
                                             ).then_inc(attn_done, 1)
                act.wait_ge(qiT_copied, g + 1)
                nc.scalar.activation(tanhT, turned_out(0), ACT.Tanh).then_inc(tanh_done, 1)
                act.wait_ge(w_used, 7 * g + 8)
                for m in range(KC):
                    ins = nc.scalar.activation(alphaT[:, m, :], PS[:, 3 + m // 2, (m % 2) * NODES:(m % 2 + 1) * NODES],
                                               ACT.Sigmoid, bias=biasT[:, 2, m:m + 1])
                ins.then_inc(alpha_done, 1)

            def norm_x(n):
                act.wait_ge(var_ready, n)
                nc.scalar.activation(sd[:], mv[:, :, 1], ACT.Sqrt, bias=eps[:, 0:1]).then_inc(sd_ready, 1)

            def turn_x(n):
                act.wait_ge(x_turned, n)
                nc.scalar.copy(xT[:], turned_out(0)).then_inc(xT_ready, 1)

            def scale_rows(n):
                act.wait_ge(w_used, 16 if n == 1 else FIRST34 + R34 + 1)
                if n == 1:
                    act.wait_ge(dinv_ready, 1)
                for t in range(NT):
                    ins = nc.scalar.activation(hN[:, t, :].rearrange("p (h f) -> p h f", h=2), PS[:, 4 + 2 * t:6 + 2 * t, 0:HALF],
                                               ACT.Copy, scale=dinv[:, t:t + 1])
                ins.then_inc(gcn_scaled, 1)

            norm_x(1)
            turn_x(1)
            scale_rows(1)
            norm_x(2)
            turn_x(2)
            u0 = 0
            for l, H in enumerate((HEADS1, 1)):
                for r in range(R3):
                    act.wait_ge(w_used, 17 + l * R3 + r)
                    for t in range(NT):
                        ins = nc.scalar.copy(XR[:, r, t, :].rearrange("p (h f) -> p h f", h=2),
                                             PS[:, 4 * (r % 2) + 2 * t:4 * (r % 2) + 2 * t + 2, 0:HALF])
                    ins.then_inc(xr_copied, 1)
                act.wait_ge(qkn_copied, l + 1)
                for h in range(H):
                    act.wait_ge(key_spread, u0 // 2 + h + 1)
                    for t in range(NT):
                        u = u0 + 2 * h + t
                        if u >= 2:
                            act.wait_ge(exp_done, u - 1)
                        for r in range(R3):
                            ins = nc.scalar.activation(SC[u % 2][:, r * NODES:(r + 1) * NODES],
                                                       PS[:, 4 + r // 2, (r % 2) * NODES:(r % 2 + 1) * NODES], ACT.Identity,
                                                       bias=qkN[:, t, r, h:h + 1])
                        ins.then_inc(score_done, 1)
                        act.wait_ge(max_ready, u + 1)
                        if u >= 2:
                            act.wait_ge(p_turned, u - 1)
                        nc.scalar.activation(EX[u % 2], SC[u % 2], ACT.Exp, bias=nmax[:, u % 8:u % 8 + 1]).then_inc(exp_done, 1)
                u0 += 2 * H
                if l == 0:
                    act.wait_ge(elu_min, 1)
                    nc.scalar.activation(xT[:], MT[0][:], ACT.Exp).then_inc(elu_exp, 1)
                    act.wait_ge(h_turned, 3)
                    nc.scalar.copy(hT[:], turned_out(0)).then_inc(hN_ready, 1)
            norm_x(3)
            turn_x(3)

            def weight_hi(p, s):
                if s >= 6:
                    p, s = p + 1, s - 6
                j, q = divmod(s, 3)
                slot = (FIRST34 + j) % 2
                if q == 0:
                    act.wait_ge(w_in[slot], p * 16 + 16 * ((FIRST34 + j) // 2 + 1))
                act.wait_ge(y_done, p * 6 + (s - 2 + CREDIT))
                nc.scalar.copy(WS[0][q][:], W[slot][:, :, q * THIRD:(q + 1) * THIRD]).then_inc(w_hi, 1)

            def counts_hi(p):
                act.wait_ge(b_done, p + 1)
                if not isinstance(p, int):
                    act.wait_ge(msum_done, p * 3)
                nc.scalar.copy(BB[:], PS[:, 7, :]).then_inc(bb_ready, 1)

            def sums_hi(p, i, mb):
                act.wait_ge(msum_done, p * 3 + (i + 1))
                if i == 0:
                    act.wait_ge(y_done, p * 6 + (CREDIT - 6))
                nc.scalar.copy(MS[0][mb][:, 2 * i:2 * i + 2, :], PS[:, 5 + i % 2, :].rearrange("p (k n) -> p k n", k=2)
                               ).then_inc(ms_hi, 1)

            def rows_hi(p, s, mb):
                if s == 0:
                    act.wait_ge(rc_ready, p + (1 + CREDIT))
                act.wait_ge(y_done, p * 6 + (s + 1 + CREDIT))
                act.wait_ge(scat_done, p * 6 + (s - 1 + CREDIT))
                nc.scalar.activation(YS[0][s % 2][:], PS[:, 3 + s % 2, 0:THIRD], ACT.Copy, scale=rcs[:, mb, s // 3:s // 3 + 1]
                                     ).then_inc(y_hi, 1)

            def pair(p, mb, nxt=True):
                for s in range(6):
                    if nxt and s == 1:
                        counts_hi(p + 1)
                    if s:
                        rows_hi(p, s - 1, mb)
                    if nxt or s + 2 < 6:
                        weight_hi(p, s + 2)
                    if nxt and s >= 4:
                        sums_hi(p + 1, s - 4, 1 - mb)
                if nxt:
                    sums_hi(p + 1, 2, 1 - mb)
                rows_hi(p, 5, mb)

            act.wait_ge(flag_ready, 1)
            overflow = act.value_load(flag[0:1, 0:1])
            with act.If(overflow < 1):
                for part in range(1):
                    nc.scalar.copy(XS[0][:], xN[:]).then_inc(xs_hi, 1)
                weight_hi(0, 0)
                weight_hi(0, 1)
                counts_hi(0)
                for i in range(3):
                    sums_hi(0, i, 0)
                with act.Fori(0, (PAIRS34 - 1) // 2) as i:
                    pair(i * 2, 0)
                    pair(i * 2 + 1, 1)
                pair(PAIRS34 - 1, 0, nxt=False)
            with act.Else():
                counts_copy(R3, A34[0])

                def relation(r, j, nxt=True):
                    if nxt:
                        act.wait_ge(nrm_ready, r + R3)
                        counts_copy(r + (R3 + 1), A34[1 - j])
                    act.wait_ge(w_used, r + (FIRST34 - 1))
                    mt_copy(r + 2 * R3, j)

                with act.Fori(0, LOOP34) as i:
                    for j in range(2):
                        relation(i * 2 + j, j)
                relation(R34 - 2, 0)
                relation(R34 - 1, 1, nxt=False)
            act.wait_ge(h_turned, 4)
            nc.scalar.copy(hT[:], turned_out(4)).then_inc(hN_ready, 1)
            scale_rows(2)
            norm_x(4)

        @block.vector
        def _(dve):
            steps = [0]

            def then(ins):
                steps[0] += 1
                ins.then_inc(dve_step, 1)
                dve.wait_ge(dve_step, steps[0])

            V = nc.vector
            dve.sem_inc(prod_done, 1)
            dve.sem_inc(qi_copied, 1)

            def onehot(out, key):
                return V.tensor_tensor(out, iota1[:].unsqueeze(1).to_broadcast([P, EC, NODES]),
                                       key.unsqueeze(2).to_broadcast([P, EC, NODES]), ALU.is_equal)

            then(V.memset(eps[:], 1e-5))
            dve.wait_ge(keys_in, 64)
            then(V.tensor_copy(keyf[:], keys[:]))
            then(V.tensor_scalar(keyf[:, 0:2, :], keyf[:, 0:2, :], 1.0, None, ALU.add))
            dve.wait_ge(consts, 1)
            onehot(S1[:], keyf[:, 0, :]).then_inc(s1_ready, 1)
            sv = SEL.rearrange("p i (j l) -> p (i j) l", j=2)
            V.tensor_copy(sv[0:64], ident[0:64, 0:64].unsqueeze(1).to_broadcast([64, 2 * PAIRS, QLEN])).then_inc(sel_ready, 1)
            V.tensor_copy(sv[64:96], ident[64:96, 64:96].unsqueeze(2).to_broadcast([32, 2 * PAIRS, QLEN])).then_inc(sel_ready, 1)
            dve.wait_ge(w_used, 1)
            dve.wait_ge(small_in, SMALL)
            for i in range(2):
                for t in range(NT):
                    for j in range(2):
                        ins = V.tensor_tensor(QH[0:64, 4 * i + 2 * t + j, :].rearrange("p (h f) -> p h f", h=2),
                                              PS[64 * j:64 * j + 64, 4 * i + 2 * t:4 * i + 2 * t + 2, 0:HALF],
                                              biasN[0:64, 0, :].rearrange("p (h f) -> p h f", h=2), ALU.add)
                ins.then_inc(qg_copied, 1)

            for r in range(R3 + 1):
                if r < R3:
                    then(V.scalar_tensor_tensor(out=ekey[:, r % 2, :], in0=keyf[:, 2, :], scalar=float(r), in1=keyf[:, 1, :],
                                                op0=ALU.is_equal, op1=ALU.mult))
                    if r == 2:
                        dve.wait_ge(cnt_summed, 1)
                    onehot(E[r % 2], ekey[:, r % 2, :]).then_inc(e_ready, 1)
                if r >= 1:
                    n = r - 1
                    dve.wait_ge(deg_spread, n + 1)
                    then(V.tensor_scalar(RC[:, 0, :], PS[:, 5, 0:NODES], 1.0, None, ALU.max))
                    then(V.reciprocal(RC[:, 1, :], RC[:, 0, :]))
                    V.tensor_tensor(NRM[:, n], CNT[:, n], RC[:, 1, :].unsqueeze(1).to_broadcast([P, NT, NODES]), ALU.mult
                                    ).then_inc(nrm_ready, 1)
            then(V.tensor_tensor(AI[:], CNT[:, 0], CNT[:, 1], ALU.add))
            then(V.tensor_tensor(AI[:], AI[:], CNT[:, 2], ALU.add))
            for s in range(NT):
                ins = V.tensor_tensor(AI[:, s, s * P:(s + 1) * P], AI[:, s, s * P:(s + 1) * P], ident[:], ALU.add)
            ins.then_inc(ai_ready, 1)
            dve.wait_ge(dinv_sd, 1)
            V.reciprocal(dinv[:], dinv[:]).then_inc(dinv_ready, 1)

            dve.wait_ge(cnt_summed, R3)
            onehot(E[1], keyf[:, 1, :]).then_inc(d1_ready, 1)
            rel = keyf[:, 3, :]
            then(V.tensor_tensor(OH, relid[:].unsqueeze(2).to_broadcast([P, R34, EC]), rel.unsqueeze(1).to_broadcast([P, R34, EC]),
                                 ALU.is_equal))
            V.tensor_copy(OHB, OH)
            then(V.memset(KEEP, 1.0))
            then(V.memset(KEEP.rearrange("p (r c) -> p r c", r=R34)[:, :, 0:1], 0.0))
            V.tensor_tensor_scan(RUN, KEEP, OH.rearrange("p r c -> p (r c)"), 0.0, ALU.mult, ALU.add).then_inc(run_ready, 1)
            dve.wait_ge(run_ready, 1)
            dve.wait_ge(offs_done, 1)
            then(V.tensor_copy(offs[:], PS[:, 4, 0:R34]))
            RV = RUN.rearrange("p (r c) -> p r c", r=R34)
            then(V.tensor_tensor(RV, RV, offs[:].unsqueeze(2).to_broadcast([P, R34, EC]), ALU.add))
            then(V.tensor_tensor(RV, RV, OH, ALU.mult))
            then(V.tensor_reduce(t34f[:, 0, :], RV.rearrange("p r c -> p c r"), AX.X, ALU.add))
            then(V.tensor_scalar(t34f[:, 0, :], t34f[:, 0, :], float(CAP), -1.0, ALU.min, ALU.add))
            then(V.tensor_scalar(t34f[:, 1, :], t34f[:, 0, :], float(P), float(1 - 2 * R34 * P), ALU.is_ge, ALU.mult))
            then(V.scalar_tensor_tensor(out=t34f[:, 1, :], in0=t34f[:, 0, :], scalar=float(2 * R34), in1=t34f[:, 1, :],
                                        op0=ALU.mult, op1=ALU.add))
            then(V.scalar_tensor_tensor(out=POS[:], in0=rel, scalar=2.0, in1=t34f[:, 1, :], op0=ALU.mult, op1=ALU.add))
            then(V.scalar_tensor_tensor(out=t34f[:, 2, :], in0=rel, scalar=float(NODES), in1=keyf[:, 1, :], op0=ALU.mult, op1=ALU.add))
            then(V.tensor_scalar(GIX[:], t34f[:, 2, :], -1.0, None, ALU.add))
            V.tensor_copy(PAY[:, :, 0], keyf[:, 0, :]).then_inc(idx_ready, 1)
            dve.wait_ge(c34_done, 1)
            C34 = PS[0:R34, 5, NODES:2 * NODES]
            V.tensor_reduce(bad[0:R34, 1:2], C34, AX.X, ALU.add)
            then(V.tensor_scalar(PRES, C34, 0.5, None, ALU.is_gt))
            then(V.tensor_tensor_scan(INCL, ones[0:R34, 0:1].to_broadcast([R34, NODES]), PRES, 0.0, ALU.mult, ALU.add))
            then(V.tensor_tensor(SLOT1, INCL, PRES, ALU.mult))
            V.tensor_copy(SLOTB, SLOT1).then_inc(slots_ready, 1)
            then(V.tensor_scalar(bad[0:R34, 0:1], INCL[:, NODES - 1:NODES], float(P), None, ALU.is_gt))
            V.scalar_tensor_tensor(out=bad[0:R34, 0:1], in0=bad[0:R34, 1:2], scalar=float(CAP), in1=bad[0:R34, 0:1],
                                   op0=ALU.is_gt, op1=ALU.add).then_inc(bad_ready, 1)
            dve.wait_ge(bad_summed, 1)
            V.tensor_copy(flag[:], PS[:, 4, 0:1]).then_inc(flag_ready, 1)

            for g in range(2):
                dve.wait_ge(w_used, 7 * g + 6)
                for b in range(1, BATCH, 2):
                    q, t = b % 4, b // 4
                    V.tensor_copy(QH[64:96, b, :].rearrange("p (h f) -> p h f", h=2),
                                  PS[32 * q:32 * q + 32, 4 + 2 * t:6 + 2 * t, 0:HALF]).then_inc(hg_copied, 1)
                with dve.Fori(0, NT) as t:
                    nb0 = t * (4 * BLOCKS) + g * BATCH * BLOCKS
                    for q in range(4 * BLOCKS):
                        b = q // BLOCKS
                        if q % BLOCKS == 0:
                            dve.wait_ge(qd_in[b % 2], t * 64 + (g * 4 * 32 + (b // 2 + 1) * 32))
                        dve.wait_ge(attn_done, nb0 + (q + 1))
                        dve.wait_ge(red_done, nb0 + q if q or g else t * (4 * BLOCKS) + 1)
                        V.tensor_tensor(PRD[q % 2].rearrange("p (u f) -> p u f", u=2), SIG[q % 2].rearrange("p (u f) -> p u f", u=2),
                                        QD[b % 2].unsqueeze(1).to_broadcast([P, 2, FEAT]), ALU.mult).then_inc(prod_done, 1)
                    dve.wait_ge(red_done, nb0 + (4 * BLOCKS + 1))
                    dve.wait_ge(tab_out, 32)
                    V.tensor_copy(qiN[:, bass.ds(t, 1), :].rearrange("p a (h f) -> p (a h) f", h=2), PS[:, 6:8, 0:HALF]).then_inc(qi_copied, 1)
                dve.wait_ge(qi_turned, g + 1)
                V.tensor_copy(qiT, PS[:, 0:3, :].rearrange("p b (k n) -> p (b k) n", k=2)).then_inc(qiT_copied, 1)
                dve.wait_ge(tanh_done, g + 1)
                then(V.tensor_tensor(tanhT, tanhT, hT[:], ALU.subtract))
                dve.wait_ge(alpha_done, g + 1)
                then(V.tensor_tensor(tanhT, tanhT, alphaT, ALU.mult))
                V.tensor_tensor(hT[:], hT[:], tanhT, ALU.add).then_inc(gate_done, 1)
                dve.wait_ge(h_turned, g + 1)
                for t in range(NT):
                    ps = PS[:, 2 * t:2 * t + 2, :].rearrange("p b n -> p (b n)")[:, 0:FEAT].rearrange("p (k n) -> p k n", k=KC)
                    if g == 0:
                        ins = V.tensor_copy(hN[:, t, :].rearrange("p (n k) -> p k n", k=KC), ps)
                    else:
                        xv = xN[:, t, :].rearrange("p (n k) -> p k n", k=KC)
                        ins = V.tensor_tensor(xv, ps, xv, ALU.add)
                if g == 0:
                    ins.then_inc(hN_ready, 1)
                else:
                    then(ins)

            def layer_norm(n):
                for t in range(NT):
                    for h in range(2):
                        ins = V.bn_stats(stats[:, t, h, :], xN[:, t, h * HALF:(h + 1) * HALF])
                then(ins)
                for t in range(NT):
                    ins = V.bn_aggr(mv[:, t, :], stats[:, t, :, :])
                ins.then_inc(var_ready, 1)
                dve.wait_ge(sd_ready, n)
                then(V.reciprocal(rstd[:], sd[:]))
                for t in range(NT):
                    ins = V.tensor_scalar(xN[:, t, :], xN[:, t, :], mv[:, t, 0:1], rstd[:, t:t + 1], ALU.subtract, ALU.mult)
                ins.then_inc(ln_done, 1)
                dve.wait_ge(ln_done, n)

            def gcn_out(n, bias):
                then(V.tensor_tensor(xN[:], xN[:], biasN[:, bias, :].unsqueeze(1).to_broadcast([P, NT, FEAT]), ALU.add))
                dve.wait_ge(gcn_sum, n)
                for t in range(NT):
                    xv = xN[:, t, :].rearrange("p (h f) -> p h f", h=2)
                    ins = V.scalar_tensor_tensor(out=xv, in0=PS[:, 2 * t:2 * t + 2, 0:HALF], scalar=dinv[:, t:t + 1], in1=xv,
                                                 op0=ALU.mult, op1=ALU.add)
                then(ins)

            layer_norm(1)
            dve.wait_ge(x_turned, 1)
            gcn_out(1, 1)
            layer_norm(2)
            dve.wait_ge(x_turned, 2)
            dve.wait_ge(cn_turned, 1)
            for t in range(NT):
                ins = V.tensor_copy(CN[:, t, :], PS[:, 4 + 2 * t:6 + 2 * t, :].rearrange("p b n -> p (b n)")[:, 0:FEAT])
            then(ins)
            V.tensor_scalar(NM, CN, 0.5, MASKED, ALU.is_lt, ALU.mult).then_inc(cn_ready, 1)
            dve.wait_ge(cn_ready, 1)

            u0 = 0
            for l, (H, bias) in enumerate(((HEADS1, 2), (1, 3))):
                for j in range(9):
                    dve.wait_ge(xr_turned, l * 9 + j + 1)
                    r, k = divmod(2 * j, KC)
                    V.tensor_copy(XT[:, r, k:k + 2, :], PS[:, j % 2, :].rearrange("p (k n) -> p k n", k=2)).then_inc(xrT_copied, 1)
                dve.wait_ge(qk_done, l + 1)
                V.tensor_copy(qkT[0:2 * H, :], PS[0:2 * H, 2:4, :].rearrange("p b n -> p (b n)")[:, 0:R3 * NODES]).then_inc(qk_copied, 1)
                dve.wait_ge(qkn_done, l + 1)
                V.tensor_copy(qkN[:, :, :, 0:2 * H], PS[:, 0, 0:NT * R3 * 2 * H].rearrange("p (t r h) -> p t r h", t=NT, r=R3)
                              ).then_inc(qkn_copied, 1)
                for h in range(H):
                    for t in range(NT):
                        u = u0 + 2 * h + t
                        c = u % 8
                        dve.wait_ge(score_done, u + 1)
                        then(V.scalar_tensor_tensor(out=SC[u % 2], in0=SC[u % 2], scalar=SLOPE, in1=SC[u % 2],
                                                    op0=ALU.mult, op1=ALU.max))
                        then(V.tensor_tensor_reduce(SC[u % 2], SC[u % 2], NM[:, t, :], 1.0, -3e38, ALU.add, ALU.max,
                                                    rmax[:, c:c + 1]))
                        V.tensor_scalar(nmax[:, c:c + 1], rmax[:, c:c + 1], -1.0, None, ALU.mult).then_inc(max_ready, 1)
                        dve.wait_ge(exp_done, u + 1)
                        V.tensor_tensor_reduce(EX[u % 2], EX[u % 2], CN[:, t, :], 1.0, 0.0, ALU.mult, ALU.add, zsum[:, c:c + 1]
                                               ).then_inc(p_ready, 1)
                        dve.wait_ge(p_ready, u + 1)
                        then(V.tensor_scalar(zinv[:, c:c + 1], zsum[:, c:c + 1], 1e-16, None, ALU.add))
                        then(V.reciprocal(zinv[:, c:c + 1], zinv[:, c:c + 1]))
                        dve.wait_ge(p_turned, u + 1)
                        V.tensor_copy(PT[u % 2], PS[:, 6:8, :].rearrange("p b (c n) -> p (b c) n", c=4)[:, 0:R3 * NT, :]
                                      ).then_inc(pt_copied, 1)
                dve.wait_ge(att_sum, u0 + 2 * H)
                if l == 1:
                    then(V.tensor_tensor(xN[:], xN[:], biasN[:, bias, :].unsqueeze(1).to_broadcast([P, NT, FEAT]), ALU.add))
                width = min(FEAT // H, HALF)
                for h in range(H):
                    for t in range(NT):
                        c = (u0 + 2 * h + t) % 8
                        for part in range(FEAT // H // width):
                            at = h * (FEAT // H) + part * width
                            other = biasN[:, bias, at:at + width] if l == 0 else xN[:, t, at:at + width]
                            dest = hN if l == 0 else xN
                            ins = V.scalar_tensor_tensor(out=dest[:, t, at:at + width],
                                                         in0=PS[:, 2 * t + at // HALF, at % HALF:at % HALF + width],
                                                         scalar=zinv[:, c:c + 1], in1=other, op0=ALU.mult, op1=ALU.add)
                then(ins)
                u0 += 2 * H
                if l == 0:
                    flat = lambda a: a.rearrange("p a b -> p (a b)")
                    V.tensor_scalar(flat(MT[0][:]), flat(hN[:]), 0.0, None, ALU.min).then_inc(elu_min, 1)
                    then(V.tensor_scalar(hN[:], hN[:], 0.0, -1.0, ALU.max, ALU.add))
                    dve.wait_ge(elu_exp, 1)
                    V.tensor_tensor(flat(hN[:]), flat(hN[:]), flat(xT[:]), ALU.add).then_inc(att_done, 1)
                    dve.wait_ge(att_done, 1)
            layer_norm(3)
            dve.wait_ge(x_turned, 3)

            def weight_lo(p, s):
                if s >= 6:
                    p, s = p + 1, s - 6
                j, q = divmod(s, 3)
                dve.wait_ge(w_hi, p * 6 + (s + 1))
                V.tensor_tensor(WS[1][q][:], W[(FIRST34 + j) % 2][:, :, q * THIRD:(q + 1) * THIRD], WS[0][q][:].bitcast(F32),
                                ALU.subtract).then_inc(w_lo if q < 2 else w_used, 1)

            def pair_onehots(p):
                dve.wait_ge(c_done, p + CREDIT)
                for j in range(2):
                    V.tensor_tensor(OS[j][:], iota1[:].unsqueeze(1).to_broadcast([P, 2, NODES]),
                                    KS[:, bass.ds(p * 4 + 2 * j, 2), 0:1].to_broadcast([P, 2, NODES]), ALU.is_equal)
                    ins = V.tensor_tensor(OT[j][:], iota1[:, 0:P].unsqueeze(1).to_broadcast([P, 2, P]),
                                          KS[:, bass.ds(p * 4 + 2 * j, 2), 1:2].to_broadcast([P, 2, P]), ALU.is_equal)
                ins.then_inc(oh_ready, 1)

            def slot_onehots(p, j):
                dve.wait_ge(scat_done, p * 6 + (3 * j - 3 + CREDIT))
                V.tensor_scalar(CT[j][:], SLB[:, bass.ds(p * (2 * NODES) + j * NODES, NODES)], pidx1[:, 0:1], None, ALU.is_equal
                                ).then_inc(ct_ready, 1)

            def count_inverse(p, mb):
                dve.wait_ge(c_done, p + (1 + CREDIT))
                V.tensor_scalar(rcm[:], PS[:, 7, 0:2], 1.0, None, ALU.max).then_inc(rc_max, 1)
                dve.wait_ge(rc_max, p + 1)
                V.reciprocal(rcs[:, mb, :], rcm[:]).then_inc(rc_ready, 1)

            def sums_lo(p, i, mb):
                dve.wait_ge(ms_hi, p * 3 + (i + 1))
                V.tensor_tensor(MS[1][mb][:, 2 * i:2 * i + 2, :], PS[:, 5 + i % 2, :].rearrange("p (k n) -> p k n", k=2),
                                MS[0][mb][:, 2 * i:2 * i + 2, :].bitcast(F32), ALU.subtract).then_inc(ms_ready, 1)

            def rows_lo(p, s, mb):
                dve.wait_ge(y_hi, p * 6 + (s + 1))
                V.scalar_tensor_tensor(out=YS[1][s % 2][:], in0=PS[:, 3 + s % 2, 0:THIRD], scalar=rcs[:, mb, s // 3:s // 3 + 1],
                                       in1=YS[0][s % 2][:].bitcast(F32), op0=ALU.mult, op1=ALU.subtract).then_inc(y_ready, 1)

            def pair(p, mb, nxt=True):
                slot_onehots(p, 0)
                if nxt:
                    pair_onehots(p + 1)
                for s in range(6):
                    if s:
                        rows_lo(p, s - 1, mb)
                    if nxt or s + 2 < 6:
                        weight_lo(p, s + 2)
                    if s == 1:
                        slot_onehots(p, 1)
                    if nxt and s == 2:
                        count_inverse(p + 1, 1 - mb)
                    if nxt and s >= 4:
                        sums_lo(p + 1, s - 4, 1 - mb)
                if nxt:
                    sums_lo(p + 1, 2, 1 - mb)
                rows_lo(p, 5, mb)

            def keys34(r, buf):
                return V.scalar_tensor_tensor(out=ekey[:, buf, :], in0=keyf[:, 3, :], scalar=relid[:, r], in1=keyf[:, 1, :],
                                              op0=ALU.is_equal, op1=ALU.mult)


            def onehot34(r, rel, buf):
                dve.wait_ge(cnt_summed, r + 2)
                keys34(rel, buf).then_inc(key_ready, 1)
                dve.wait_ge(key_ready, r + 1)
                onehot(E[buf], ekey[:, buf, :]).then_inc(e_ready, 1)

            def normalise34(r, j):
                dve.wait_ge(deg_spread, r + (R3 + 1))
                V.tensor_scalar(RC[:, 0, :], PS[:, 5, 0:NODES], 1.0, None, ALU.max).then_inc(rc_step, 1)
                dve.wait_ge(rc_step, r * 2 + 1)
                V.reciprocal(RC[:, 1, :], RC[:, 0, :]).then_inc(rc_step, 1)
                dve.wait_ge(rc_step, r * 2 + 2)
                dve.wait_ge(agg_done, (r + (2 * R3 - 1)) * 3)
                V.tensor_tensor(N34[j], A34[j], RC[:, 1, :].unsqueeze(1).to_broadcast([P, NT, NODES]), ALU.mult).then_inc(nrm_ready, 1)


            dve.wait_ge(sorted_in, 32)
            overflow = dve.value_load(flag[0:1, 0:1])
            with dve.If(overflow < 1):
                for x in (rc_ready, ms_ready, y_ready):
                    dve.sem_inc(x, CREDIT)
                pair_onehots(0)
                dve.wait_ge(xs_hi, 1)
                V.tensor_tensor(XS[1][:], xN[:], XS[0][:].bitcast(F32), ALU.subtract).then_inc(xs_ready, 1)
                weight_lo(0, 0)
                weight_lo(0, 1)
                count_inverse(0, 0)
                for i in range(3):
                    sums_lo(0, i, 0)
                with dve.Fori(0, (PAIRS34 - 1) // 2) as i:
                    pair(i * 2, 0)
                    pair(i * 2 + 1, 1)
                pair(PAIRS34 - 1, 0, nxt=False)
            with dve.Else():
                onehot(S1[:], keyf[:, 0, :]).then_inc(s1_ready, 1)
                onehot34(0, slice(0, 1), 1)
                with dve.Fori(0, LOOP34) as i:
                    for j in range(2):
                        onehot34(i * 2 + (j + 1), bass.ds(i * 2 + (j + 1), 1), j)
                        normalise34(i * 2 + j, j)
                onehot34(R34 - 1, slice(R34 - 1, R34), 0)
                normalise34(R34 - 2, 0)
                normalise34(R34 - 1, 1)
            dve.wait_ge(enc_done, 1)
            V.tensor_tensor(hN[:], PS[:, 0:3, :].rearrange("p b n -> p (b n)").rearrange("p (t f) -> p t f", t=NT),
                            biasN[:, 4, :].unsqueeze(1).to_broadcast([P, NT, FEAT]), ALU.add).then_inc(h1_copied, 1)
            gcn_out(2, 5)
            layer_norm(4)


_IN = {
    "x": ("x", None), "xT": ("x", "T"), "q": ("L0_gnn_query_embs", "rows"), "qT": ("L0_gnn_query_embs", "rowsT"),
    "src": ("src", None), "dst": ("dst", None), "t3": ("edge_type_3", None), "t34": ("edge_type_34", None),
    "W_rel1": ("L0_gnn_W_rel1", None), "W_root1": ("L0_gnn_W_root1", None), "b1": ("L0_gnn_b1", None),
    "W_rel2": ("L0_gnn_W_rel2", None), "W_root2": ("L0_gnn_W_root2", None), "b2": ("L0_gnn_b2", None),
    "WgT": ("L0_gnn_Wg", "T"), "bg": ("L0_gnn_bg", None), "WqT": ("L0_gnn_Wq", "T"), "bq": ("L0_gnn_bq", None),
    "L1_W": ("L1_gnn_W", None), "L1_b": ("L1_gnn_b", None),
    "W1": ("L2_gnn_W1", None), "qk1": (("L2_gnn_q1", "L2_gnn_k1"), "cols"), "L2_b1": ("L2_gnn_b1", None),
    "W2": ("L2_gnn_W2", None), "qk2": (("L2_gnn_q2", "L2_gnn_k2"), "cols"), "L2_b2": ("L2_gnn_b2", None),
    "L3_rel": ("L3_gnn_W_rel", None), "L3_root": ("L3_gnn_W_root", None), "b_rgcn": ("L3_gnn_b_rgcn", None),
    "L3_gcn": ("L3_gnn_W_gcn", None), "b_gcn": ("L3_gnn_b_gcn", None),
}


def kernel(**inputs):
    import numpy as np
    import concourse.bacc as bacc
    from concourse.bass_utils import run_bass_kernel_spmd

    nc = bacc.Bacc("TRN2", target_bir_lowering=False, num_devices=1)
    arrays, handles = {}, {}
    for name, (source, layout) in _IN.items():
        if layout == "cols":
            a = np.concatenate([np.asarray(inputs[n]) for n in source], axis=1)
        else:
            a = np.asarray(inputs[source])
        if layout in ("rows", "rowsT"):
            a = a.reshape(-1, a.shape[-1])
        if layout in ("T", "rowsT"):
            a = a.T
        a = np.ascontiguousarray(a)
        arrays[f"in_{name}"] = a
        handles[name] = nc.dram_tensor(f"in_{name}", a.shape, mybir.dt.from_np(a.dtype), kind="ExternalInput").ap()
    handles["out"] = nc.dram_tensor("out", (NODES, FEAT), F32, kind="ExternalOutput").ap()
    build(nc, handles)
    r = run_bass_kernel_spmd(nc, [arrays], core_ids=[0])
    return r.results[0]["out"]
```

```python
from contextlib import ExitStack
from itertools import product

import concourse.bass as bass
from concourse import mybir

P = 128
F32 = mybir.dt.float32
F32R = mybir.dt.float32r
BF16 = mybir.dt.bfloat16
I32 = mybir.dt.int32
ALU = mybir.AluOpType
ACT = mybir.ActivationFunctionType
AX = mybir.AxisListType

NODES, FEAT, EDGES = 256, 768, 4352
NT = NODES // P
KC = FEAT // P
EC = EDGES // P
HALF = FEAT // 2
BATCH, QLEN = 8, 64
BN = NODES // BATCH
QUADS = BN // 4
HQ = QLEN // 2
GATE_B = BATCH // NT
UNITS = NT * 3
UB = 2 * QUADS
R3, R34 = 3, 34
HEADS1 = 4
SLOPE, MASKED = 0.2, -1e30
CAP = 2 * P
THIRD = FEAT // 3
PAIRS34 = R34 // 2
CREDIT = 7


def build(nc, A):
    with ExitStack() as ctx:
        def sb(name, shape, dt=F32):
            return ctx.enter_context(nc.sbuf_tensor(name, shape, dt))

        def sem(name):
            return ctx.enter_context(nc.semaphore(name))

        PS = ctx.enter_context(nc.psum_tensor("PS", [P, 8, 512], F32))
        W = [sb(f"W{i}", [P, KC, FEAT]) for i in range(2)]
        xN, xT = sb("xN", [P, NT, FEAT]), sb("xT", [P, KC, NODES])
        at_h = (nc.sbuf_base + 63) // 64 * 64
        hN, hT = sb("hN", [P, NT, FEAT]), sb("hT", [P, KC, NODES])
        biasN = sb("biasN", [P, 6, FEAT])
        S1 = nc.alloc_sbuf_tensor_at("S1", [P, EC, NODES], BF16, offset=at_h)
        SMALL = 16 * 10
        AI = sb("AI", [P, NT, NODES])
        base = (nc.sbuf_base + 63) // 64 * 64
        ctx.enter_context(nc.sbuf_tensor("stretch", [P, 111 * 256], F32))

        def put(name, shape, dt, at):
            return nc.alloc_sbuf_tensor_at(name, shape, dt, offset=base + int(at * 1024))

        MT = [put(f"MT{i}", [P, KC, NODES], F32, 6 * i) for i in range(2)]
        CNT = put("CNT", [P, R3, NT, NODES], F32, 12)
        NRM = put("NRM", [P, R3, NT, NODES], F32, 18)
        arena = put("arena", [P, 14848], F32, 41)
        selmem = put("selmem", [P, 3072], F32, 99)
        ident, ones = sb("ident", [P, P]), sb("ones", [P, P])
        iota1, iotab = sb("iota1", [P, NODES]), sb("iotab", [P, NODES], BF16)
        relid = sb("relid", [P, R34])
        keys = sb("keys", [P, 4, EC], I32)
        keyf = sb("keyf", [P, 4, EC])
        ekey = sb("ekey", [P, 2, EC])
        biasT = sb("biasT", [P, 3, KC])
        qk1, qk2 = sb("qk1", [P, KC, 2 * HEADS1]), sb("qk2", [P, KC, 2])
        qkT = sb("qkT", [2 * HEADS1, R3 * NODES])
        qkN = sb("qkN", [P, NT, R3, 2 * HEADS1])
        RC = sb("RC", [P, 2, NODES])
        stats, mv = sb("stats", [P, NT, 2, 6]), sb("mv", [P, NT, 2])
        sd, rstd = sb("sd", [P, NT]), sb("rstd", [P, NT])
        eps = sb("eps", [P, 1])
        dinv = sb("dinv", [P, NT])
        rmax, nmax = sb("rmax", [P, 8]), sb("nmax", [P, 8])
        zsum, zinv = sb("zsum", [P, 8]), sb("zinv", [P, 8])

        def view(t, at, n, dt=F32):
            v = t[:, at:at + n]
            return v if dt == F32 else v.bitcast(dt)

        QH = [put(f"QH{h}", [P, UNITS, GATE_B, THIRD], F32R, 24 + 24 * h) for h in range(2)]
        SIG = [view(arena, 7936 + 1024 * i, 1024) for i in range(2)]
        PRD = [view(arena, 9984 + 1024 * i, 1024) for i in range(2)]
        QD = [view(arena, 12032 + 1024 * i, 1024) for i in range(2)]
        qiT, tanhT = MT[0][:], MT[1][:]
        alphaT = view(arena, 7936, 1536).rearrange("p (k n) -> p k n", k=KC)
        qiN = hN
        qT = [MT[0], MT[1]]

        def tiles3(bank):
            return PS[:, bank:bank + 3, :].rearrange("p b n -> p (b n)").rearrange("p (t q f) -> p t q f", t=NT, q=3)

        def query_rows(part, t, j, h):
            return QH[h][HQ * part:HQ * part + HQ, 3 * t:3 * t + 3].rearrange("p q (c j) f -> p j c q f", j=2)[:, j]

        def query_sums(t, j, h):
            return tiles3(3 * t)[QLEN * j + HQ * h:QLEN * j + HQ * h + HQ]

        def node_rows(part, b):
            return QH[0][64 + BN * part:64 + BN * part + BN, :, b, :].rearrange("p (t q) f -> p t q f", t=NT)

        E = [put(f"E{i}", [P, EC, NODES], BF16, 72 + 17 * i)[:] for i in range(2)]
        WL = [[put(f"WL{x}{b}", [P, KC, 2, P], F32R, 72 + 12 * b + 6 * i) for b in range(2)] for i, x in enumerate(("hi", "lo"))]

        def third_turned(Wm, q):
            return Wm[:].rearrange("p k (f c) -> p k c f", c=KC)[:, :, 2 * q:2 * q + 2, :]

        XR = view(arena, 0, 4608).rearrange("p (r t f) -> p r t f", r=R3, t=NT)
        XT = view(arena, 4608, 4608).rearrange("p (r k n) -> p r k n", r=R3, k=KC)
        SC = [view(arena, 9216 + 768 * i, 768) for i in range(2)]
        EX = [view(arena, 10752 + 768 * i, 768) for i in range(2)]
        TS = [put(f"T{x}", [P, KC, NODES], F32R, 6 * i) for i, x in enumerate(("hi", "lo"))]
        WT = [[put(f"WT{x}{b}", [P, KC, THIRD], F32R, 12 + 12 * b + 6 * i) for b in range(2)] for i, x in enumerate(("hi", "lo"))]
        PT = [view(arena, 12288 + 768 * i, 768).rearrange("p (c n) -> p c n", c=R3 * NT) for i in range(2)]
        SEL = put("SEL", [P, QUADS, P], F32R, 96)
        RED = view(selmem, 7 * 256, 256).rearrange("p (i m) -> p i m", i=QUADS)
        CN = view(selmem, 0, 1536).rearrange("p (t c) -> p t c", t=NT)
        NM = view(selmem, 1536, 1536).rearrange("p (t c) -> p t c", t=NT)
        OH = view(arena, 7936, 1156).rearrange("p (r c) -> p r c", r=R34)
        RUN = view(arena, 9092, 1156)
        KEEP = view(arena, 10248, 1156)
        OHB = view(arena, 11404, 578, BF16).rearrange("p (r c) -> p r c", r=R34)
        PRES, INCL, SLOT1 = (hN[0:R34, 0, 256 * i:256 * i + 256] for i in range(3))
        SLOTB = hN[0:R34, 1, 0:128].bitcast(BF16)
        WS = [[put(f"W{x}{q}", [P, KC, THIRD], F32R, 41 + 12 * q + 6 * i) for q in range(3)] for i, x in enumerate(("hi", "lo"))]
        MS = [[put(f"M{x}{b}", [P, KC, NODES], F32R, 77 + 12 * b + 6 * i) for b in range(2)] for i, x in enumerate(("hi", "lo"))]
        XS = [put(f"X{x}", [P, NT, FEAT], F32R, 6 * i) for i, x in enumerate(("hi", "lo"))]
        BB = put("BB", [P, NT * NODES], F32R, 12)
        CT = [put(f"CT{j}", [P, NODES], F32R, 14 + j) for j in range(2)]
        YS = [[put(f"Y{x}{b}", [P, THIRD], F32R, 16 + 2 * b + i) for b in range(2)] for i, x in enumerate(("hi", "lo"))]
        OS = [put(f"OS{j}", [P, 2, NODES], BF16, 20 + j) for j in range(2)]
        OT = [put(f"OT{j}", [P, 2, P], BF16, 22 + 0.5 * j) for j in range(2)]
        SLB = put("SLB", [P, R34 * NODES], BF16, 24)
        PAY = sb("PAY", [P, EC, 2])
        KS = sb("KS", [P, 2 * R34, 2])
        POS, GIX = sb("POS", [P, EC], I32), sb("GIX", [P, EC], I32)
        t34f = sb("t34f", [P, 3, EC])
        offs = sb("offs", [P, R34])
        spare = sb("spare", [P, EC])
        UT = sb("UT", [P, P])
        pidx1, onesb = sb("pidx1", [P, 1]), sb("onesb", [P, 1], BF16)
        zrow = sb("zrow", [P, 2 * 2 * R34])
        bad, flag = sb("bad", [P, 2]), sb("flag", [P, 1], I32)
        rcs, rcm = sb("rcs", [P, 2, 2]), sb("rcm", [P, 2])
        key_ready, rc_step = sem("key_ready"), sem("rc_step")
        slot_tab = nc.dram_tensor("slot_tab", (R34 * NODES, 1), F32).ap()
        slot_tabb = nc.dram_tensor("slot_tabb", (R34 * NODES,), BF16).ap()
        by_rel = nc.dram_tensor("by_rel", (R34 * CAP + EDGES, 2), F32).ap()
        S1L = put("S1L", [P, EC, NODES], BF16, 24)
        A34 = [CNT[:, i] for i in range(2)]
        N34 = [NRM[:, i] for i in range(2)]

        keys_in, x_in, bg_in, small_in, out_done = (sem(n) for n in ("keys_in", "x_in", "bg_in", "small_in", "out_done"))
        q_in = [sem("q_in0"), sem("q_in1")]
        first_in = [sem("first_in0"), sem("first_in1")]
        w_in = [sem("w_in0"), sem("w_in1")]
        qd_in = [sem("qd_in0"), sem("qd_in1")]
        w_used = sem("w_used")
        pool_step, consts = sem("pool_step"), sem("consts")
        dve_step = sem("dve_step")
        sel_ready, s1_ready, e_ready = sem("sel_ready"), sem("s1_ready"), sem("e_ready")
        cnt_summed, cnt_copied = sem("cnt_summed"), sem("cnt_copied")
        deg_spread, nrm_ready = sem("deg_spread"), sem("nrm_ready")
        ai_ready, deg_summed, dinv_sd, dinv_ready = sem("ai_ready"), sem("deg_summed"), sem("dinv_sd"), sem("dinv_ready")
        agg_done, mt_copied = sem("agg_done"), sem("mt_copied")
        q_done, qg_hi, qg_ready = sem("q_done"), sem("qg_hi"), sem("qg_ready")
        relu_done = sem("relu_done")
        hg_hi, hg_ready, hg_copied = sem("hg_hi"), sem("hg_ready"), sem("hg_copied")
        sums_done, attn_done, prod_done, red_done = sem("sums_done"), sem("attn_done"), sem("prod_done"), sem("red_done")
        qi_copied, qi_turned, qiT_copied, tanh_done = sem("qi_copied"), sem("qi_turned"), sem("qiT_copied"), sem("tanh_done")
        alpha_done, gate_done = sem("alpha_done"), sem("gate_done")
        h_turned, hN_ready = sem("h_turned"), sem("hN_ready")
        var_ready, sd_ready, ln_done, x_turned, xT_ready = (sem(n) for n in ("var_ready", "sd_ready", "ln_done", "x_turned", "xT_ready"))
        gcn_scaled, gcn_sum = sem("gcn_scaled"), sem("gcn_sum")
        cn_turned, cn_ready = sem("cn_turned"), sem("cn_ready")
        wl_hi, wl_ready, wl_used = sem("wl_hi"), sem("wl_ready"), sem("wl_used")
        hs_hi, hs_ready, mt_hi = sem("hs_hi"), sem("hs_ready"), sem("mt_hi")
        wt_hi, wt_ready, wt_used, ts_ready = sem("wt_hi"), sem("wt_ready"), sem("wt_used"), sem("ts_ready")
        xr_copied, xr_turned, xrT_copied = sem("xr_copied"), sem("xr_turned"), sem("xrT_copied")
        qk_done, qk_copied, qkn_done, qkn_copied = sem("qk_done"), sem("qk_copied"), sem("qkn_done"), sem("qkn_copied")
        key_spread, score_done, max_ready, exp_done = sem("key_spread"), sem("score_done"), sem("max_ready"), sem("exp_done")
        p_ready, p_turned, pt_copied, att_sum, att_done = (sem(n) for n in ("p_ready", "p_turned", "pt_copied", "att_sum", "att_done"))
        elu_min, elu_exp = sem("elu_min"), sem("elu_exp")
        enc_done, h1_copied = sem("enc_done"), sem("h1_copied")
        run_ready, offs_done, d1_ready, c34_done, slots_ready, bad_ready, bad_summed, flag_ready, idx_ready = (
            sem(n) for n in ("run_ready", "offs_done", "d1_ready", "c34_done", "slots_ready", "bad_ready", "bad_summed",
                             "flag_ready", "idx_ready"))
        zero_out, tab_out, slot_in, sorted_out, sorted_in = (sem(n) for n in ("zero_out", "tab_out", "slot_in", "sorted_out", "sorted_in"))
        xs_hi, xs_ready, oh_ready, b_done, bb_ready, c_done, rc_max, rc_ready = (
            sem(n) for n in ("xs_hi", "xs_ready", "oh_ready", "b_done", "bb_ready", "c_done", "rc_max", "rc_ready"))
        msum_done, ms_hi, ms_ready, w_hi, w_lo, y_done, y_hi, y_ready, scat_done, ct_ready = (
            sem(n) for n in ("msum_done", "ms_hi", "ms_ready", "w_hi", "w_lo", "y_done", "y_hi", "y_ready", "scat_done", "ct_ready"))

        turned = lambda a: a.rearrange("(p t) n -> p t n", t=KC)
        WgT, WqT = A["WgT"], A["WqT"]
        gate_w = [WgT[0:FEAT], WqT[0:FEAT], WqT[FEAT:]]
        stream = [WgT[FEAT:], A["W_root1"]] + [A["W_rel1"][r] for r in range(R3)] + gate_w
        stream += [A["W_root2"]] + [A["W_rel2"][r] for r in range(R3)] + gate_w
        stream += [A["L1_W"]] + [A["W1"][r] for r in range(R3)] + [A["W2"][r] for r in range(R3)] + [A["L3_root"]]
        FIRST34 = len(stream)
        LOOP34 = (R34 - 2) // 2

        block = ctx.enter_context(nc.Block())

        @block.sync
        def _(sp):
            for i, n in enumerate(("src", "dst", "t3", "t34")):
                sp.dma_start(keys[:, i, :], A[n].rearrange("(p c) -> p c", c=EC)).then_inc(keys_in, 16)
            for m, w in enumerate(stream):
                if m < 2:
                    sp.dma_start(qT[m][:], turned(A["qT"])[:, :, m * NODES:(m + 1) * NODES]).then_inc(q_in[m], 16)
                else:
                    sp.wait_ge(w_used, m - 1)
                if m == 0:
                    for q in range(3):
                        cols = slice(q * THIRD, (q + 1) * THIRD)
                        sp.dma_start(W[0][:, :, cols], turned(w)[:, :, cols]).then_inc(w_in[0] if q == 2 else first_in[q], 16)
                else:
                    sp.dma_start(W[m % 2][:], turned(w)).then_inc(w_in[m % 2], 16)
            with sp.Fori(0, LOOP34 + 1) as i:
                for j in range(2):
                    sp.wait_ge(w_used, i * 2 + (FIRST34 + j - 1))
                    sp.dma_start(W[(FIRST34 + j) % 2][:], A["L3_rel"][bass.ds(i * 2 + j, 1)].rearrange("a (p t) n -> p (a t) n", t=KC)
                                 ).then_inc(w_in[(FIRST34 + j) % 2], 16)
            m = FIRST34 + R34
            sp.wait_ge(w_used, m - 1)
            sp.dma_start(W[m % 2][:], turned(A["L3_gcn"])).then_inc(w_in[m % 2], 16)
            sp.wait_ge(ln_done, 4)
            sp.dma_start(A["out"].rearrange("(t p) f -> p t f", p=P), xN[:]).then_inc(out_done, 16)
            sp.wait_ge(out_done, 16)

        @block.gpsimd
        def _(pool):
            steps = [0]

            def then(ins):
                steps[0] += 1
                ins.then_inc(pool_step, 1)
                pool.wait_ge(pool_step, steps[0])

            then(nc.gpsimd.iota(iota1[:], pattern=[[1, NODES]], base=1, channel_multiplier=0,
                                allow_small_or_imprecise_dtypes=True))
            nc.gpsimd.tensor_copy(iotab[:], iota1[:]).then_inc(consts, 1)
            pool.dma_start(biasN[:, 5, :], A["bg"].partition_broadcast(P)).then_inc(bg_in, 16)
            then(nc.gpsimd.iota(relid[:], pattern=[[1, R34]], base=0, channel_multiplier=0,
                                allow_small_or_imprecise_dtypes=True))
            then(nc.gpsimd.iota(pidx1[:], pattern=[[0, 1]], base=1, channel_multiplier=1,
                                allow_small_or_imprecise_dtypes=True))
            then(nc.gpsimd.memset(onesb[:], 1.0))
            then(nc.gpsimd.memset(zrow[:], 0.0))
            pool.dma_start(by_rel[0:R34 * CAP].rearrange("(p a) b -> p (a b)", p=P), zrow[:]).then_inc(zero_out, 16)
            then(nc.gpsimd.iota(spare[:], pattern=[[1, EC]], base=R34 * CAP, channel_multiplier=EC,
                                allow_small_or_imprecise_dtypes=True))
            then(nc.gpsimd.memset(ones[:], 1.0))
            then(nc.gpsimd.affine_select(out=UT[:], in_=ones[:], compare_op=ALU.is_gt, fill=0.0, base=0,
                                         pattern=[[1, P]], channel_multiplier=-1))
            then(nc.gpsimd.memset(RED, 0.0))
            for j in range(4):
                v = RED[HQ * j:HQ * j + HQ]
                then(nc.gpsimd.affine_select(out=v, in_=v, compare_op=ALU.not_equal, fill=1.0, base=j,
                                             pattern=[[4, QUADS], [-1, BN]], channel_multiplier=0))
            then(nc.gpsimd.memset(ident[:], 0.0))
            nc.gpsimd.affine_select(out=ident[:], in_=ident[:], compare_op=ALU.not_equal, fill=1.0, base=0,
                                    pattern=[[-1, P]], channel_multiplier=1).then_inc(consts, 1)
            pool.wait_ge(w_in[0], 16)
            pool.dma_start(xN[:], A["x"].rearrange("(t p) f -> p t f", p=P)).then_inc(x_in, 16)
            pool.dma_start(xT[:], turned(A["xT"])).then_inc(x_in, 16)
            pool.wait_ge(cnt_summed, R3)
            for i, n in enumerate(("b1", "b2", "bq")):
                pool.dma_start(biasT[:, i, :], A[n].rearrange("(p t) -> p t", t=KC)).then_inc(small_in, 16)
            for i, n in enumerate(("b_gcn", "L1_b", "L2_b1", "L2_b2", "b_rgcn")):
                pool.dma_start(biasN[:, i, :], A[n].partition_broadcast(P)).then_inc(small_in, 16)
            for t, n in ((qk1, "qk1"), (qk2, "qk2")):
                pool.dma_start(t[:], turned(A[n])).then_inc(small_in, 16)
            pool.wait_ge(slots_ready, 1)
            pool.dma_start(slot_tab.rearrange("(r n) a -> r (n a)", r=R34), SLOT1).then_inc(tab_out, 16)
            pool.dma_start(slot_tabb.rearrange("(r n) -> r n", r=R34), SLOTB).then_inc(tab_out, 16)
            def queries(u, h):
                for j in range(4):
                    pool.dma_start(QD[h][HQ * j:HQ * j + HQ, :], A["qU"][bass.ds(u, 1), HQ * h:HQ * h + HQ].rearrange(
                        "a l n -> (a l) n")).then_inc(qd_in[h], 16)

            pool.wait_ge(c34_done, 1)
            for g in range(2):
                for h in range(2):
                    if g:
                        pool.wait_ge(wl_used, 3 * (R3 + 1))
                        pool.wait_ge(prod_done, UNITS * UB + ((h - 1) * QUADS + 1))
                    queries(0, h)
                pool.wait_ge(hg_ready, GATE_B * (g + 1))
                pool.dma_start(QH[1][64:P], QH[0][64:P]).then_inc(hg_copied, 16)
                with pool.Fori(1, UNITS) as u:
                    for h in range(2):
                        pool.wait_ge(prod_done, u * UB + (g * UNITS * UB + (h - 1) * QUADS + 1))
                        queries(u, h)
            pool.wait_ge(idx_ready, 1)
            pool.wait_ge(tab_out, 32)
            pool.wait_ge(zero_out, 16)
            for c in range(EC):
                pool.indirect_dma_start(PAY[:, c, 1:2], None, slot_tab, bass.IndirectOffsetOnAxis(GIX[:, c:c + 1], 0)
                                        ).then_inc(slot_in, 16)
            pool.wait_ge(slot_in, 16 * EC)
            for c in range(EC):
                pool.indirect_dma_start(by_rel, bass.IndirectOffsetOnAxis(POS[:, c:c + 1], 0), PAY[:, c, :], None
                                        ).then_inc(sorted_out, 16)
            pool.wait_ge(sorted_out, 16 * EC)
            pool.dma_start(KS[:].rearrange("p a b -> p (a b)"), by_rel[0:R34 * CAP].rearrange("(p a) b -> p (a b)", p=P)).then_inc(sorted_in, 16)
            pool.wait_ge(wt_used, 3 * 2 * R3)
            pool.dma_start(SLB[:], slot_tabb.partition_broadcast(P)).then_inc(sorted_in, 16)

        @block.tensor
        def _(pe):
            def weights(m):
                pe.wait_ge(w_in[m % 2], 16 * (m // 2 + 1))

            def natural(bank, T, Wm, first=True, last=True):
                for t in range(NT):
                    for h in range(2):
                        for k in range(KC):
                            mm = pe.matmul(PS[:, bank + 2 * t + h, 0:HALF], T[:, k, t * P:(t + 1) * P],
                                           Wm[:, k, h * HALF:(h + 1) * HALF],
                                           start=first and k == 0, stop=last and k == KC - 1)
                return mm

            def turned_product(bank, T, Wm, first=True, last=True):
                for m in range(KC):
                    for k in range(KC):
                        mm = pe.matmul(PS[:, bank + m // 2, (m % 2) * NODES:(m % 2 + 1) * NODES], Wm[:, k, m::KC],
                                       T[:, k, :], start=first and k == 0 and m % 2 == 0,
                                       stop=last and k == KC - 1 and m % 2 == 1, skip_group_check=True)
                return mm

            def counts(n, e, bank=4, S1=S1):
                pe.wait_ge(e_ready, n + 1)
                pe.wait_ge(cnt_copied, n)
                for s in range(NT):
                    for c in range(EC):
                        mm = pe.matmul(PS[:, bank, s * NODES:(s + 1) * NODES], S1[:, c, s * P:(s + 1) * P], E[e][:, c, :],
                                       start=c == 0, stop=c == EC - 1)
                mm.then_inc(cnt_summed, 1)

            def spread_counts(n, cnt, bank=5):
                pe.wait_ge(cnt_copied, n + 1)
                pe.wait_ge(nrm_ready, n)
                for s in range(NT):
                    mm = pe.matmul(PS[:, bank, 0:NODES], ones[:], cnt[:, s, :], start=s == 0, stop=s == NT - 1)
                mm.then_inc(deg_spread, 1)

            def natural3(T, Wm, bank=0, first=False, last=False, tiles=range(NT), thirds=range(3)):
                for t in tiles:
                    for q in thirds:
                        at = 3 * t + q
                        out = PS[:, bank + at // 2, (at % 2) * THIRD:(at % 2 + 1) * THIRD]
                        for k in range(KC):
                            mm = pe.matmul(out, T[:, k, t * P:(t + 1) * P], Wm[:, k, q * THIRD:(q + 1) * THIRD],
                                           start=first and k == 0 and at % 2 == 0,
                                           stop=last and k == KC - 1 and at % 2 == 1, skip_group_check=True)
                return mm

            def aggregate(n, x, nrm):
                for j in range(3):
                    if not isinstance(n, int) or n * 3 + j > 1:
                        pe.wait_ge(mt_copied, n * 3 + j - 1)
                    for kk in range(2):
                        k = 2 * j + kk
                        for s in range(NT):
                            mm = pe.matmul(PS[:, 6 + j % 2, kk * NODES:(kk + 1) * NODES], x[:, s, k::KC], nrm[:, s, :],
                                           start=s == 0, stop=s == NT - 1)
                    mm.then_inc(agg_done, 1)

            def to_natural(bank, T):
                for t in range(NT):
                    for k in range(KC):
                        mm = pe.transpose(PS[:, bank + 2 * t + k // 4, (k % 4) * P:(k % 4 + 1) * P],
                                          T[:, k, t * P:(t + 1) * P], ident[:])
                return mm

            def to_turned(bank, N):
                for k in range(KC):
                    for t in range(NT):
                        mm = pe.transpose(PS[:, bank + k // 2, (k % 2) * NODES + t * P:(k % 2) * NODES + (t + 1) * P],
                                          N[:, t, k::KC], ident[:])
                return mm

            pe.sem_inc(red_done, 1)
            pe.wait_ge(consts, 2)
            pe.wait_ge(bg_in, 16)
            for at in range(4 * 3):
                pe.matmul(PS[:, at // 2, (at % 2) * THIRD:(at % 2 + 1) * THIRD], ones[0:1, :],
                          biasN[0:1, 5, at % 3 * THIRD:(at % 3 + 1) * THIRD], start=at % 2 == 0, stop=False, skip_group_check=True)
            pe.wait_ge(q_in[0], 16)
            for q in range(3):
                pe.wait_ge(w_in[0] if q == 2 else first_in[q], 16)
                mm = natural3(qT[0], W[0], last=True, thirds=[q])
            mm.then_inc(q_done, 1)
            for r in range(R3):
                if r == 0:
                    pe.wait_ge(s1_ready, 1)
                counts(r, r % 2, bank=6)
                if r < 2:
                    if r == 0:
                        pe.wait_ge(q_in[1], 16)
                    mm = natural3(qT[1], W[0], bank=3, last=True, tiles=[r])
                    if r == 1:
                        mm.then_inc(w_used, 1)
                spread_counts(r, CNT[:, r], bank=7)
            pe.wait_ge(qg_ready, 8)

            def split_product(p):
                for q in range(3):
                    w = 3 * p + q
                    pe.wait_ge(wl_ready, w + 1)
                    for c in range(2):
                        for i, (k, (a, b)) in enumerate(product(range(KC), ((0, 0), (1, 0), (0, 1)))):
                            mm = pe.matmul(PS[:, q, c * NODES:(c + 1) * NODES], WL[b][w % 2][:, k, c, :], TS[a][:, k, :],
                                           start=p == 0 and i == 0 and c == 0, stop=p == R3 and i == 3 * KC - 1 and c == 1,
                                           skip_group_check=True)
                    mm.then_inc(wl_used, 1)

            for g in range(2):
                m0 = 1 + 7 * g
                src = xN if g == 0 else hN
                if g == 0:
                    pe.wait_ge(x_in, 32)
                else:
                    pe.wait_ge(gate_done, 1)
                if g == 0:
                    weights(m0)
                    turned_product(0, xT, W[m0 % 2], last=False).then_inc(w_used, 1)
                else:
                    pe.wait_ge(hN_ready, 1)
                    pe.wait_ge(hs_ready, 1)
                    split_product(0)
                for r in range(R3):
                    if g == 0 and r == 0:
                        pe.wait_ge(nrm_ready, R3)
                    n = g * R3 + r
                    aggregate(n, src, NRM[:, r])
                    pe.wait_ge(mt_copied, 3 * (n + 1))
                    if g == 0:
                        weights(m0 + 1 + r)
                        mm = turned_product(0, MT[n % 2], W[(m0 + 1 + r) % 2], first=False, last=r == R3 - 1)
                        mm.then_inc(w_used, 1)
                    else:
                        split_product(r + 1)
                    if n == 0:
                        pe.wait_ge(run_ready, 1)
                        pe.matmul(PS[:, 4, 0:R34], UT[:], RUN.rearrange("p (r c) -> p r c", r=R34)[:, :, EC - 1],
                                  start=True, stop=True).then_inc(offs_done, 1)
                        pe.wait_ge(d1_ready, 1)
                        for c in range(EC):
                            mm = pe.matmul(PS[0:R34, 5, NODES:2 * NODES], OHB[:, :, c], E[1][:, c, :], start=c == 0, stop=c == EC - 1)
                        mm.then_inc(c34_done, 1)
                    if n == 1:
                        pe.wait_ge(bad_ready, 1)
                        pe.matmul(PS[:, 4, 0:1], ones[0:R34, :], bad[0:R34, 0:1], start=True, stop=True).then_inc(bad_summed, 1)
                        pe.wait_ge(ai_ready, 1)
                        for t in range(NT):
                            for s in range(NT):
                                mm = pe.matmul(PS[:, 5, t:t + 1], AI[:, s, t * P:(t + 1) * P], ones[:, 0:1],
                                               start=s == 0, stop=s == NT - 1)
                        mm.then_inc(deg_summed, 1)
                pe.wait_ge(relu_done, g + 1)
                pe.wait_ge(flag_ready, 1)
                pe.wait_ge(dinv_sd, 1)
                pe.wait_ge(w_used, m0 + 4)
                weights(m0 + 4)
                natural3(hT, W[(m0 + 4) % 2], bank=3, first=True, last=True).then_inc(w_used, 1)
                pe.wait_ge(hg_ready, GATE_B * (g + 1))
                pe.wait_ge(sel_ready, 4)

                def sums(u, c, n):
                    h, i = divmod(c % UB, QUADS)
                    if c >= 2 or g:
                        pe.wait_ge(attn_done, n - 1)
                    if c == QUADS:
                        pe.wait_ge(hg_copied, 16 * (g + 1))
                    for b in range(GATE_B):
                        mm = pe.matmul(PS[:, 2 * (c % 2) + b // 2, (b % 2) * THIRD:(b % 2 + 1) * THIRD], SEL[:, i, :],
                                       QH[h][:, bass.ds(u + c // UB, 1), b, :].rearrange("p a f -> p (a f)"), start=True, stop=True)
                    mm.then_inc(sums_done, 1)

                def reduce(c, n):
                    s, i = divmod(c, UB)
                    pe.wait_ge(prod_done, n + 2)
                    for b in range(GATE_B):
                        mm = pe.matmul(PS[32 * b:32 * b + 32, 6 + s, 0:THIRD], RED[:, i % QUADS, :],
                                       PRD[c % 2][:, b * THIRD:(b + 1) * THIRD], start=i == 0, stop=i == UB - 1)
                    mm.then_inc(red_done, 1)

                with pe.Fori(0, UNITS // 2) as u2:
                    n = lambda c: u2 * (2 * UB) + (g * UNITS * UB + c)
                    for c in range(2 * UB):
                        sums(u2 * 2, c, n(c))
                        if c >= 2:
                            if (c - 2) % UB == 0:
                                pe.wait_ge(qi_copied, u2 * 2 + (g * UNITS + (c - 2) // UB + 1))
                            reduce(c - 2, n(c - 2))
                    for c in (2 * UB - 2, 2 * UB - 1):
                        reduce(c, n(c))
                pe.wait_ge(qi_copied, UNITS * (g + 1) + 2)
                to_turned(0, qiN).then_inc(qi_turned, 1)
                weights(m0 + 5)
                turned_product(3, hT, W[(m0 + 5) % 2], last=False).then_inc(w_used, 1)
                pe.wait_ge(qiT_copied, g + 1)
                weights(m0 + 6)
                turned_product(3, qiT, W[(m0 + 6) % 2], first=False).then_inc(w_used, 1)
                pe.wait_ge(gate_done, g + 1)
                to_natural(0, hT).then_inc(h_turned, 1)

            def turn_x(n):
                pe.wait_ge(ln_done, n)
                to_turned(0, xN).then_inc(x_turned, 1)
                pe.wait_ge(xT_ready, n)

            turn_x(1)
            m = 15
            weights(m)
            natural(4, xT, W[m % 2]).then_inc(w_used, 1)

            def gcn_aggregate(n):
                pe.wait_ge(gcn_scaled, n)
                for t in range(NT):
                    for h in range(2):
                        for s in range(NT):
                            mm = pe.matmul(PS[:, 2 * t + h, 0:HALF], AI[:, s, t * P:(t + 1) * P],
                                           hN[:, s, h * HALF:(h + 1) * HALF], start=s == 0, stop=s == NT - 1)
                mm.then_inc(gcn_sum, 1)

            gcn_aggregate(1)
            for t in range(NT):
                for c in range(R3 * NT):
                    mm = pe.transpose(PS[:, 4 + 2 * t + c // 4, (c % 4) * P:(c % 4 + 1) * P],
                                      CNT[:, c // NT, c % NT, t * P:(t + 1) * P], ident[:])
            mm.then_inc(cn_turned, 1)

            def turn_rows(l, r):
                pe.wait_ge(xr_copied, R3 * l + r + 1)
                for j in range(3 * r, 3 * r + 3):
                    if l * 9 + j >= 2:
                        pe.wait_ge(xrT_copied, l * 9 + j - 1)
                    for kk in range(2):
                        k = (2 * j + kk) % KC
                        for t in range(NT):
                            mm = pe.transpose(PS[:, 6 + j % 2, kk * NODES + t * P:kk * NODES + (t + 1) * P], XR[:, r, t, k::KC],
                                              ident[:])
                    mm.then_inc(xr_turned, 1)

            def queries_keys(l, r, H, qk):
                pe.wait_ge(xrT_copied, 9 * l + 3 * (r + 1))
                for k in range(KC):
                    mm = pe.matmul(PS[0:2 * H, 3 + r // 2, (r % 2) * NODES:(r % 2 + 1) * NODES], qk[:, k, :], XT[:, r, k, :],
                                   start=k == 0, stop=k == KC - 1)
                return mm

            def rows(n, bank):
                for q in range(3):
                    w = 3 * n + q
                    pe.wait_ge(wt_ready, w + 1)
                    for t in range(NT):
                        at = 3 * t + q
                        for i, (k, (a, b)) in enumerate(product(range(KC), ((0, 0), (1, 0), (0, 1)))):
                            mm = pe.matmul(PS[:, bank + at // 2, (at % 2) * THIRD:(at % 2 + 1) * THIRD],
                                           TS[a][:, k, t * P:(t + 1) * P], WT[b][w % 2][:, k, :],
                                           start=i == 0 and at in (0, 3, 4), stop=i == 3 * KC - 1 and q == 2, skip_group_check=True)
                    mm.then_inc(wt_used, 1)

            turn_x(2)
            u0 = 0
            for l, (H, qk) in enumerate(((HEADS1, qk1), (1, qk2))):
                pe.wait_ge(ts_ready, l + 1)
                for r in range(R3):
                    if r == 1:
                        pe.wait_ge(cn_ready, 1)
                    if r == 2:
                        pe.wait_ge(xr_copied, R3 * l + 1)
                    rows(R3 * l + r, 3 * (r % 2))
                    if r:
                        turn_rows(l, r - 1)
                pe.wait_ge(small_in, SMALL)
                for r in range(R3 - 1):
                    queries_keys(l, r, H, qk)
                turn_rows(l, R3 - 1)
                queries_keys(l, R3 - 1, H, qk).then_inc(qk_done, 1)
                pe.wait_ge(qk_copied, l + 1)
                for t in range(NT):
                    for r in range(R3):
                        mm = pe.transpose(PS[:, 0, (t * R3 + r) * 2 * H:(t * R3 + r + 1) * 2 * H],
                                          qkT[0:2 * H, r * NODES + t * P:r * NODES + (t + 1) * P], ident[0:2 * H, 0:2 * H])
                mm.then_inc(qkn_done, 1)

                def spread_keys(h):
                    if h:
                        pe.wait_ge(score_done, u0 + 2 * h)
                    sel = ident[0:2 * H, H + h:H + h + 1].to_broadcast([2 * H, P])
                    pe.matmul(PS[:, 4, :], sel, qkT[0:2 * H, 0:512], start=True, stop=True)
                    pe.matmul(PS[:, 5, 0:256], sel, qkT[0:2 * H, 512:768], start=True, stop=True).then_inc(key_spread, 1)

                def turn_probs(u):
                    pe.wait_ge(p_ready, u + 1)
                    if u > u0:
                        pe.wait_ge(pt_copied, u)
                    for c in range(R3 * NT):
                        mm = pe.transpose(PS[:, 6 + c // 4, (c % 4) * P:(c % 4 + 1) * P], EX[u % 2][:, c * P:(c + 1) * P], ident[:])
                    mm.then_inc(p_turned, 1)

                def weighted_sum(u):
                    h, t = divmod(u - u0, NT)
                    pe.wait_ge(pt_copied, u + 1)
                    if u == u0:
                        pe.wait_ge(qkn_copied, l + 1)
                    width = min(FEAT // H, HALF)
                    for part in range(FEAT // H // width):
                        at = h * (FEAT // H) + part * width
                        for c in range(R3 * NT):
                            mm = pe.matmul(PS[:, 2 * t + at // HALF, at % HALF:at % HALF + width], PT[u % 2][:, c, :],
                                           XR[:, c // NT, c % NT, at:at + width], start=c == 0, stop=c == R3 * NT - 1)
                    mm.then_inc(att_sum, 1)

                spread_keys(0)
                for i in range(2 * H):
                    if i == 0 and H > 1:
                        spread_keys(1)
                    turn_probs(u0 + i)
                    if i % 2 and i // 2 + 2 < H:
                        spread_keys(i // 2 + 2)
                    if i:
                        weighted_sum(u0 + i - 1)
                weighted_sum(u0 + 2 * H - 1)
                u0 += 2 * H
                if l == 0:
                    pe.wait_ge(att_done, 1)
                    to_turned(0, hN).then_inc(h_turned, 1)
                    pe.wait_ge(hN_ready, 2)

            turn_x(3)
            m = FIRST34 - 1
            weights(m)
            pe.wait_ge(ln_done, 3)
            natural3(xT, W[m % 2], first=True).then_inc(w_used, 1)

            def count_pair(p):
                pe.wait_ge(oh_ready, p + 1)
                pe.wait_ge(rc_ready, p + CREDIT)
                for j in range(2):
                    for t in range(NT):
                        for e in range(2):
                            mm = pe.matmul(PS[:, 7, t * NODES + j * P:t * NODES + (j + 1) * P], OS[j][:, e, t * P:(t + 1) * P],
                                           OT[j][:, e, :], start=e == 0, stop=e == 1)
                mm.then_inc(b_done, 1)

            def count_slots(p):
                pe.wait_ge(bb_ready, p + 1)
                for j in range(2):
                    for e in range(2):
                        mm = pe.matmul(PS[:, 7, j:j + 1], OT[j][:, e, :], onesb[:], start=e == 0, stop=e == 1)
                mm.then_inc(c_done, 1)

            def sum_sources(p, i):
                if i == 0:
                    pe.wait_ge(bb_ready, p + 1)
                pe.wait_ge(ms_ready, p * 3 + (CREDIT + (1 if i == 2 else 0)))
                for kk in range(2):
                    k = 2 * i + kk
                    n = 0
                    for t in range(NT):
                        for part in range(2):
                            mm = pe.matmul(PS[:, 5 + i % 2, kk * NODES:(kk + 1) * NODES], XS[part][:, t, k::KC],
                                           BB[:, t * NODES:(t + 1) * NODES], start=n == 0, stop=n == 3)
                            n += 1
                mm.then_inc(msum_done, 1)

            def third_product(p, s, mb):
                j, q = divmod(s, 3)
                if s == 0:
                    pe.wait_ge(ms_ready, p * 3 + (CREDIT + 3))
                if q < 2:
                    pe.wait_ge(w_lo, p * 4 + (2 * j + q + 1))
                else:
                    pe.wait_ge(w_used, p * 2 + (FIRST34 + j + 1))
                pe.wait_ge(y_ready, p * 6 + (s - 1 + CREDIT))
                n = 0
                for k in range(KC):
                    for a, b in ((0, 0), (1, 0), (0, 1)):
                        mm = pe.matmul(PS[:, 3 + s % 2, 0:THIRD], MS[a][mb][:, k, j * P:(j + 1) * P], WS[b][q][:, k, :],
                                       start=n == 0, stop=n == 17)
                        n += 1
                mm.then_inc(y_done, 1)

            def scatter(p, s, last=False):
                j, q = divmod(s, 3)
                pe.wait_ge(y_ready, p * 6 + (s + 1 + CREDIT))
                if q == 0:
                    pe.wait_ge(ct_ready, p * 2 + (j + 1))
                for t in range(NT):
                    at = 3 * t + q
                    for part in range(2):
                        mm = pe.matmul(PS[:, at // 2, (at % 2) * THIRD:(at % 2 + 1) * THIRD], CT[j][:, t * P:(t + 1) * P],
                                       YS[part][s % 2][:], start=False, stop=last and part == 1, skip_group_check=True)
                return mm.then_inc(enc_done if last else scat_done, 1)

            def pair(p, mb, first=False, nxt=True):
                for s in range(6):
                    third_product(p, s, mb)
                    if s:
                        scatter(p, s - 1)
                    elif not first:
                        scatter(p - 1, 5)
                    if nxt and s == 1:
                        count_pair(p + 1)
                    if nxt and s == 2:
                        count_slots(p + 1)
                    if nxt and 2 <= s < 5:
                        sum_sources(p + 1, s - 2)
                if not nxt:
                    scatter(p, 5, last=True)

            overflow = pe.value_load(flag[0:1, 0:1])
            with pe.If(overflow < 1):
                for x in (c_done, y_done, scat_done):
                    pe.sem_inc(x, CREDIT)
                pe.wait_ge(xs_ready, 1)
                count_pair(0)
                count_slots(0)
                for i in range(3):
                    sum_sources(0, i)
                pair(0, 0, first=True)
                with pe.Fori(0, (PAIRS34 - 3) // 2) as i:
                    pair(i * 2 + 1, 1)
                    pair(i * 2 + 2, 0)
                pair(PAIRS34 - 2, 1)
                pair(PAIRS34 - 1, 0, nxt=False)
            with pe.Else():
                pe.wait_ge(s1_ready, 2)
                counts(R3, 1, S1=S1L)
                spread_counts(R3, A34[0])

                def relation(r, j, nxt=True, last=False):
                    if nxt:
                        counts(r + (R3 + 1), j % 2, S1=S1L)
                    pe.wait_ge(nrm_ready, r + (R3 + 1))
                    aggregate(r + 2 * R3, xN, N34[j])
                    if nxt:
                        spread_counts(r + (R3 + 1), A34[1 - j])
                    pe.wait_ge(mt_copied, (r + (2 * R3 + 1)) * 3)
                    slot = (FIRST34 + j) % 2
                    pe.wait_ge(w_in[slot], (r - j) * 8 + 16 * ((FIRST34 + j) // 2 + 1))
                    mm = natural3(MT[j], W[slot], last=last)
                    mm.then_inc(w_used, 1)
                    return mm

                with pe.Fori(0, LOOP34) as i:
                    for j in range(2):
                        relation(i * 2 + j, j)
                relation(R34 - 2, 0)
                relation(R34 - 1, 1, nxt=False, last=True)
                pe.wait_ge(w_used, FIRST34 + R34)
                pe.sem_inc(enc_done, 1)
            pe.wait_ge(h1_copied, 1)
            to_turned(4, hN).then_inc(h_turned, 1)
            pe.wait_ge(hN_ready, 3)
            m = FIRST34 + R34
            weights(m)
            natural(4, hT, W[m % 2]).then_inc(w_used, 1)
            gcn_aggregate(2)

        @block.scalar
        def _(act):
            def turned_out(bank):
                return PS[:, bank:bank + 3, :].rearrange("p b (k n) -> p (b k) n", k=2)

            def counts_copy(n, cnt, bank=4):
                act.wait_ge(cnt_summed, n + 1)
                nc.scalar.copy(cnt, PS[:, bank, :].rearrange("p (s n) -> p s n", s=NT)).then_inc(cnt_copied, 1)

            def mt_copy(n, buf):
                for j in range(3):
                    act.wait_ge(agg_done, n * 3 + (j + 1))
                    nc.scalar.copy(MT[buf][:, 2 * j:2 * j + 2, :], PS[:, 6 + j % 2, :].rearrange("p (k n) -> p k n", k=2)
                                   ).then_inc(mt_copied, 1)

            for r in range(R3):
                if r:
                    t = r - 1
                    act.wait_ge(q_done if t == 0 else w_used, 1)
                    for j, h in product(range(2), range(2)):
                        nc.scalar.copy(query_rows(0, t, j, h), query_sums(t, j, h)).then_inc(qg_hi, 1)
                counts_copy(r, CNT[:, r], bank=6)
            def third_hi_turned(w):
                m = 8 + w // 3
                if w % 3 == 0:
                    act.wait_ge(w_in[m % 2], 16 * (m // 2 + 1))
                if w >= 2:
                    act.wait_ge(wl_used, w - 1)
                nc.scalar.copy(WL[0][w % 2][:], third_turned(W[m % 2], w % 3)).then_inc(wl_hi, 1)

            for g in range(2):
                if g:
                    act.wait_ge(gate_done, 1)
                    nc.scalar.copy(TS[0][:], hT[:]).then_inc(hs_hi, 1)
                    third_hi_turned(0)
                    third_hi_turned(1)
                    for p in range(R3 + 1):
                        for w in range(3 * p + 2, 3 * p + 4):
                            if w < 3 * (R3 + 1):
                                third_hi_turned(w)
                        for j in range(3):
                            if p < R3:
                                act.wait_ge(agg_done, (R3 + p) * 3 + j + 1)
                                nc.scalar.copy(TS[0][:, 2 * j:2 * j + 2, :], PS[:, 6 + j % 2, :].rearrange("p (k n) -> p k n", k=2)
                                               ).then_inc(mt_hi, 1)
                        if p < R3:
                            third_hi_turned(3 * p + 4)
                    act.wait_ge(wl_used, 3 * (R3 + 1))
                for r in range(R3 if g == 0 else 0):
                    n = g * R3 + r
                    if r >= 2:
                        act.wait_ge(w_used, 1 + 7 * g + 1 + (r - 1))
                    mt_copy(n, n % 2)
                    if n == 1:
                        act.wait_ge(deg_summed, 1)
                        nc.scalar.activation(dinv[:], PS[:, 5, 0:NT], ACT.Sqrt).then_inc(dinv_sd, 1)
                if g == 0:
                    act.wait_ge(small_in, SMALL)
                if g == 0:
                    act.wait_ge(w_used, 5)
                for m in range(KC):
                    ins = nc.scalar.activation(hT[:, m, :], PS[:, m // 2, (m % 2) * NODES:(m % 2 + 1) * NODES], ACT.Relu,
                                               bias=biasT[:, g, m:m + 1])
                ins.then_inc(relu_done, 1)
                act.wait_ge(w_used, 7 * g + 6)
                for b in range(GATE_B):
                    nc.scalar.copy(node_rows(0, b), tiles3(3)[32 * b:32 * b + 32]).then_inc(hg_hi, 1)
                with act.Fori(0, UNITS // 2) as u2:
                    for c in range(2 * UB):
                        n = u2 * (2 * UB) + (g * UNITS * UB + c)
                        act.wait_ge(sums_done, n + 1)
                        act.wait_ge(prod_done, n if c or g else u2 * (2 * UB) + 1)
                        nc.scalar.activation(SIG[c % 2], PS[:, 2 * (c % 2):2 * (c % 2) + 2, :].rearrange("p b n -> p (b n)"),
                                             ACT.Sigmoid).then_inc(attn_done, 1)
                act.wait_ge(qiT_copied, g + 1)
                nc.scalar.activation(tanhT, turned_out(0), ACT.Tanh).then_inc(tanh_done, 1)
                act.wait_ge(w_used, 7 * g + 8)
                for m in range(KC):
                    ins = nc.scalar.activation(alphaT[:, m, :], PS[:, 3 + m // 2, (m % 2) * NODES:(m % 2 + 1) * NODES],
                                               ACT.Sigmoid, bias=biasT[:, 2, m:m + 1])
                ins.then_inc(alpha_done, 1)

            def norm_x(n):
                act.wait_ge(var_ready, n)
                nc.scalar.activation(sd[:], mv[:, :, 1], ACT.Sqrt, bias=eps[:, 0:1]).then_inc(sd_ready, 1)

            def turn_x(n):
                act.wait_ge(x_turned, n)
                nc.scalar.copy(xT[:], turned_out(0)).then_inc(xT_ready, 1)

            def scale_rows(n):
                act.wait_ge(w_used, 16 if n == 1 else FIRST34 + R34 + 1)
                if n == 1:
                    act.wait_ge(dinv_ready, 1)
                for t in range(NT):
                    ins = nc.scalar.activation(hN[:, t, :].rearrange("p (h f) -> p h f", h=2), PS[:, 4 + 2 * t:6 + 2 * t, 0:HALF],
                                               ACT.Copy, scale=dinv[:, t:t + 1])
                ins.then_inc(gcn_scaled, 1)

            norm_x(1)
            turn_x(1)
            def third_hi(w):
                n, q = divmod(w, 3)
                m = 16 + n
                if q == 0:
                    act.wait_ge(w_in[m % 2], 16 * (m // 2 + 1))
                if w >= 2:
                    act.wait_ge(wt_used, w - 1)
                nc.scalar.copy(WT[0][w % 2][:], W[m % 2][:, :, q * THIRD:(q + 1) * THIRD]).then_inc(wt_hi, 1)

            scale_rows(1)
            act.wait_ge(cn_turned, 1)
            third_hi(0)
            third_hi(1)
            norm_x(2)
            act.wait_ge(x_turned, 2)
            nc.scalar.copy(TS[0][:], turned_out(0)).then_inc(xT_ready, 1)
            u0 = 0
            for l, H in enumerate((HEADS1, 1)):
                for r in range(R3):
                    for w in range(9 * l + 3 * r, 9 * l + 3 * r + 3):
                        if w + 2 < 18:
                            third_hi(w + 2)
                    act.wait_ge(wt_used, 3 * (l * R3 + r + 1))
                    nc.scalar.copy(XR[:, r].rearrange("p t f -> p (t f)"),
                                   PS[:, 3 * (r % 2):3 * (r % 2) + 3, :].rearrange("p b n -> p (b n)")).then_inc(xr_copied, 1)
                act.wait_ge(qkn_copied, l + 1)

                def scores(u):
                    h, t = divmod(u - u0, NT)
                    act.wait_ge(key_spread, u0 // 2 + h + 1)
                    if u >= 2:
                        act.wait_ge(exp_done, u - 1)
                    for r in range(R3):
                        ins = nc.scalar.activation(SC[u % 2][:, r * NODES:(r + 1) * NODES],
                                                   PS[:, 4 + r // 2, (r % 2) * NODES:(r % 2 + 1) * NODES], ACT.Identity,
                                                   bias=qkN[:, t, r, h:h + 1])
                    ins.then_inc(score_done, 1)

                scores(u0)
                for u in range(u0, u0 + 2 * H):
                    if u + 1 < u0 + 2 * H:
                        scores(u + 1)
                    act.wait_ge(max_ready, u + 1)
                    if u >= 2:
                        act.wait_ge(p_turned, u - 1)
                    nc.scalar.activation(EX[u % 2], SC[u % 2], ACT.Exp, bias=nmax[:, u % 8:u % 8 + 1]).then_inc(exp_done, 1)
                u0 += 2 * H
                if l == 0:
                    act.wait_ge(elu_min, 1)
                    nc.scalar.activation(xT[:], MT[0][:], ACT.Exp).then_inc(elu_exp, 1)
                    act.wait_ge(h_turned, 3)
                    nc.scalar.copy(TS[0][:], turned_out(0)).then_inc(hN_ready, 1)
            norm_x(3)
            turn_x(3)

            def weight_hi(p, s):
                if s >= 6:
                    p, s = p + 1, s - 6
                j, q = divmod(s, 3)
                slot = (FIRST34 + j) % 2
                if q == 0:
                    act.wait_ge(w_in[slot], p * 16 + 16 * ((FIRST34 + j) // 2 + 1))
                act.wait_ge(y_done, p * 6 + (s - 2 + CREDIT))
                nc.scalar.copy(WS[0][q][:], W[slot][:, :, q * THIRD:(q + 1) * THIRD]).then_inc(w_hi, 1)

            def counts_hi(p):
                act.wait_ge(b_done, p + 1)
                if not isinstance(p, int) or p:
                    act.wait_ge(msum_done, p * 3)
                nc.scalar.copy(BB[:], PS[:, 7, :]).then_inc(bb_ready, 1)

            def sums_hi(p, i, mb):
                act.wait_ge(msum_done, p * 3 + (i + 1))
                if i == 0:
                    act.wait_ge(y_done, p * 6 + (CREDIT - 6))
                nc.scalar.copy(MS[0][mb][:, 2 * i:2 * i + 2, :], PS[:, 5 + i % 2, :].rearrange("p (k n) -> p k n", k=2)
                               ).then_inc(ms_hi, 1)

            def rows_hi(p, s, mb):
                if s == 0:
                    act.wait_ge(rc_ready, p + (1 + CREDIT))
                act.wait_ge(y_done, p * 6 + (s + 1 + CREDIT))
                act.wait_ge(scat_done, p * 6 + (s - 1 + CREDIT))
                nc.scalar.activation(YS[0][s % 2][:], PS[:, 3 + s % 2, 0:THIRD], ACT.Copy, scale=rcs[:, mb, s // 3:s // 3 + 1]
                                     ).then_inc(y_hi, 1)

            def pair(p, mb, first=False, nxt=True):
                for s in range(6):
                    if s:
                        rows_hi(p, s - 1, mb)
                    elif not first:
                        rows_hi(p - 1, 5, 1 - mb)
                    if nxt and s == 2:
                        counts_hi(p + 1)
                    if nxt and s == 5:
                        sums_hi(p + 1, 2, 1 - mb)
                    if nxt or s + 2 < 6:
                        weight_hi(p, s + 2)
                    if nxt and 3 <= s < 5:
                        sums_hi(p + 1, s - 3, 1 - mb)
                if not nxt:
                    rows_hi(p, 5, mb)

            act.wait_ge(flag_ready, 1)
            overflow = act.value_load(flag[0:1, 0:1])
            with act.If(overflow < 1):
                nc.scalar.copy(XS[0][:], xN[:]).then_inc(xs_hi, 1)
                weight_hi(0, 0)
                weight_hi(0, 1)
                counts_hi(0)
                for i in range(3):
                    sums_hi(0, i, 0)
                pair(0, 0, first=True)
                with act.Fori(0, (PAIRS34 - 3) // 2) as i:
                    pair(i * 2 + 1, 1)
                    pair(i * 2 + 2, 0)
                pair(PAIRS34 - 2, 1)
                pair(PAIRS34 - 1, 0, nxt=False)
            with act.Else():
                counts_copy(R3, A34[0])

                def relation(r, j, nxt=True):
                    if nxt:
                        act.wait_ge(nrm_ready, r + R3)
                        counts_copy(r + (R3 + 1), A34[1 - j])
                    act.wait_ge(w_used, r + (FIRST34 - 1))
                    mt_copy(r + 2 * R3, j)

                with act.Fori(0, LOOP34) as i:
                    for j in range(2):
                        relation(i * 2 + j, j)
                relation(R34 - 2, 0)
                relation(R34 - 1, 1, nxt=False)
            act.wait_ge(h_turned, 4)
            nc.scalar.copy(hT[:], turned_out(4)).then_inc(hN_ready, 1)
            scale_rows(2)
            norm_x(4)

        @block.vector
        def _(dve):
            steps = [0]

            def then(ins):
                steps[0] += 1
                ins.then_inc(dve_step, 1)
                dve.wait_ge(dve_step, steps[0])

            V = nc.vector
            dve.sem_inc(prod_done, 1)
            dve.sem_inc(qi_copied, 2)

            def onehot(out, key):
                for c in range(EC):
                    ins = V.tensor_scalar(out[:, c, :], iotab[:], key[:, c:c + 1], None, ALU.is_equal)
                return ins

            then(V.memset(eps[:], 1e-5))
            dve.wait_ge(keys_in, 64)
            then(V.tensor_copy(keyf[:], keys[:]))
            then(V.tensor_scalar(keyf[:, 0:2, :], keyf[:, 0:2, :], 1.0, None, ALU.add))
            dve.wait_ge(consts, 1)
            onehot(S1[:], keyf[:, 0, :]).then_inc(s1_ready, 1)
            for r in range(R3 + 1):
                if r < R3:
                    then(V.scalar_tensor_tensor(out=ekey[:, r % 2, :], in0=keyf[:, 2, :], scalar=float(r), in1=keyf[:, 1, :],
                                                op0=ALU.is_equal, op1=ALU.mult))
                    if r == 2:
                        dve.wait_ge(cnt_summed, 1)
                    onehot(E[r % 2], ekey[:, r % 2, :]).then_inc(e_ready, 1)
                if r >= 1:
                    n = r - 1
                    if n != 1:
                        t = n // 2
                        for j, h in product(range(2), range(2)):
                            dve.wait_ge(qg_hi, 4 * t + 2 * j + h + 1)
                            V.tensor_tensor(query_rows(1, t, j, h), query_sums(t, j, h), query_rows(0, t, j, h).bitcast(F32),
                                            ALU.subtract).then_inc(qg_ready, 1)
                    dve.wait_ge(deg_spread, n + 1)
                    then(V.tensor_scalar(RC[:, 0, :], PS[:, 7, 0:NODES], 1.0, None, ALU.max))
                    then(V.reciprocal(RC[:, 1, :], RC[:, 0, :]))
                    V.tensor_tensor(NRM[:, n], CNT[:, n], RC[:, 1, :].unsqueeze(1).to_broadcast([P, NT, NODES]), ALU.mult
                                    ).then_inc(nrm_ready, 1)
            then(V.tensor_tensor(AI[:], CNT[:, 0], CNT[:, 1], ALU.add))
            then(V.tensor_tensor(AI[:], AI[:], CNT[:, 2], ALU.add))
            dve.wait_ge(consts, 2)
            for s in range(NT):
                ins = V.tensor_tensor(AI[:, s, s * P:(s + 1) * P], AI[:, s, s * P:(s + 1) * P], ident[:], ALU.add)
            ins.then_inc(ai_ready, 1)

            dve.wait_ge(cnt_summed, R3)
            onehot(E[1], keyf[:, 1, :]).then_inc(d1_ready, 1)
            rel = keyf[:, 3, :]
            then(V.tensor_tensor(OH, relid[:].unsqueeze(2).to_broadcast([P, R34, EC]), rel.unsqueeze(1).to_broadcast([P, R34, EC]),
                                 ALU.is_equal))
            V.tensor_copy(OHB, OH)
            then(V.memset(KEEP, 1.0))
            then(V.memset(KEEP.rearrange("p (r c) -> p r c", r=R34)[:, :, 0:1], 0.0))
            V.tensor_tensor_scan(RUN, KEEP, OH.rearrange("p r c -> p (r c)"), 0.0, ALU.mult, ALU.add).then_inc(run_ready, 1)
            dve.wait_ge(run_ready, 1)
            dve.wait_ge(offs_done, 1)
            then(V.tensor_copy(offs[:], PS[:, 4, 0:R34]))
            RV = RUN.rearrange("p (r c) -> p r c", r=R34)
            then(V.tensor_tensor(RV, RV, offs[:].unsqueeze(2).to_broadcast([P, R34, EC]), ALU.add))
            then(V.tensor_tensor(RV, RV, OH, ALU.mult))
            then(V.tensor_reduce(t34f[:, 0, :], RV.rearrange("p r c -> p c r"), AX.X, ALU.add))
            then(V.tensor_scalar(t34f[:, 0, :], t34f[:, 0, :], -1.0, None, ALU.add))
            then(V.tensor_scalar(t34f[:, 1, :], t34f[:, 0, :], float(P), float(1 - 2 * R34 * P), ALU.is_ge, ALU.mult))
            then(V.scalar_tensor_tensor(out=t34f[:, 1, :], in0=t34f[:, 0, :], scalar=float(2 * R34), in1=t34f[:, 1, :],
                                        op0=ALU.mult, op1=ALU.add))
            then(V.scalar_tensor_tensor(out=t34f[:, 1, :], in0=rel, scalar=2.0, in1=t34f[:, 1, :], op0=ALU.mult, op1=ALU.add))
            then(V.tensor_tensor(t34f[:, 2, :], spare[:], t34f[:, 1, :], ALU.subtract))
            then(V.scalar_tensor_tensor(out=t34f[:, 2, :], in0=t34f[:, 0, :], scalar=float(CAP), in1=t34f[:, 2, :],
                                        op0=ALU.is_ge, op1=ALU.mult))
            then(V.tensor_tensor(POS[:], t34f[:, 1, :], t34f[:, 2, :], ALU.add))
            then(V.scalar_tensor_tensor(out=t34f[:, 2, :], in0=rel, scalar=float(NODES), in1=keyf[:, 1, :], op0=ALU.mult, op1=ALU.add))
            then(V.tensor_scalar(GIX[:], t34f[:, 2, :], -1.0, None, ALU.add))
            V.tensor_copy(PAY[:, :, 0], keyf[:, 0, :]).then_inc(idx_ready, 1)
            dve.wait_ge(c34_done, 1)
            sv = SEL[:].rearrange("p i (j l) -> p (i j) l", j=4)
            for i in range(4):
                rows = slice(32 * i, 32 * i + 32)
                V.tensor_copy(sv[rows], ident[rows, rows].unsqueeze(1 if i < 2 else 2).to_broadcast([32, BN, HQ])
                              ).then_inc(sel_ready, 1)
            dve.wait_ge(c34_done, 1)
            C34 = PS[0:R34, 5, NODES:2 * NODES]
            V.tensor_reduce(bad[0:R34, 1:2], C34, AX.X, ALU.add)
            then(V.tensor_scalar(PRES, C34, 0.5, None, ALU.is_gt))
            then(V.tensor_tensor_scan(INCL, ones[0:R34, 0:1].to_broadcast([R34, NODES]), PRES, 0.0, ALU.mult, ALU.add))
            then(V.tensor_tensor(SLOT1, INCL, PRES, ALU.mult))
            V.tensor_copy(SLOTB, SLOT1).then_inc(slots_ready, 1)
            then(V.tensor_scalar(bad[0:R34, 0:1], INCL[:, NODES - 1:NODES], float(P), None, ALU.is_gt))
            V.scalar_tensor_tensor(out=bad[0:R34, 0:1], in0=bad[0:R34, 1:2], scalar=float(CAP), in1=bad[0:R34, 0:1],
                                   op0=ALU.is_gt, op1=ALU.add).then_inc(bad_ready, 1)
            dve.wait_ge(bad_summed, 1)
            V.tensor_copy(flag[:], PS[:, 4, 0:1]).then_inc(flag_ready, 1)
            dve.wait_ge(dinv_sd, 1)
            V.reciprocal(dinv[:], dinv[:]).then_inc(dinv_ready, 1)

            def third_lo_turned(w):
                dve.wait_ge(wl_hi, w + 1)
                V.tensor_tensor(WL[1][w % 2][:], third_turned(W[(8 + w // 3) % 2], w % 3), WL[0][w % 2][:].bitcast(F32),
                                ALU.subtract).then_inc(wl_ready, 1)
                if w % 3 == 2:
                    dve.wait_ge(wl_ready, w + 1)
                    dve.sem_inc(w_used, 1)

            for g in range(2):
                for b in range(GATE_B):
                    dve.wait_ge(hg_hi, GATE_B * g + b + 1)
                    V.tensor_tensor(node_rows(1, b), tiles3(3)[32 * b:32 * b + 32], node_rows(0, b).bitcast(F32),
                                    ALU.subtract).then_inc(hg_ready, 1)
                dve.wait_ge(tab_out, 32)
                qiU = qiN[:].rearrange("p t (q f) -> p (t q) f", q=3)

                with dve.Fori(0, UNITS // 2) as u2:
                    n0 = u2 * (2 * UB) + g * UNITS * UB

                    def copy_sum(s):
                        dve.wait_ge(red_done, n0 + (UB * (s + 1) + 1))
                        V.tensor_copy(qiU[:, bass.ds(u2 * 2 + s, 1), :].rearrange("p a f -> p (a f)"), PS[:, 6 + s, 0:THIRD]
                                      ).then_inc(qi_copied, 1)

                    for c in range(2 * UB):
                        s, (h, i) = c // UB, divmod(c % UB, QUADS)
                        if i == 0:
                            dve.wait_ge(qd_in[h], u2 * 128 + 64 * (g * UNITS + s + 1))
                        dve.wait_ge(attn_done, n0 + (c + 1))
                        dve.wait_ge(red_done, n0 + c if c or g else u2 * (2 * UB) + 1)
                        V.tensor_tensor(PRD[i % 2], SIG[i % 2], QD[h], ALU.mult).then_inc(prod_done, 1)
                        if c == UB + 3:
                            copy_sum(0)
                    copy_sum(1)
                dve.wait_ge(qi_turned, g + 1)
                V.tensor_copy(qiT, PS[:, 0:3, :].rearrange("p b (k n) -> p (b k) n", k=2)).then_inc(qiT_copied, 1)
                dve.wait_ge(tanh_done, g + 1)
                then(V.tensor_tensor(tanhT, tanhT, hT[:], ALU.subtract))
                dve.wait_ge(alpha_done, g + 1)
                then(V.tensor_tensor(tanhT, tanhT, alphaT, ALU.mult))
                V.tensor_tensor(hT[:], hT[:], tanhT, ALU.add).then_inc(gate_done, 1)
                if g == 0:
                    dve.wait_ge(hs_hi, 1)
                    V.tensor_tensor(TS[1][:], hT[:], TS[0][:].bitcast(F32), ALU.subtract).then_inc(hs_ready, 1)
                dve.wait_ge(h_turned, g + 1)
                for t in range(NT):
                    ps = PS[:, 2 * t:2 * t + 2, :].rearrange("p b n -> p (b n)")[:, 0:FEAT].rearrange("p (k n) -> p k n", k=KC)
                    if g == 0:
                        ins = V.tensor_copy(hN[:, t, :].rearrange("p (n k) -> p k n", k=KC), ps)
                    else:
                        xv = xN[:, t, :].rearrange("p (n k) -> p k n", k=KC)
                        ins = V.tensor_tensor(xv, ps, xv, ALU.add)
                if g == 0:
                    ins.then_inc(hN_ready, 1)
                    third_lo_turned(0)
                    third_lo_turned(1)
                    for p in range(R3 + 1):
                        for w in range(3 * p + 2, 3 * p + 4):
                            if w < 3 * (R3 + 1):
                                third_lo_turned(w)
                        for j in range(3):
                            if p < R3:
                                dve.wait_ge(mt_hi, 3 * p + j + 1)
                                V.tensor_tensor(TS[1][:, 2 * j:2 * j + 2, :], PS[:, 6 + j % 2, :].rearrange("p (k n) -> p k n", k=2),
                                                TS[0][:, 2 * j:2 * j + 2, :].bitcast(F32), ALU.subtract).then_inc(mt_copied, 1)
                        if p < R3:
                            third_lo_turned(3 * p + 4)
                else:
                    then(ins)

            def layer_norm(n):
                for t in range(NT):
                    for h in range(2):
                        ins = V.bn_stats(stats[:, t, h, :], xN[:, t, h * HALF:(h + 1) * HALF])
                then(ins)
                for t in range(NT):
                    ins = V.bn_aggr(mv[:, t, :], stats[:, t, :, :])
                ins.then_inc(var_ready, 1)
                dve.wait_ge(sd_ready, n)
                then(V.reciprocal(rstd[:], sd[:]))
                for t in range(NT):
                    ins = V.tensor_scalar(xN[:, t, :], xN[:, t, :], mv[:, t, 0:1], rstd[:, t:t + 1], ALU.subtract, ALU.mult)
                ins.then_inc(ln_done, 1)
                dve.wait_ge(ln_done, n)

            def gcn_out(n, bias):
                then(V.tensor_tensor(xN[:], xN[:], biasN[:, bias, :].unsqueeze(1).to_broadcast([P, NT, FEAT]), ALU.add))
                dve.wait_ge(gcn_sum, n)
                for t in range(NT):
                    xv = xN[:, t, :].rearrange("p (h f) -> p h f", h=2)
                    ins = V.scalar_tensor_tensor(out=xv, in0=PS[:, 2 * t:2 * t + 2, 0:HALF], scalar=dinv[:, t:t + 1], in1=xv,
                                                 op0=ALU.mult, op1=ALU.add)
                then(ins)

            layer_norm(1)
            dve.wait_ge(x_turned, 1)
            gcn_out(1, 1)
            layer_norm(2)

            def third_lo(w):
                n, q = divmod(w, 3)
                dve.wait_ge(wt_hi, w + 1)
                V.tensor_tensor(WT[1][w % 2][:], W[n % 2][:, :, q * THIRD:(q + 1) * THIRD], WT[0][w % 2][:].bitcast(F32),
                                ALU.subtract).then_inc(wt_ready, 1)
                if q == 2:
                    dve.wait_ge(wt_ready, w + 1)
                    dve.sem_inc(w_used, 1)

            def rows_lo_turned(l):
                dve.wait_ge(*((xT_ready, 2) if l == 0 else (hN_ready, 2)))
                V.tensor_tensor(TS[1][:], PS[:, 0:3, :].rearrange("p b (k n) -> p (b k) n", k=2), TS[0][:].bitcast(F32),
                                ALU.subtract).then_inc(ts_ready, 1)

            third_lo(0)
            rows_lo_turned(0)
            third_lo(1)
            dve.wait_ge(cn_turned, 1)
            for t in range(NT):
                ins = V.tensor_copy(CN[:, t, :], PS[:, 4 + 2 * t:6 + 2 * t, :].rearrange("p b n -> p (b n)")[:, 0:FEAT])
            then(ins)
            V.tensor_scalar(NM, CN, 0.5, MASKED, ALU.is_lt, ALU.mult).then_inc(cn_ready, 1)
            dve.wait_ge(cn_ready, 1)

            u0 = 0
            for l, (H, bias) in enumerate(((HEADS1, 2), (1, 3))):
                if l == 1:
                    rows_lo_turned(1)
                order = [2, 3, 4, 5, 6, 7, "r0", 8, 9, "r1", 10, "r2"]
                for x in order:
                    if isinstance(x, int):
                        if 9 * l + x < 18:
                            third_lo(9 * l + x)
                        continue
                    r = int(x[1])
                    for j in range(3 * r, 3 * r + 3):
                        k = 2 * j % KC
                        dve.wait_ge(xr_turned, l * 9 + j + 1)
                        V.tensor_copy(XT[:, r, k:k + 2, :], PS[:, 6 + j % 2, :].rearrange("p (k n) -> p k n", k=2)
                                      ).then_inc(xrT_copied, 1)
                dve.wait_ge(qk_done, l + 1)
                V.tensor_copy(qkT[0:2 * H, :], PS[0:2 * H, 3:5, :].rearrange("p b n -> p (b n)")[:, 0:R3 * NODES]).then_inc(qk_copied, 1)
                dve.wait_ge(qkn_done, l + 1)
                V.tensor_copy(qkN[:, :, :, 0:2 * H], PS[:, 0, 0:NT * R3 * 2 * H].rearrange("p (t r h) -> p t r h", t=NT, r=R3)
                              ).then_inc(qkn_copied, 1)

                def row_max(u):
                    c = u % 8
                    dve.wait_ge(score_done, u + 1)
                    then(V.scalar_tensor_tensor(out=SC[u % 2], in0=SC[u % 2], scalar=SLOPE, in1=SC[u % 2],
                                                op0=ALU.mult, op1=ALU.max))
                    then(V.tensor_tensor_reduce(SC[u % 2], SC[u % 2], NM[:, (u - u0) % NT, :], 1.0, -3e38, ALU.add, ALU.max,
                                                rmax[:, c:c + 1]))
                    V.tensor_scalar(nmax[:, c:c + 1], rmax[:, c:c + 1], -1.0, None, ALU.mult).then_inc(max_ready, 1)

                def turned_probs(u):
                    dve.wait_ge(p_turned, u + 1)
                    V.tensor_copy(PT[u % 2], PS[:, 6:8, :].rearrange("p b (c n) -> p (b c) n", c=4)[:, 0:R3 * NT, :]
                                  ).then_inc(pt_copied, 1)

                row_max(u0)
                for u in range(u0, u0 + 2 * H):
                    if u + 1 < u0 + 2 * H:
                        row_max(u + 1)
                    if u > u0:
                        turned_probs(u - 1)
                    c = u % 8
                    dve.wait_ge(exp_done, u + 1)
                    V.tensor_tensor_reduce(EX[u % 2], EX[u % 2], CN[:, (u - u0) % NT, :], 1.0, 0.0, ALU.mult, ALU.add,
                                           zsum[:, c:c + 1]).then_inc(p_ready, 1)
                    dve.wait_ge(p_ready, u + 1)
                    then(V.tensor_scalar(zinv[:, c:c + 1], zsum[:, c:c + 1], 1e-16, None, ALU.add))
                    then(V.reciprocal(zinv[:, c:c + 1], zinv[:, c:c + 1]))
                turned_probs(u0 + 2 * H - 1)
                dve.wait_ge(att_sum, u0 + 2 * H)
                if l == 1:
                    then(V.tensor_tensor(xN[:], xN[:], biasN[:, bias, :].unsqueeze(1).to_broadcast([P, NT, FEAT]), ALU.add))
                width = min(FEAT // H, HALF)
                for h in range(H):
                    for t in range(NT):
                        c = (u0 + 2 * h + t) % 8
                        for part in range(FEAT // H // width):
                            at = h * (FEAT // H) + part * width
                            other = biasN[:, bias, at:at + width] if l == 0 else xN[:, t, at:at + width]
                            dest = hN if l == 0 else xN
                            ins = V.scalar_tensor_tensor(out=dest[:, t, at:at + width],
                                                         in0=PS[:, 2 * t + at // HALF, at % HALF:at % HALF + width],
                                                         scalar=zinv[:, c:c + 1], in1=other, op0=ALU.mult, op1=ALU.add)
                then(ins)
                u0 += 2 * H
                if l == 0:
                    flat = lambda a: a.rearrange("p a b -> p (a b)")
                    V.tensor_scalar(flat(MT[0][:]), flat(hN[:]), 0.0, None, ALU.min).then_inc(elu_min, 1)
                    then(V.tensor_scalar(hN[:], hN[:], 0.0, -1.0, ALU.max, ALU.add))
                    dve.wait_ge(elu_exp, 1)
                    V.tensor_tensor(flat(hN[:]), flat(hN[:]), flat(xT[:]), ALU.add).then_inc(att_done, 1)
                    dve.wait_ge(att_done, 1)
            layer_norm(3)
            dve.wait_ge(x_turned, 3)

            def weight_lo(p, s):
                if s >= 6:
                    p, s = p + 1, s - 6
                j, q = divmod(s, 3)
                dve.wait_ge(w_hi, p * 6 + (s + 1))
                V.tensor_tensor(WS[1][q][:], W[(FIRST34 + j) % 2][:, :, q * THIRD:(q + 1) * THIRD], WS[0][q][:].bitcast(F32),
                                ALU.subtract).then_inc(w_lo if q < 2 else w_used, 1)

            def pair_onehots(p, js=range(2)):
                dve.wait_ge(c_done, p + CREDIT)
                for j in js:
                    V.tensor_tensor(OS[j][:], iota1[:].unsqueeze(1).to_broadcast([P, 2, NODES]),
                                    KS[:, bass.ds(p * 4 + 2 * j, 2), 0:1].to_broadcast([P, 2, NODES]), ALU.is_equal)
                    ins = V.tensor_tensor(OT[j][:], iota1[:, 0:P].unsqueeze(1).to_broadcast([P, 2, P]),
                                          KS[:, bass.ds(p * 4 + 2 * j, 2), 1:2].to_broadcast([P, 2, P]), ALU.is_equal)
                if j == 1:
                    ins.then_inc(oh_ready, 1)

            def slot_onehots(p, j):
                dve.wait_ge(scat_done, p * 6 + (3 * j - 3 + CREDIT))
                V.tensor_scalar(CT[j][:], SLB[:, bass.ds(p * (2 * NODES) + j * NODES, NODES)], pidx1[:, 0:1], None, ALU.is_equal
                                ).then_inc(ct_ready, 1)

            def count_inverse(p, mb):
                dve.wait_ge(c_done, p + (1 + CREDIT))
                V.tensor_scalar(rcm[:], PS[:, 7, 0:2], 1.0, None, ALU.max).then_inc(rc_max, 1)
                dve.wait_ge(rc_max, p + 1)
                V.reciprocal(rcs[:, mb, :], rcm[:]).then_inc(rc_ready, 1)

            def sums_lo(p, i, mb):
                dve.wait_ge(ms_hi, p * 3 + (i + 1))
                V.tensor_tensor(MS[1][mb][:, 2 * i:2 * i + 2, :], PS[:, 5 + i % 2, :].rearrange("p (k n) -> p k n", k=2),
                                MS[0][mb][:, 2 * i:2 * i + 2, :].bitcast(F32), ALU.subtract).then_inc(ms_ready, 1)

            def rows_lo(p, s, mb):
                dve.wait_ge(y_hi, p * 6 + (s + 1))
                V.scalar_tensor_tensor(out=YS[1][s % 2][:], in0=PS[:, 3 + s % 2, 0:THIRD], scalar=rcs[:, mb, s // 3:s // 3 + 1],
                                       in1=YS[0][s % 2][:].bitcast(F32), op0=ALU.mult, op1=ALU.subtract).then_inc(y_ready, 1)

            def pair(p, mb, first=False, nxt=True):
                for s in range(6):
                    if nxt and s == 3:
                        count_inverse(p + 1, 1 - mb)
                    if s:
                        rows_lo(p, s - 1, mb)
                    elif not first:
                        rows_lo(p - 1, 5, 1 - mb)
                    if nxt and s == 1:
                        pair_onehots(p + 1, js=[1])
                    if nxt and s == 5:
                        sums_lo(p + 1, 2, 1 - mb)
                    if nxt or s + 2 < 6:
                        weight_lo(p, s + 2)
                    if s == 0:
                        slot_onehots(p, 0)
                    if s == 1:
                        slot_onehots(p, 1)
                    if nxt and s == 0:
                        pair_onehots(p + 1, js=[0])
                    if nxt and 3 <= s < 5:
                        sums_lo(p + 1, s - 3, 1 - mb)
                if not nxt:
                    rows_lo(p, 5, mb)

            def keys34(r, buf):
                return V.scalar_tensor_tensor(out=ekey[:, buf, :], in0=keyf[:, 3, :], scalar=relid[:, r], in1=keyf[:, 1, :],
                                              op0=ALU.is_equal, op1=ALU.mult)


            def onehot34(r, rel, buf):
                dve.wait_ge(cnt_summed, r + 2)
                keys34(rel, buf).then_inc(key_ready, 1)
                dve.wait_ge(key_ready, r + 1)
                onehot(E[buf], ekey[:, buf, :]).then_inc(e_ready, 1)

            def normalise34(r, j):
                dve.wait_ge(deg_spread, r + (R3 + 1))
                V.tensor_scalar(RC[:, 0, :], PS[:, 5, 0:NODES], 1.0, None, ALU.max).then_inc(rc_step, 1)
                dve.wait_ge(rc_step, r * 2 + 1)
                V.reciprocal(RC[:, 1, :], RC[:, 0, :]).then_inc(rc_step, 1)
                dve.wait_ge(rc_step, r * 2 + 2)
                dve.wait_ge(agg_done, (r + (2 * R3 - 1)) * 3)
                V.tensor_tensor(N34[j], A34[j], RC[:, 1, :].unsqueeze(1).to_broadcast([P, NT, NODES]), ALU.mult).then_inc(nrm_ready, 1)


            dve.wait_ge(sorted_in, 32)
            overflow = dve.value_load(flag[0:1, 0:1])
            with dve.If(overflow < 1):
                for x in (rc_ready, ms_ready, y_ready):
                    dve.sem_inc(x, CREDIT)
                pair_onehots(0)
                dve.wait_ge(xs_hi, 1)
                V.tensor_tensor(XS[1][:], xN[:], XS[0][:].bitcast(F32), ALU.subtract).then_inc(xs_ready, 1)
                weight_lo(0, 0)
                weight_lo(0, 1)
                count_inverse(0, 0)
                for i in range(3):
                    sums_lo(0, i, 0)
                pair(0, 0, first=True)
                with dve.Fori(0, (PAIRS34 - 3) // 2) as i:
                    pair(i * 2 + 1, 1)
                    pair(i * 2 + 2, 0)
                pair(PAIRS34 - 2, 1)
                pair(PAIRS34 - 1, 0, nxt=False)
            with dve.Else():
                onehot(S1L[:], keyf[:, 0, :]).then_inc(s1_ready, 1)
                onehot34(0, slice(0, 1), 1)
                with dve.Fori(0, LOOP34) as i:
                    for j in range(2):
                        onehot34(i * 2 + (j + 1), bass.ds(i * 2 + (j + 1), 1), j)
                        normalise34(i * 2 + j, j)
                onehot34(R34 - 1, slice(R34 - 1, R34), 0)
                normalise34(R34 - 2, 0)
                normalise34(R34 - 1, 1)
            dve.wait_ge(enc_done, 1)
            V.tensor_tensor(hN[:], PS[:, 0:3, :].rearrange("p b n -> p (b n)").rearrange("p (t f) -> p t f", t=NT),
                            biasN[:, 4, :].unsqueeze(1).to_broadcast([P, NT, FEAT]), ALU.add).then_inc(h1_copied, 1)
            gcn_out(2, 0)
            layer_norm(4)


_IN = {
    "x": ("x", None), "xT": ("x", "T"), "qU": ("L0_gnn_query_embs", "units"), "qT": ("L0_gnn_query_embs", "rowsT"),
    "src": ("src", None), "dst": ("dst", None), "t3": ("edge_type_3", None), "t34": ("edge_type_34", None),
    "W_rel1": ("L0_gnn_W_rel1", None), "W_root1": ("L0_gnn_W_root1", None), "b1": ("L0_gnn_b1", None),
    "W_rel2": ("L0_gnn_W_rel2", None), "W_root2": ("L0_gnn_W_root2", None), "b2": ("L0_gnn_b2", None),
    "WgT": ("L0_gnn_Wg", "T"), "bg": ("L0_gnn_bg", None), "WqT": ("L0_gnn_Wq", "T"), "bq": ("L0_gnn_bq", None),
    "L1_W": ("L1_gnn_W", None), "L1_b": ("L1_gnn_b", None),
    "W1": ("L2_gnn_W1", None), "qk1": (("L2_gnn_q1", "L2_gnn_k1"), "cols"), "L2_b1": ("L2_gnn_b1", None),
    "W2": ("L2_gnn_W2", None), "qk2": (("L2_gnn_q2", "L2_gnn_k2"), "cols"), "L2_b2": ("L2_gnn_b2", None),
    "L3_rel": ("L3_gnn_W_rel", None), "L3_root": ("L3_gnn_W_root", None), "b_rgcn": ("L3_gnn_b_rgcn", None),
    "L3_gcn": ("L3_gnn_W_gcn", None), "b_gcn": ("L3_gnn_b_gcn", None),
}


def kernel(**inputs):
    import numpy as np
    import concourse.bacc as bacc
    from concourse.bass_utils import run_bass_kernel_spmd

    nc = bacc.Bacc("TRN2", target_bir_lowering=False, num_devices=1)
    arrays, handles = {}, {}
    for name, (source, layout) in _IN.items():
        if layout == "cols":
            a = np.concatenate([np.asarray(inputs[n]) for n in source], axis=1)
        else:
            a = np.asarray(inputs[source])
        if layout in ("rows", "rowsT"):
            a = a.reshape(-1, a.shape[-1])
        if layout == "units":
            a = a.reshape(NT, GATE_B, QLEN, 3, THIRD).transpose(0, 3, 2, 1, 4).reshape(UNITS, QLEN, GATE_B * THIRD)
        if layout in ("T", "rowsT"):
            a = a.T
        a = np.ascontiguousarray(a)
        arrays[f"in_{name}"] = a
        handles[name] = nc.dram_tensor(f"in_{name}", a.shape, mybir.dt.from_np(a.dtype), kind="ExternalInput").ap()
    handles["out"] = nc.dram_tensor("out", (NODES, FEAT), F32, kind="ExternalOutput").ap()
    build(nc, handles)
    r = run_bass_kernel_spmd(nc, [arrays], core_ids=[0])
    return r.results[0]["out"]
```
